# Optimizing a Trainium2 kernel written in Bass

```python
import numpy as np
import jax
import jax.numpy as jnp

def _softmax(x, axis=-1):
    return jax.nn.softmax(x, axis=axis)

def _gelu(x):
    return jax.nn.gelu(x, approximate=True)

def _silu(x):
    return jax.nn.silu(x)

def _sigmoid(x):
    return jax.nn.sigmoid(x)

def _layernorm(x, axis=-1, eps=1e-05):
    m = jnp.mean(x, axis=axis, keepdims=True)
    v = jnp.var(x, axis=axis, keepdims=True)
    return (x - m) / jnp.sqrt(v + eps)

def _scatter_add(tgt, idx, src, axis=0):
    return tgt.at[idx].add(src)

def _segment_sum(src, seg, n):
    return jax.ops.segment_sum(src, seg, n)
kernel_name = 'mk_early_fusion_embed_d1_tok_img768_r4_820302'

def setup_inputs(seed: int=0):
    np.random.seed(seed)
    _w = jnp.asarray

    def _rec_inputs():
        import jax
        import jax.numpy as jnp
        _rk = jax.random.key(seed)
        x = -0.00016672 + 0.999947 * jax.random.normal(jax.random.fold_in(_rk, 1), (32, 3, 96, 96), jnp.float32)
        x_txt = jax.random.randint(jax.random.fold_in(_rk, 51), (32, 32), 0, 31993, jnp.int32)
        return (x, x_txt)
    x, x_txt = _rec_inputs()

    def _L0_tok_setup():
        import jax, jax.numpy as jnp
        import numpy as np
        B, C, H, W = (64, 3, 96, 96)
        P = 16
        EMB = 192
        N_PATCH = H // P * (W // P)
        IN_FEAT = P * P * C
        key = jax.random.key(seed)
        k1, k2, k3, k4 = jax.random.split(key, 4)
        x = jax.random.normal(k1, (B, C, H, W), dtype=jnp.float32)
        bound = 1.0 / np.sqrt(IN_FEAT)
        proj_w = jax.random.uniform(k2, (EMB, IN_FEAT), minval=-bound, maxval=bound, dtype=jnp.float32)
        proj_b = jax.random.uniform(k3, (EMB,), minval=-bound, maxval=bound, dtype=jnp.float32)
        pos_emb = jax.random.normal(k4, (N_PATCH, EMB), dtype=jnp.float32)
        return {'x': x, 'proj_w': proj_w, 'proj_b': proj_b, 'pos_emb': pos_emb}
    _L0_tok_all = _L0_tok_setup()
    _L0_tok_in = {k: v for k, v in _L0_tok_all.items() if k in ('proj_w', 'proj_b', 'pos_emb')}
    del _L0_tok_all

    def _L0_txt_setup():
        import jax, jax.numpy as jnp
        import numpy as np
        VOCAB = 8000
        key = jax.random.key(seed)
        k1, k2 = jax.random.split(key)
        input_ids = jax.random.randint(k1, (4, 512), 0, VOCAB, dtype=jnp.int64 if jax.config.jax_enable_x64 else jnp.int32)
        weight = jax.random.normal(k2, (VOCAB, 192), dtype=jnp.float32)
        return {'input_ids': input_ids, 'weight': weight}
    _L0_txt_all = _L0_txt_setup()
    _L0_txt_in = {k: v for k, v in _L0_txt_all.items() if k in ('weight',)}
    del _L0_txt_all

    def _L0_attn_setup():
        import jax, jax.numpy as jnp
        import numpy as np
        import math
        B, N, DIM = (4, 512, 192)
        HEADS, DIM_HEAD = (12, 64)
        SCALE = math.sqrt(DIM_HEAD)

        def _split_heads(t):
            b, n, _ = t.shape
            return t.reshape(b, n, HEADS, DIM_HEAD).transpose(0, 2, 1, 3)
        key = jax.random.key(seed)
        ks = jax.random.split(key, 5)
        inner = HEADS * DIM_HEAD
        x = jax.random.normal(ks[0], (B, N, DIM), dtype=jnp.float32)
        w_q = jax.random.normal(ks[1], (DIM, inner), dtype=jnp.float32) * 0.02
        w_k = jax.random.normal(ks[2], (DIM, inner), dtype=jnp.float32) * 0.02
        w_v = jax.random.normal(ks[3], (DIM, inner), dtype=jnp.float32) * 0.02
        w_o = jax.random.normal(ks[4], (inner, DIM), dtype=jnp.float32) * 0.02
        b_o = jnp.zeros((DIM,), dtype=jnp.float32)
        return {'x': x, 'w_q': w_q, 'w_k': w_k, 'w_v': w_v, 'w_o': w_o, 'b_o': b_o}
    _L0_attn_all = _L0_attn_setup()
    _L0_attn_in = {k: v for k, v in _L0_attn_all.items() if k in ('w_q', 'w_k', 'w_v', 'w_o', 'b_o')}
    del _L0_attn_all

    def _L0_ffn_setup():
        import jax, jax.numpy as jnp
        import numpy as np
        D = 192
        M = 768
        G = 4
        E = 8
        KG = 2
        KE = 4
        EPS = 1e-06

        def _topk_gates(logits, k):
            top, idx = jax.lax.top_k(logits, k)
            gates = jax.nn.softmax(top, axis=-1)
            gates = jnp.where(gates >= EPS, gates, jnp.zeros_like(gates))
            return (gates, idx)
        key = jax.random.key(seed)
        ks = jax.random.split(key, 9)
        x = jax.random.normal(ks[0], (1, 256, D), dtype=jnp.float32)
        Wg = jax.random.normal(ks[1], (D, G), dtype=jnp.float32) * 0.02
        bg = jax.random.normal(ks[2], (G,), dtype=jnp.float32) * 0.01
        We = jax.random.normal(ks[3], (G, D, E), dtype=jnp.float32) * 0.02
        be = jax.random.normal(ks[4], (G, E), dtype=jnp.float32) * 0.01
        W1 = jax.random.normal(ks[5], (G, E, D, M), dtype=jnp.float32) * 0.02
        b1 = jax.random.normal(ks[6], (G, E, M), dtype=jnp.float32) * 0.01
        W2 = jax.random.normal(ks[7], (G, E, M, D), dtype=jnp.float32) * 0.02
        b2 = jax.random.normal(ks[8], (G, E, D), dtype=jnp.float32) * 0.01
        return {'x': x, 'Wg': Wg, 'bg': bg, 'We': We, 'be': be, 'W1': W1, 'b1': b1, 'W2': W2, 'b2': b2}
    _L0_ffn_all = _L0_ffn_setup()
    _L0_ffn_in = {k: v for k, v in _L0_ffn_all.items() if k in ('Wg', 'bg', 'We', 'be', 'W1', 'b1', 'W2', 'b2')}
    del _L0_ffn_all
    return {'x': x, 'x_txt': x_txt, 'L0_tok_proj_w': _L0_tok_in['proj_w'], 'L0_tok_proj_b': _L0_tok_in['proj_b'], 'L0_tok_pos_emb': _L0_tok_in['pos_emb'], 'L0_txt_weight': _L0_txt_in['weight'], 'L0_attn_w_q': _L0_attn_in['w_q'], 'L0_attn_w_k': _L0_attn_in['w_k'], 'L0_attn_w_v': _L0_attn_in['w_v'], 'L0_attn_w_o': _L0_attn_in['w_o'], 'L0_attn_b_o': _L0_attn_in['b_o'], 'L0_ffn_Wg': _L0_ffn_in['Wg'], 'L0_ffn_bg': _L0_ffn_in['bg'], 'L0_ffn_We': _L0_ffn_in['We'], 'L0_ffn_be': _L0_ffn_in['be'], 'L0_ffn_W1': _L0_ffn_in['W1'], 'L0_ffn_b1': _L0_ffn_in['b1'], 'L0_ffn_W2': _L0_ffn_in['W2'], 'L0_ffn_b2': _L0_ffn_in['b2']}

def reference(x, x_txt, L0_tok_proj_w, L0_tok_proj_b, L0_tok_pos_emb, L0_txt_weight, L0_attn_w_q, L0_attn_w_k, L0_attn_w_v, L0_attn_w_o, L0_attn_b_o, L0_ffn_Wg, L0_ffn_bg, L0_ffn_We, L0_ffn_be, L0_ffn_W1, L0_ffn_b1, L0_ffn_W2, L0_ffn_b2):
    import jax
    import jax.numpy as jnp

    def _L0_tok_ref(x, proj_w, proj_b, pos_emb):
        import jax, jax.numpy as jnp
        import numpy as np
        B, C, H, W = (64, 3, 96, 96)
        P = 16
        EMB = 192
        N_PATCH = H // P * (W // P)
        IN_FEAT = P * P * C
        b, c, h, w = x.shape
        p = P
        patches = x.reshape(b, c, h // p, p, w // p, p)
        patches = patches.transpose(0, 2, 4, 3, 5, 1).reshape(b, h // p * (w // p), p * p * c)
        out = jnp.einsum('bnf,ef->bne', patches, proj_w) + proj_b
        return out + pos_emb

    def _L0_txt_ref(input_ids, weight):
        import jax, jax.numpy as jnp
        import numpy as np
        VOCAB = 8000
        one_hot = jax.nn.one_hot(input_ids, VOCAB, dtype=weight.dtype)
        return jnp.einsum('bsv,vd->bsd', one_hot, weight)

    def _L0_attn_ref(x, w_q, w_k, w_v, w_o, b_o):
        import jax, jax.numpy as jnp
        import numpy as np
        import math
        B, N, DIM = (4, 512, 192)
        HEADS, DIM_HEAD = (12, 64)
        SCALE = math.sqrt(DIM_HEAD)

        def _split_heads(t):
            b, n, _ = t.shape
            return t.reshape(b, n, HEADS, DIM_HEAD).transpose(0, 2, 1, 3)
        q = _split_heads(x @ w_q)
        k = _split_heads(x @ w_k)
        v = _split_heads(x @ w_v)
        scores = jnp.einsum('bhnd,bhmd->bhnm', q, k) / SCALE
        attn = jax.nn.softmax(scores, axis=-1)
        h = jnp.einsum('bhnm,bhmd->bhnd', attn, v)
        H = h.transpose(0, 2, 1, 3).reshape(x.shape[0], x.shape[1], HEADS * DIM_HEAD)
        out = H @ w_o + b_o
        return out

    def _L0_ffn_ref(x, Wg, bg, We, be, W1, b1, W2, b2):
        import jax, jax.numpy as jnp
        import numpy as np
        D = 192
        M = 768
        G = 4
        E = 8
        KG = 2
        KE = 4
        EPS = 1e-06

        def _topk_gates(logits, k):
            top, idx = jax.lax.top_k(logits, k)
            gates = jax.nn.softmax(top, axis=-1)
            gates = jnp.where(gates >= EPS, gates, jnp.zeros_like(gates))
            return (gates, idx)
        orig_shape = x.shape
        xf = x.reshape(-1, D)
        glog = xf @ Wg + bg
        ggates, gidx = _topk_gates(glog, KG)
        gw = jnp.einsum('nk,nkg->ng', ggates, jax.nn.one_hot(gidx, G, dtype=xf.dtype))
        elog = jnp.einsum('nd,gde->nge', xf, We) + be
        egates, eidx = _topk_gates(elog, KE)
        ew = jnp.einsum('ngk,ngke->nge', egates, jax.nn.one_hot(eidx, E, dtype=xf.dtype))
        combine = gw[:, :, None] * ew
        y = jnp.zeros_like(xf)
        for g in range(G):
            h = jax.nn.gelu(jnp.einsum('nd,edm->enm', xf, W1[g]) + b1[g][:, None, :], approximate=False)
            o = jnp.einsum('enm,emd->end', h, W2[g]) + b2[g][:, None, :]
            y = y + jnp.einsum('end,ne->nd', o, combine[:, g, :])
        return y.reshape(orig_shape)
    h = _L0_tok_ref(x, L0_tok_proj_w, L0_tok_proj_b, L0_tok_pos_emb)
    h = jnp.concatenate([h, _L0_txt_ref(x_txt, L0_txt_weight)], axis=1)
    h = h + _L0_attn_ref(_layernorm(h, axis=-1), L0_attn_w_q, L0_attn_w_k, L0_attn_w_v, L0_attn_w_o, L0_attn_b_o)
    h = h + _L0_ffn_ref(_layernorm(h, axis=-1), L0_ffn_Wg, L0_ffn_bg, L0_ffn_We, L0_ffn_be, L0_ffn_W1, L0_ffn_b1, L0_ffn_W2, L0_ffn_b2)
    return h

_drawn_inputs = setup_inputs


def setup_inputs(seed=0):
    import zlib

    import numpy as np

    out = dict(_drawn_inputs(seed))
    spreads = {'L0_attn_b_o': (0.0, 0.1)}
    factors = {'L0_tok_proj_b': 3.411,
     'L0_attn_w_q': 8.0,
     'L0_attn_w_k': 8.0,
     'L0_attn_w_v': 3.212,
     'L0_attn_w_o': 3.224,
     'L0_ffn_bg': 28.763,
     'L0_ffn_be': 46.896,
     'L0_ffn_b1': 64.0,
     'L0_ffn_b2': 21.38,
     'L0_ffn_We': 2.674}
    for name, (base, spread) in spreads.items():
        noise = np.random.default_rng([zlib.crc32(name.encode()), seed]).standard_normal(out[name].shape)
        drawn = base * np.exp(spread * noise) if base else spread * noise
        out[name] = jnp.asarray(drawn.astype(out[name].dtype))
    for name, factor in factors.items():
        out[name] = (out[name] * factor).astype(out[name].dtype)
    return out
```

```python
import concourse.bass as bass
from concourse import mybir
from contextlib import ExitStack

F32, F16, I32 = mybir.dt.float32, mybir.dt.float16, mybir.dt.int32
ALU, ACT, AX = mybir.AluOpType, mybir.ActivationFunctionType, mybir.AxisListType

P = 128
B, S_IMG, S_TXT = 32, 36, 32
S = S_IMG + S_TXT
N = B * S
NT = N // P
D = 192
DR = D - P
FEAT = 768
KF = FEAT // P
VOCAB = 8000
H, DH = 12, 64
INNER = H * DH
HP = H // 2
G, E, KG, KE = 4, 8, 2, 4
GE = G * E
M = 768
KM = M // P
LN_EPS, GATE_EPS = 1e-5, 1e-6
NPAIR = B // 2
S2 = 2 * S
IMG_TILES, TXT_TILES = S_IMG * B // P, S_TXT * B // P
NPADDED = N + P
XROW = D + GE
SLOTS = 18
GRAN = 2 * P
HALF_N = N // 2
WSCALE = 256.0
SG = P // B


def build(nc, io):
    ctx = ExitStack()
    with ctx:
        def sb(name, shape, dt=F32):
            return ctx.enter_context(nc.sbuf_tensor(name, shape, dt))

        def dram(name, shape, dt=F32):
            return nc.dram_tensor(name, shape, dt).ap()

        d = dict(h0=dram("h0_d", [N, D]), attn=dram("attn_d", [N, D]),
                 xrow=dram("xrow_d", [NPADDED, XROW]), b1s=dram("b1s_d", [2, GE, M], F16),
                 y=[dram("ya_d", [NPADDED, D]), dram("yb_d", [NPADDED, D])])
        ident = sb("ident", [P, P])
        h = sb("h", [P, NT, D])
        slots = sb("slots", [P, GE * SLOTS], I32)
        n_gran = sb("n_gran", [1, GE], I32)
        gran0 = sb("gran0", [1, GE + 1], I32)
        front(nc, io, ident, h, d)
        route(nc, io, ident, h, d, slots, n_gran, gran0)
        experts(nc, io, h, d, slots, n_gran, gran0)


def front(nc, io, ident, h0, d):
    h0_d, attn_d = d["h0"], d["attn"]
    ctx = ExitStack()
    with ctx:
        def sb(name, shape, dt=F32):
            return ctx.enter_context(nc.sbuf_tensor(name, shape, dt))

        def sem(name):
            return ctx.enter_context(nc.semaphore(name))

        bank = [ctx.enter_context(nc.psum_tensor(f"fbank{i}", [P, 512], F32)) for i in range(8)]

        xp = sb("xp", [P, KF, S_IMG * B])
        pw = sb("pw", [P, KF, D])
        pos = sb("pos", [P, IMG_TILES, D])
        pbias = sb("pbias", [P, D])
        emb = sb("emb", [P, IMG_TILES, D])
        ids = sb("ids", [P, TXT_TILES], I32)
        idf = sb("idf", [P, TXT_TILES])
        idc = sb("idc", [P, TXT_TILES], I32)
        inside = sb("inside", [P, TXT_TILES])
        words = sb("words", [P, TXT_TILES, D])
        stats = sb("stats", [P, NT, 6])
        mv = sb("mv", [P, NT, 2])
        eps = sb("eps", [P, 1])
        rstd = sb("rstd", [P, NT])
        xn = sb("xn", [P, NT, D])
        xnT = sb("xnT", [P, N + S2])
        xnTr = sb("xnTr", [DR, N + S2])
        wqkv = sb("wqkv", [P, 3 * INNER])
        wqkvr = sb("wqkvr", [DR, 3 * INNER])
        wo = sb("wo", [P, HP, D])
        xg = sb("xg", [P, S2])
        xgr = sb("xgr", [DR, S2])
        qk = sb("qk", [P, 2 * HP, S2])
        v = sb("v", [S, 2, INNER])
        mx = sb("mx", [S, 2, 2, HP])
        diff = sb("diff", [S, 2, 2, HP, S])
        ex = sb("ex", [S, 2, 2, HP, S])
        den = sb("den", [S, 2, 2, HP])
        rden = sb("rden", [S, 2, 2, HP])
        prob = sb("prob", [S, 2, 2, HP, S])
        probT = sb("probT", [S, 2, 2, HP, S])
        hT = sb("hT", [P, 2, HP, S])
        ao = sb("ao", [S, 2, D])

        s_id, s_patch, s_pos, s_idin = sem("ident_in"), sem("patches_in"), sem("pos_in"), sem("ids_in")
        s_w = sem("attn_weights_in")
        s_posb = sem("pos_biased")
        s_idc = sem("ids_clamped")
        s_words = sem("words_gathered")
        s_wm = sem("words_masked")
        s_pe = sem("patch_products")
        s_emb = sem("patch_rows")
        s_h0out, s_h0in = sem("h0_stored"), sem("h0_loaded")
        s_chain = sem("dve_step")
        s_var, s_std, s_xn = sem("variance_ready"), sem("std_ready"), sem("xn_ready")
        s_tp, s_tev = sem("xn_transposed"), sem("xnT_copied")
        s_pad = sem("pads_zeroed")
        s_xg = sem("xg_ready")
        s_pf, s_pev = sem("projection_full"), sem("projection_copied")
        s_sf, s_df, s_ex, s_p = sem("scores_full"), sem("diff_ready"), sem("exp_ready"), sem("probs_ready")
        s_ptf, s_ptev = sem("probT_full"), sem("probT_copied")
        s_hf, s_hev = sem("hT_full"), sem("hT_copied")
        s_wf, s_wev, s_aout = sem("wo_full"), sem("wo_copied"), sem("attn_stored")
        s_ach = sem("softmax_step")

        block = ctx.enter_context(nc.Block())
        TG = [(t0, min(4, NT - t0)) for t0 in range(0, NT, 4)]
        img_rows = h0_d.rearrange("(b s) d -> b s d", s=S)

        def projT(k):
            return 8 * k

        @block.sync
        def _(sp):
            sp.dma_start(ids[:, :], io["idsT"][:, :]).then_inc(s_idin, 16)
            sp.dma_start(pw[:, :, :], io["pwT"][:, :, :]).then_inc(s_patch, 16)
            for k in range(KF):
                sp.dma_start(xp[:, k, :], io["xpT"][:, k, :]).then_inc(s_patch, 16)
            sp.dma_start(ident[:, :], io["ident"][:, :]).then_inc(s_id, 16)
            sp.dma_start(pbias[:, :], io["L0_tok_proj_b"].partition_broadcast(P)).then_inc(s_pos, 16)
            for a in range(SG):
                src = io["L0_tok_pos_emb"].rearrange("(t a) d -> a t d", a=SG)[a]
                sp.dma_start(pos[B * a:B * a + B, :, :], src.partition_broadcast(B)).then_inc(s_pos, 16)
            sp.dma_start(wqkv[:, :], io["wqkv"][0:P, :]).then_inc(s_w, 16)
            sp.dma_start(wqkvr[:, :], io["wqkv"][P:D, :]).then_inc(s_w, 16)
            sp.dma_start(wo[:, :, :], io["L0_attn_w_o"].rearrange("(c p) d -> p c d", p=P)).then_inc(s_w, 16)
            sp.wait_ge(s_wm, 1)
            for a in range(SG):
                dst = img_rows[:, S_IMG + a:S:SG, :]
                sp.dma_start(dst, words[B * a:B * a + B, :, :]).then_inc(s_h0out, 16)
            sp.wait_ge(s_emb, IMG_TILES)
            for a in range(SG):
                dst = img_rows[:, a:S_IMG:SG, :]
                sp.dma_start(dst, emb[B * a:B * a + B, :, :]).then_inc(s_h0out, 16)
            sp.wait_ge(s_h0out, 16 * 2 * SG)
            sp.dma_start(h0[:, :, :], h0_d.rearrange("(p t) d -> p t d", t=NT)).then_inc(s_h0in, 16)
            sp.sem_inc(s_aout, 16)
            with sp.Fori(0, NPAIR) as i:
                for b in range(2):
                    sp.wait_ge(s_wev, 2 * i + b + 2)
                    sp.dma_start(attn_d[bass.ds(i * S2 + b * S, S), :], ao[:, b, :]).then_inc(s_aout, 16)
            sp.wait_ge(s_aout, 16 * B + 16)

        @block.gpsimd
        def _(pool):
            nc.gpsimd.memset(eps[:, :], LN_EPS).then_inc(s_pad, 1)
            nc.gpsimd.memset(xnT[:, N:N + S2], 0.0).then_inc(s_pad, 1)
            nc.gpsimd.memset(xnTr[:, N:N + S2], 0.0).then_inc(s_pad, 1)
            pool.wait_ge(s_idc, 1)
            for t in range(TXT_TILES):
                pool.indirect_dma_start(words[:, t, :], None, io["L0_txt_weight"][:, :],
                                        bass.IndirectOffsetOnAxis(ap=idc[:, t:t + 1], axis=0)).then_inc(s_words, 16)
            pool.wait_ge(s_tev, 2 * len(TG))
            pool.wait_ge(s_pad, 3)

            def group(k):
                nc.gpsimd.tensor_copy(xg[:, :], xnT[:, bass.ds(k * S2, S2)]).then_inc(s_xg, 1)
                nc.gpsimd.tensor_copy(xgr[:, :], xnTr[:, bass.ds(k * S2, S2)]).then_inc(s_xg, 1)
            group(0)
            with pool.Fori(0, NPAIR) as i:
                pool.wait_ge(s_pf, projT(i + 1))
                group(i + 1)

        @block.tensor
        def _(pe):
            pe.wait_ge(s_patch, 16 * (KF + 1))
            for t in range(IMG_TILES):
                if t >= 2:
                    pe.wait_ge(s_emb, t - 1)
                for k in range(KF):
                    mm = nc.tensor.matmul(bank[t % 2][:, 0:D], xp[:, k, P * t:P * t + P], pw[:, k, :],
                                          start=(k == 0), stop=(k == KF - 1))
                mm.then_inc(s_pe, 1)
            pe.wait_ge(s_id, 16)
            for g, (t0, n) in enumerate(TG):
                pe.wait_ge(s_xn, t0 + n)
                for part, (rows, lo) in enumerate(((P, 0), (DR, P))):
                    if g >= 1:
                        pe.wait_ge(s_tev, 2 * g - 1 + part)
                    for j in range(n):
                        tr = nc.tensor.transpose(bank[2 + part][0:rows, P * j:P * j + P],
                                                 xn[:, t0 + j, lo:lo + rows], ident[:, :])
                    tr.then_inc(s_tp, 1)
            pe.wait_ge(s_w, 48)

            def project_qk(k):
                pe.wait_ge(s_xg, 2 * k + 2)
                for f in range(4):
                    if not (isinstance(k, int) and 8 * k + f < 2):
                        pe.wait_ge(s_pev, 8 * k + f - 1)
                    for j in range(3):
                        c = 3 * f + j
                        nc.tensor.matmul(bank[6 + f % 2][:, S2 * j:S2 * j + S2], wqkv[:, P * c:P * c + P], xg[:, :],
                                         start=True, stop=False)
                        mm = nc.tensor.matmul(bank[6 + f % 2][:, S2 * j:S2 * j + S2], wqkvr[:, P * c:P * c + P],
                                              xgr[:, :], start=False, stop=True)
                    mm.then_inc(s_pf, 1)

            def project_v(k):
                for f in range(4):
                    b, half = divmod(f, 2)
                    pe.wait_ge(s_pev, 8 * k + 4 + f - 1)
                    lo, w = 2 * INNER + half * INNER // 2, INNER // 2
                    nc.tensor.matmul(bank[6 + f % 2][0:S, 0:w], xg[:, S * b:S * b + S], wqkv[:, lo:lo + w],
                                     start=True, stop=False)
                    nc.tensor.matmul(bank[6 + f % 2][0:S, 0:w], xgr[:, S * b:S * b + S], wqkvr[:, lo:lo + w],
                                     start=False, stop=True).then_inc(s_pf, 1)

            project_qk(0)
            project_v(0)
            with pe.Fori(0, NPAIR) as i:
                pe.wait_ge(s_pev, 8 * i + 8)
                for b in range(2):
                    for hp in range(HP):
                        for odd in range(2):
                            mm = nc.tensor.matmul(bank[2 * b + odd][0:S, S * hp:S * hp + S],
                                                  qk[DH * odd:DH * odd + DH, hp, S * b:S * b + S],
                                                  qk[DH * odd:DH * odd + DH, HP + hp, S * b:S * b + S],
                                                  start=True, stop=True)
                    mm.then_inc(s_sf, 1)
                project_qk(i + 1)
                for b in range(2):
                    pe.wait_ge(s_p, 2 * i + b + 1)
                    for odd in range(2):
                        for hp in range(HP):
                            tr = nc.tensor.transpose(bank[2 * b + odd][0:S, S * hp:S * hp + S],
                                                     prob[:, b, odd, hp, :], ident[0:S, 0:S])
                    tr.then_inc(s_ptf, 1)
                    pe.wait_ge(s_ptev, 2 * i + b + 1)
                    pe.wait_ge(s_hev, 2 * i + b + 1)
                    for hp in range(HP):
                        for odd in range(2):
                            h = 2 * hp + odd
                            mm = nc.tensor.matmul(bank[4][DH * odd:DH * odd + DH, S * hp:S * hp + S],
                                                  v[:, b, DH * h:DH * h + DH], probT[:, b, odd, hp, :],
                                                  start=True, stop=True)
                    mm.then_inc(s_hf, 1)
                project_v(i + 1)
                for b in range(2):
                    pe.wait_ge(s_hev, 2 * i + b + 2)
                    pe.wait_ge(s_wev, 2 * i + b + 1)
                    for c in range(HP):
                        mm = nc.tensor.matmul(bank[5][0:S, 0:D], hT[:, b, c, :], wo[:, c, :],
                                              start=(c == 0), stop=(c == HP - 1))
                    mm.then_inc(s_wf, 1)

        @block.scalar
        def _(act):
            act.wait_ge(s_var, 1)
            act.wait_ge(s_pad, 1)
            nc.scalar.activation(rstd[:, :], mv[:, :, 1], ACT.Sqrt, bias=eps[:, 0:1], scale=1.0).then_inc(s_std, 1)

            def copy_qk(k):
                for f in range(4):
                    act.wait_ge(s_pf, 8 * k + f + 1)
                    nc.scalar.copy(qk[:, 3 * f:3 * f + 3, :], bank[6 + f % 2][:, 0:3 * S2]).then_inc(s_pev, 1)

            def copy_v(k):
                for f in range(4):
                    b, half = divmod(f, 2)
                    act.wait_ge(s_pf, 8 * k + 4 + f + 1)
                    w = INNER // 2
                    nc.scalar.copy(v[:, b, w * half:w * half + w], bank[6 + f % 2][0:S, 0:w]).then_inc(s_pev, 1)

            copy_qk(0)
            copy_v(0)
            act.sem_inc(s_hev, 1)
            act.sem_inc(s_wev, 1)
            with act.Fori(0, NPAIR) as i:
                for b in range(2):
                    act.wait_ge(s_df, 2 * i + b + 1)
                    nc.scalar.activation(ex[:, b], diff[:, b], ACT.Exp, scale=float(DH) ** -0.5).then_inc(s_ex, 1)
                copy_qk(i + 1)
                for b in range(2):
                    act.wait_ge(s_ptf, 2 * i + b + 1)
                    for odd in range(2):
                        cp = nc.scalar.copy(probT[:, b, odd], bank[2 * b + odd][0:S, 0:HP * S])
                    cp.then_inc(s_ptev, 1)
                    act.wait_ge(s_hf, 2 * i + b + 1)
                    nc.scalar.copy(hT[:, b], bank[4][:, 0:HP * S]).then_inc(s_hev, 1)
                copy_v(i + 1)
                for b in range(2):
                    act.wait_ge(s_wf, 2 * i + b + 1)
                    act.wait_ge(s_aout, 32 * i + 16)
                    nc.scalar.copy(ao[:, b, :], bank[5][0:S, 0:D]).then_inc(s_wev, 1)

        @block.vector
        def _(dve):
            n = [0]

            def link(ins):
                n[0] += 1
                ins.then_inc(s_chain, 1)
                dve.wait_ge(s_chain, n[0])

            dve.wait_ge(s_idin, 16)
            link(nc.vector.tensor_copy(idf[:, :], ids[:, :]))
            nc.vector.tensor_scalar(idc[:, :], idf[:, :], 0.0, float(VOCAB - 1), ALU.max, ALU.min).then_inc(s_idc, 1)
            link(nc.vector.tensor_scalar(inside[:, :], idf[:, :], 0.0, None, ALU.is_ge))
            link(nc.vector.scalar_tensor_tensor(out=inside[:, :], in0=idf[:, :], scalar=float(VOCAB - 1),
                                                in1=inside[:, :], op0=ALU.is_le, op1=ALU.mult))
            dve.wait_ge(s_pos, 16 * (1 + SG))
            link(nc.vector.tensor_tensor(pos[:, :, :], pos[:, :, :],
                                         pbias[:, :].unsqueeze(1).broadcast_to([P, IMG_TILES, D]), ALU.add))
            dve.wait_ge(s_words, 16 * TXT_TILES)
            nc.vector.tensor_tensor(words[:, :, :], words[:, :, :],
                                    inside[:, :].unsqueeze(2).broadcast_to([P, TXT_TILES, D]),
                                    ALU.mult).then_inc(s_wm, 1)
            for t in range(IMG_TILES):
                dve.wait_ge(s_pe, t + 1)
                nc.vector.tensor_tensor(emb[:, t, :], bank[t % 2][:, 0:D], pos[:, t, :], ALU.add).then_inc(s_emb, 1)
            dve.wait_ge(s_h0in, 16)
            layer_norm(nc, dve, link, h0, stats, mv, rstd, xn, s_var, s_std, s_xn)
            for g, (t0, cnt) in enumerate(TG):
                for part, (rows, dst) in enumerate(((P, xnT), (DR, xnTr))):
                    dve.wait_ge(s_tp, 2 * g + part + 1)
                    out = dst[0:rows, 0:N].rearrange("q (p t) -> q t p", t=NT)[:, t0:t0 + cnt, :]
                    src = bank[2 + part][0:rows, 0:P * cnt].rearrange("q (t p) -> q t p", p=P)
                    nc.vector.tensor_copy(out, src).then_inc(s_tev, 1)

            STEPS = 4
            with dve.Fori(0, NPAIR) as i:
                for b in range(2):
                    dve.wait_ge(s_sf, 2 * i + b + 1)
                    for odd in range(2):
                        sc = bank[2 * b + odd][0:S, 0:HP * S].rearrange("q (h k) -> q h k", k=S)
                        mxs = nc.vector.tensor_reduce(mx[:, b, odd, :], sc, AX.X, ALU.max)
                    mxs.then_inc(s_ach, 1)
                    dve.wait_ge(s_ach, 6 * i + b + 1)
                    for odd in range(2):
                        sc = bank[2 * b + odd][0:S, 0:HP * S].rearrange("q (h k) -> q h k", k=S)
                        sub = nc.vector.tensor_tensor(diff[:, b, odd], sc,
                                                      mx[:, b, odd, :].unsqueeze(2).broadcast_to([S, HP, S]),
                                                      ALU.subtract)
                    sub.then_inc(s_df, 1)
                    if b == 0:
                        continue
                    for c in range(2):
                        dve.wait_ge(s_ex, 2 * i + c + 1)
                        nc.vector.tensor_reduce(den[:, c], ex[:, c], AX.X, ALU.add).then_inc(s_ach, 1)
                        dve.wait_ge(s_ach, 6 * i + 2 * c + 3)
                        nc.vector.reciprocal(rden[:, c], den[:, c]).then_inc(s_ach, 1)
                        dve.wait_ge(s_ach, 6 * i + 2 * c + 4)
                        nc.vector.tensor_tensor(prob[:, c], ex[:, c],
                                                rden[:, c].unsqueeze(3).broadcast_to([S, 2, HP, S]),
                                                ALU.mult).then_inc(s_p, 1)


def bcast(vec, n):
    return vec.partition_broadcast(n)


def layer_norm(nc, dve, link, h, stats, mv, rstd, xn, s_var, s_std, s_xn):
    for t in range(NT):
        last = nc.vector.bn_stats(stats[:, t, :], h[:, t, :])
    link(last)
    for t in range(NT):
        last = nc.vector.bn_aggr(mv[:, t, :], stats[:, t, :])
    last.then_inc(s_var, 1)
    dve.wait_ge(s_std, 1)
    link(nc.vector.reciprocal(rstd[:, :], rstd[:, :]))
    for t in range(NT):
        nc.vector.tensor_scalar(xn[:, t, :], h[:, t, :], mv[:, t, 0:1], rstd[:, t:t + 1],
                                ALU.subtract, ALU.mult).then_inc(s_xn, 1)


def route(nc, io, ident, h, d, slots, n_gran, gran0):
    ctx = ExitStack()
    with ctx:
        def sb(name, shape, dt=F32):
            return ctx.enter_context(nc.sbuf_tensor(name, shape, dt))

        def sem(name):
            return ctx.enter_context(nc.semaphore(name))

        bank = [ctx.enter_context(nc.psum_tensor(f"rbank{i}", [P, 512], F32)) for i in range(8)]
        NR = G + GE
        TE = NT * GE
        at = sb("at", [P, NT, D])
        bo = sb("bo", [P, D])
        wr = sb("wr", [P, NR])
        wrr = sb("wrr", [DR, NR])
        br = sb("br", [P, NR])
        b2 = sb("b2", [GE, D])
        b1 = sb("b1", [GE, M])
        b1h = sb("b1h", [GE, M], F16)
        b1l = sb("b1l", [GE, M], F16)
        stats = sb("stats2", [P, NT, 6])
        mv = sb("mv2", [P, NT, 2])
        eps = sb("eps2", [P, 1])
        rstd = sb("rstd2", [P, NT])
        xn = sb("xn2", [P, NT, D])
        xrow = sb("xrow", [P, NT, XROW])
        x16 = xrow[:, :, 0:D].bitcast(F16)
        xT = sb("x2T", [P, NT, P])
        xTr = sb("x2Tr", [DR, NT, P])
        zeros = sb("zeros", [P, NPADDED // P * D])
        gl = sb("gl", [P, NT, 1, G])
        el = sb("el", [P, NT, G, E])
        cmp_g = sb("cmp_g", [P, NT, 1, G, G], F16)
        cmp_e = sb("cmp_e", [P, NT, G, E, E], F16)
        rank_g, rank_e = sb("rank_g", [P, NT, 1, G]), sb("rank_e", [P, NT, G, E])
        top_g, top_e = sb("top_g", [P, NT, 1]), sb("top_e", [P, NT, G])
        exp_g, exp_e = sb("exp_g", [P, NT, 1, G]), sb("exp_e", [P, NT, G, E])
        sum_g, sum_e = sb("sum_g", [P, NT, 1]), sb("sum_e", [P, NT, G])
        mask = sb("mask", [P, NT, G, E], F16)
        comb = sb("comb", [P, NT, G, E])
        before = sb("before", [P, NT + 1, GE], F16)
        ltri = sb("ltri", [P, P], F16)
        ones = sb("ones", [P, P], F16)
        pos_f = sb("pos_f", [P, GE, NT])
        pos_i = sb("pos_i", [P, GE, NT], I32)
        place_i = sb("place_i", [P, GE, NT], I32)
        place = sb("place", [P, GE, NT])
        tile_of = sb("tile_of", [P, GE, NT])
        code = sb("code", [P, NT])
        code_b = sb("code_b", [P, GE, NT])
        mask_f = sb("mask_f", [P, GE, NT])
        rhs = sb("rhs", [P, GE, NT, SLOTS], F16)
        iota = sb("iota", [P, P], F16)
        one_hot = sb("one_hot", [P, 2, NT, P], F16)
        place_e = sb("place_e", [P, 2, NT])
        rhs_e = sb("rhs_e", [P, 2, NT, SLOTS], F16)
        codes = sb("codes", [P, GE * SLOTS])
        pos_code = sb("pos_code", [P, GE * SLOTS])
        pad_row = sb("pad_row", [P, 1])
        empty = sb("empty", [P, GE * SLOTS])
        tot = sb("tot", [1, GE])
        tot_i = sb("tot_i", [1, GE], I32)
        n_f = sb("n_f", [1, GE])
        earlier = sb("earlier", [1, (GE + 1) * GE])
        prod = sb("prod", [1, (GE + 1) * GE])
        g0_f = sb("g0_f", [1, GE + 1])
        combT = sb("combT", [GE, NT, P])

        s_in, s_att, s_b1in = sem("router_in"), sem("attn_in"), sem("b1_in")
        s_chain, s_z, s_zout = sem("route_step"), sem("zeros_ready"), sem("zeros_stored")
        s_var, s_std, s_xn = sem("variance2"), sem("std2"), sem("xn2_ready")
        s_hi, s_b1, s_b1out = sem("x_high"), sem("b1_halves"), sem("b1_stored")
        s_tp, s_tev = sem("xn2_transposed"), sem("x2T_copied")
        s_lg, s_dif, s_exp = sem("logits_full"), sem("logits_shifted"), sem("gates_exp")
        s_row, s_rowout = sem("rows_ready"), sem("rows_stored")
        s_bef, s_pos = sem("prefix_ready"), sem("positions_full")
        s_rhs, s_stage = sem("lists_ready"), sem("expert_staged")
        s_oh, s_lf, s_lev = sem("one_hots_ready"), sem("list_full"), sem("list_copied")
        s_ct, s_ctev, s_b2f, s_b2ev = sem("combT_full"), sem("combT_copied"), sem("b2_full"), sem("b2_added")
        block = ctx.enter_context(nc.Block())
        TG = [(t0, min(4, NT - t0)) for t0 in range(0, NT, 4)]
        LG = [(0, 9), (9, NT - 9)]

        @block.sync
        def _(sp):
            sp.dma_start(at[:, :, :], d["attn"].rearrange("(p t) d -> p t d", t=NT)).then_inc(s_att, 16)
            sp.dma_start(bo[:, :], io["L0_attn_b_o"].partition_broadcast(P)).then_inc(s_att, 16)
            sp.dma_start(b1[:, :], io["b1"][:, :]).then_inc(s_b1in, 16)
            for dst, src in ((wr, io["wr"][0:P, :]), (wrr, io["wr"][P:D, :]), (br, io["br"].partition_broadcast(P)),
                             (b2, io["b2"][:, :]), (ltri, io["ltri"][:, :]), (ones, io["ones"][:, :]),
                             (iota, io["iota"][:, :]), (code, io["code"][:, :]), (pad_row, io["pad_row"][:, :]),
                             (earlier, io["earlier"][:, :])):
                sp.dma_start(dst[:, :], src).then_inc(s_in, 16)
            sp.wait_ge(s_z, 1)
            for y in d["y"]:
                sp.dma_start(y.rearrange("(p t) d -> p (t d)", p=P), zeros[:, :]).then_inc(s_zout, 16)
            sp.dma_start(d["xrow"][N:NPADDED, :], zeros[:, 0:XROW]).then_inc(s_zout, 16)
            sp.wait_ge(s_b1, 1)
            sp.dma_start(d["b1s"][0], b1h[:, :]).then_inc(s_b1out, 16)
            sp.dma_start(d["b1s"][1], b1l[:, :]).then_inc(s_b1out, 16)
            sp.wait_ge(s_row, 1)
            sp.dma_start(d["xrow"][0:N, :].rearrange("(p t) d -> p t d", t=NT), xrow[:, :, :]).then_inc(s_rowout, 16)
            sp.wait_ge(s_zout, 48)
            sp.wait_ge(s_b1out, 32)
            sp.wait_ge(s_rowout, 16)

        @block.gpsimd
        def _(pool):
            nc.gpsimd.memset(zeros[:, :], 0.0).then_inc(s_z, 1)

        @block.scalar
        def _(act):
            act.wait_ge(s_var, 1)
            nc.scalar.activation(rstd[:, :], mv[:, :, 1], ACT.Sqrt, bias=eps[:, 0:1], scale=1.0).then_inc(s_std, 1)
            act.wait_ge(s_xn, NT)
            nc.scalar.copy(x16[:, :, 0:P], xn[:, :, 0:P])
            nc.scalar.copy(x16[:, :, 2 * P:2 * P + DR], xn[:, :, P:D]).then_inc(s_hi, 1)
            for n, (x, ex) in enumerate(((gl, exp_g), (el, exp_e))):
                act.wait_ge(s_dif, n + 1)
                nc.scalar.activation(ex[:], x[:], ACT.Exp).then_inc(s_exp, 1)
            act.wait_ge(s_rhs, 1)
            with act.Fori(0, GE // 2) as e_pair:
                e = e_pair * 2
                for par in range(2):
                    if par == 0:
                        act.wait_ge(s_lf, e + 1)
                    nc.scalar.copy(place_e[:, par, :], place[:, bass.ds(e + par, 1), :]).then_inc(s_stage, 1)
                    nc.scalar.copy(rhs_e[:, par], rhs[:, bass.ds(e + par, 1)]).then_inc(s_stage, 1)

        @block.tensor
        def _(pe):
            for g, (t0, n) in enumerate(TG):
                pe.wait_ge(s_xn, t0 + n)
                for part, (rows, lo) in enumerate(((P, 0), (DR, P))):
                    if g >= 1:
                        pe.wait_ge(s_tev, 2 * g - 1 + part)
                    for j in range(n):
                        tr = nc.tensor.transpose(bank[part][0:rows, P * j:P * j + P],
                                                 xn[:, t0 + j, lo:lo + rows], ident[:, :])
                    tr.then_inc(s_tp, 1)
            pe.wait_ge(s_tev, 2 * len(TG))
            pe.wait_ge(s_in, 160)
            for k, (t0, n) in enumerate(LG):
                for t in range(t0, t0 + n):
                    o = NR * (t - t0)
                    nc.tensor.matmul(bank[2 + k][:, o:o + NR], xT[:, t, :], wr[:, :], start=True, stop=False)
                    mm = nc.tensor.matmul(bank[2 + k][:, o:o + NR], xTr[:, t, :], wrr[:, :], start=False, stop=True)
                mm.then_inc(s_lg, 1)
            pe.wait_ge(s_bef, 1)
            for k, (t0, n) in enumerate(LG):
                for t in range(t0, t0 + n):
                    o = GE * (t - t0)
                    nc.tensor.matmul(bank[4 + k][:, o:o + GE], ltri[:, :], mask[:, t].rearrange("p g e -> p (g e)"),
                                     start=True, stop=False)
                    nc.tensor.matmul(bank[4 + k][:, o:o + GE], ones[:, :], before[:, t, :], start=False, stop=True)
            nc.tensor.matmul(bank[6][:, 0:GE], ones[:, :], before[:, NT, :], start=True, stop=True).then_inc(s_pos, 1)
            for g, (t0, n) in enumerate(TG):
                if g >= 1:
                    pe.wait_ge(s_ctev, g)
                for j in range(n):
                    tr = nc.tensor.transpose(bank[7][0:GE, P * j:P * j + P],
                                             comb[:, t0 + j].rearrange("p g e -> p (g e)"), ident[:, :])
                tr.then_inc(s_ct, 1)
            pe.wait_ge(s_ctev, len(TG))
            for t in range(NT):
                if t >= 2:
                    pe.wait_ge(s_b2ev, t - 1)
                nc.tensor.matmul(bank[t % 2][:, 0:D], combT[:, t, :], b2[:, :], start=True, stop=True).then_inc(s_b2f, 1)
            pe.sem_inc(s_lf, 1)
            with pe.Fori(0, GE // 2) as e_pair:
                e = e_pair * 2
                for par in range(2):
                    pe.wait_ge(s_oh, e + par + 1)
                    for t in range(NT):
                        mm = nc.tensor.matmul(bank[2 + par][:, 0:SLOTS], one_hot[:, par, t, :], rhs_e[:, par, t, :],
                                              start=(t == 0), stop=(t == NT - 1))
                    mm.then_inc(s_lf, 1)

        @block.vector
        def _(dve):
            n = [0]

            def link(ins):
                n[0] += 1
                ins.then_inc(s_chain, 1)
                dve.wait_ge(s_chain, n[0])

            nc.vector.memset(eps[:, :], LN_EPS)
            dve.wait_ge(s_b1in, 16)
            link(nc.vector.tensor_scalar(b1h[:, :], b1[:, :], WSCALE, None, ALU.mult))
            nc.vector.scalar_tensor_tensor(out=b1l[:, :], in0=b1[:, :], scalar=WSCALE, in1=b1h[:, :],
                                           op0=ALU.mult, op1=ALU.subtract).then_inc(s_b1, 1)
            dve.wait_ge(s_att, 32)
            link(nc.vector.tensor_tensor(at[:], at[:], bo[:, :].unsqueeze(1).broadcast_to([P, NT, D]), ALU.add))
            link(nc.vector.tensor_tensor(h[:], h[:], at[:], ALU.add))
            layer_norm(nc, dve, link, h, stats, mv, rstd, xn, s_var, s_std, s_xn)
            for g, (t0, cnt) in enumerate(TG):
                for part, (rows, dst) in enumerate(((P, xT), (DR, xTr))):
                    dve.wait_ge(s_tp, 2 * g + part + 1)
                    nc.vector.tensor_copy(dst[0:rows, t0:t0 + cnt, :],
                                          bank[part][0:rows, 0:P * cnt].rearrange("q (t p) -> q t p", p=P)).then_inc(s_tev, 1)
            dve.wait_ge(s_hi, 1)
            nc.vector.tensor_tensor(x16[:, :, P:2 * P], xn[:, :, 0:P], x16[:, :, 0:P], ALU.subtract)
            nc.vector.tensor_tensor(x16[:, :, 2 * P + DR:2 * D], xn[:, :, P:D], x16[:, :, 2 * P:2 * P + DR],
                                    ALU.subtract)
            dve.wait_ge(s_in, 160)
            for k, (t0, cnt) in enumerate(LG):
                dve.wait_ge(s_lg, k + 1)
                lg = bank[2 + k][:, 0:NR * cnt].rearrange("p (t r) -> p t r", r=NR)
                nc.vector.tensor_tensor(gl[:, t0:t0 + cnt, 0, :], lg[:, :, 0:G],
                                        br[:, 0:G].unsqueeze(1).broadcast_to([P, cnt, G]), ALU.add)
                last = nc.vector.tensor_tensor(el[:, t0:t0 + cnt].rearrange("p t g e -> p t (g e)"), lg[:, :, G:NR],
                                               br[:, G:NR].unsqueeze(1).broadcast_to([P, cnt, GE]), ALU.add)
            link(last)

            def shift_and_rank(x, cmp, rank, top, width):
                link(nc.vector.tensor_reduce(top[:], x[:], AX.X, ALU.max))
                link(nc.vector.memset(cmp[:], 0.0))
                shape = list(x.shape)
                for j in range(width):
                    for lo, hi, op in ((0, j, ALU.is_gt), (j + 1, width, ALU.is_ge)):
                        if lo < hi:
                            last = nc.vector.tensor_tensor(
                                cmp[:, :, :, lo:hi, j], x[:, :, :, j:j + 1].broadcast_to(shape[:3] + [hi - lo]),
                                x[:, :, :, lo:hi], op)
                link(last)
                link(nc.vector.tensor_reduce(rank[:], cmp[:], AX.X, ALU.add))
                nc.vector.tensor_tensor(x[:], x[:], top[:].unsqueeze(3).broadcast_to(shape), ALU.subtract).then_inc(s_dif, 1)

            def gates(ex, rank, total, k):
                shape = list(ex.shape)
                link(nc.vector.tensor_scalar(rank[:], rank[:], float(k), None, ALU.is_lt))
                link(nc.vector.tensor_tensor(ex[:], ex[:], rank[:], ALU.mult))
                link(nc.vector.tensor_reduce(total[:], ex[:], AX.X, ALU.add))
                link(nc.vector.reciprocal(total[:], total[:]))
                link(nc.vector.tensor_tensor(ex[:], ex[:], total[:].unsqueeze(3).broadcast_to(shape), ALU.mult))
                link(nc.vector.scalar_tensor_tensor(out=ex[:], in0=ex[:], scalar=GATE_EPS, in1=ex[:],
                                                    op0=ALU.is_ge, op1=ALU.mult))

            shift_and_rank(gl, cmp_g, rank_g, top_g, G)
            shift_and_rank(el, cmp_e, rank_e, top_e, E)
            dve.wait_ge(s_exp, 1)
            gates(exp_g, rank_g, sum_g, KG)
            dve.wait_ge(s_exp, 2)
            gates(exp_e, rank_e, sum_e, KE)
            by_group = [P, NT, G, E]
            link(nc.vector.tensor_tensor(mask[:], rank_e[:], rank_g[:, :, 0, :].unsqueeze(3).broadcast_to(by_group), ALU.mult))
            link(nc.vector.tensor_tensor(comb[:], exp_e[:], exp_g[:, :, 0, :].unsqueeze(3).broadcast_to(by_group), ALU.mult))
            nc.vector.tensor_copy(xrow[:, :, D:XROW], comb[:].rearrange("p t g e -> p t (g e)")).then_inc(s_row, 1)
            link(nc.vector.memset(before[:, 0, :], 0.0))
            for t in range(NT):
                last = nc.vector.tensor_tensor(before[:, t + 1, :], before[:, t, :],
                                               mask[:, t].rearrange("p g e -> p (g e)"), ALU.add)
                if t < NT - 1:
                    link(last)
            last.then_inc(s_bef, 1)
            nc.vector.tensor_copy(mask_f[:], mask[:].rearrange("p t g e -> p (g e) t"))
            nc.vector.tensor_copy(code_b[:], code[:, :].unsqueeze(1).broadcast_to([P, GE, NT]))
            nc.vector.memset(rhs[:, :, :, NT:SLOTS], 0.0)
            dve.wait_ge(s_pos, 1)
            for k, (t0, cnt) in enumerate(LG):
                last = nc.vector.tensor_copy(pos_i[:, :, t0:t0 + cnt],
                                             bank[4 + k][:, 0:GE * cnt].rearrange("p (t e) -> p e t", e=GE))
            link(last)
            nc.vector.tensor_scalar(place_i[:], pos_i[:], P - 1, None, ALU.bitwise_and)
            link(nc.vector.tensor_scalar(pos_i[:], pos_i[:], P.bit_length() - 1, None, ALU.arith_shift_right))
            link(nc.vector.tensor_copy(tile_of[:], pos_i[:]))
            link(nc.vector.scalar_tensor_tensor(out=place[:], in0=place_i[:], scalar=1.0, in1=mask_f[:],
                                                op0=ALU.add, op1=ALU.mult))
            link(nc.vector.tensor_scalar(place[:], place[:], -1.0, None, ALU.add))
            for a in range(NT):
                last = nc.vector.scalar_tensor_tensor(out=rhs[:, :, :, a], in0=tile_of[:], scalar=float(a),
                                                      in1=code_b[:], op0=ALU.is_equal, op1=ALU.mult)
            last.then_inc(s_rhs, 1)
            link(nc.vector.tensor_scalar(tot[:, :], bank[6][0:1, 0:GE], float(GRAN - 1), None, ALU.add))
            link(nc.vector.tensor_copy(tot_i[:, :], tot[:, :]))
            link(nc.vector.tensor_scalar(tot_i[:, :], tot_i[:, :], GRAN.bit_length() - 1, None, ALU.arith_shift_right))
            link(nc.vector.tensor_scalar(n_f[:, :], tot_i[:, :], 1.0, None, ALU.max))
            link(nc.vector.tensor_copy(n_gran[:, :], n_f[:, :]))
            e2 = [1, GE + 1, GE]
            link(nc.vector.tensor_tensor(prod[:, :].rearrange("o (a b) -> o a b", b=GE),
                                         earlier[:, :].rearrange("o (a b) -> o a b", b=GE),
                                         n_f[:, :].unsqueeze(1).broadcast_to(e2), ALU.mult))
            link(nc.vector.tensor_reduce(g0_f[:, :], prod[:, :].rearrange("o (a b) -> o a b", b=GE), AX.X, ALU.add))
            link(nc.vector.tensor_copy(gran0[:, :], g0_f[:, :]))
            for g, (t0, cnt) in enumerate(TG):
                dve.wait_ge(s_ct, g + 1)
                nc.vector.tensor_copy(combT[:, t0:t0 + cnt, :],
                                      bank[7][0:GE, 0:P * cnt].rearrange("q (t p) -> q t p", p=P)).then_inc(s_ctev, 1)
            for t in range(NT):
                dve.wait_ge(s_b2f, t + 1)
                nc.vector.tensor_tensor(h[:, t, :], h[:, t, :], bank[t % 2][:, 0:D], ALU.add).then_inc(s_b2ev, 1)

            with dve.Fori(0, GE // 2) as e_pair:
                e = e_pair * 2
                for par in range(2):
                    dve.wait_ge(s_stage, 2 * e + 2 * par + 2)
                    for t in range(NT):
                        last = nc.vector.tensor_scalar(one_hot[:, par, t, :], iota[:, :], place_e[:, par, t:t + 1], None,
                                                       ALU.is_equal)
                    last.then_inc(s_oh, 1)
                for par in range(2):
                    dve.wait_ge(s_lf, e + par + 2)
                    nc.vector.tensor_copy(codes[:, bass.ds((e + par) * SLOTS, SLOTS)],
                                          bank[2 + par][:, 0:SLOTS]).then_inc(s_lev, 1)
            dve.wait_ge(s_lev, GE)
            nc.vector.tensor_scalar(pos_code[:, :], codes[:, :], 0.0, None, ALU.is_gt)
            link(nc.vector.tensor_scalar(empty[:, :], codes[:, :], 0.0, pad_row[:, 0:1], ALU.is_equal, ALU.mult))
            link(nc.vector.tensor_tensor(codes[:, :], codes[:, :], pos_code[:, :], ALU.subtract))
            nc.vector.scalar_tensor_tensor(out=slots[:, :], in0=codes[:, :], scalar=float(HALF_N), in1=empty[:, :],
                                           op0=ALU.add, op1=ALU.add)


def experts(nc, io, h, d, slots, n_gran, gran0):
    ctx = ExitStack()
    with ctx:
        def sb(name, shape, dt=F32):
            return ctx.enter_context(nc.sbuf_tensor(name, shape, dt))

        def sem(name):
            return ctx.enter_context(nc.semaphore(name))

        ident16 = sb("ident16", [P, P], F16)
        raw1 = sb("raw1", [P, M])
        raw1r = sb("raw1r", [P, M])
        raw2 = sb("raw2", [P, KM * D])
        w1h = [sb(f"w1h{i}", [P, M], F16) for i in range(2)]
        w1l = [sb(f"w1l{i}", [P, M], F16) for i in range(2)]
        w1hr = [sb(f"w1hr{i}", [P, M], F16) for i in range(2)]
        w1lb = [sb(f"w1lb{i}", [P, M], F16) for i in range(2)]
        w2h = [sb(f"w2h{i}", [P, KM * D], F16) for i in range(2)]
        w2l = [sb(f"w2l{i}", [P, KM * D], F16) for i in range(2)]
        BROW = (DR, DR + 32)
        KB = BROW[1] + 1
        xrow = [sb(f"xg{i}", [P, XROW]) for i in range(2)]
        xT = sb("xT", [P, 2, 3, P], F16)
        xTb = sb("xTb", [P, 2, P], F16)
        hid = [sb(f"hid{i}", [P, KM * P]) for i in range(2)]
        hidh = [sb(f"hidh{i}", [P, KM * P], F16) for i in range(2)]
        hidl = [sb(f"hidl{i}", [P, KM * P], F16) for i in range(2)]
        weight = sb("weight", [P, 2])
        part = [sb(f"part{i}", [P, D]) for i in range(2)]
        get_at = sb("get_at", [P, 2], I32)
        put_at = sb("put_at", [P, 2], I32)
        ysum = [sb(f"ysum{i}", [P, NT, D]) for i in range(2)]
        hps = [[ctx.enter_context(nc.psum_tensor(f"hps{i}{j}", [P, 512], F32)) for j in range(2)] for i in range(2)]
        ops = [ctx.enter_context(nc.psum_tensor(f"ops{i}", [P, 512], F32)) for i in range(2)]
        xps = ctx.enter_context(nc.psum_tensor("xps", [P, 1024], F16))
        PARTS = ((0, 0, 4), (1, 4, 2))

        s_id, s_raw, s_bias = sem("ident16_in"), sem("raw_weights_in"), [sem("b1_rows_in0"), sem("b1_rows_in1")]
        s_w3, s_xtb, s_set = sem("bias_pads_zeroed"), sem("ones_rows_set"), sem("first_puts_set")
        s_wh, s_wl = sem("weights_high"), sem("weights_low")
        s_idx, s_get = sem("indices_copied"), sem("rows_gathered")
        s_c = sem("weights_taken")
        s_pool_turn, s_pe_turn = sem("pool_turn"), sem("pe_turn")
        s_xf, s_xt = sem("x_transposed"), sem("xT_copied")
        s_l1, s_hh, s_h, s_hl = sem("hidden_full"), sem("hidden_high"), sem("hidden_ready"), sem("hidden_low")
        s_l2, s_ev, s_put = ([sem(f"{w}{i}") for i in range(2)] for w in ("out_full", "part_ready", "part_added"))
        s_y, s_fin, s_out = sem("sums_in"), sem("result_ready"), sem("result_stored")
        block = ctx.enter_context(nc.Block())
        W1 = io["W1"]
        W2 = io["W2"]

        def over_granules(eng, body, per_expert=lambda par, e, g: None):
            with eng.Fori(0, GE // 2) as e_pair:
                e0 = e_pair * 2
                for par in range(2):
                    first = eng.value_load(gran0[0:1, bass.ds(e0 + par, 1)], min_val=0, max_val=MAXG)
                    count = eng.value_load(n_gran[0:1, bass.ds(e0 + par, 1)], min_val=1, max_val=SLOTS // 2)
                    per_expert(par, e0 + par, first)
                    with eng.Fori(0, count) as j:
                        body(par, e0 + par, first + j, j)

        MAXG = N * KG * KE // GRAN + GE

        @block.sync
        def _(sp):
            sp.dma_start(ident16[:, :], io["ident16"][:, :]).then_inc(s_id, 16)

            def load(par, e, n):
                sp.dma_start(raw1[:, :], W1[bass.ds(e * D, P), :]).then_inc(s_raw, 16)
                for k in range(2):
                    sp.dma_start(raw1r[DR * k:DR * k + DR, :], W1[bass.ds(e * D + P, DR), :]).then_inc(s_raw, 16)
                sp.dma_start(raw2[:, :], W2[bass.ds(e, 1), :, :].rearrange("o p n -> (o p) n")).then_inc(s_raw, 16)

            def load_bias(par, e):
                for k in range(2):
                    sp.dma_start(w1lb[par][BROW[k]:BROW[k] + 1, :], d["b1s"][k, bass.ds(e, 1), :]).then_inc(s_bias[par], 16)

            load(0, 0, 0)
            sp.wait_ge(s_w3, 2)
            load_bias(0, 0)
            with sp.Fori(0, GE // 2) as e_pair:
                e0 = e_pair * 2
                for par in range(2):
                    after = (e0 + par + 1) % GE
                    sp.wait_ge(s_wl, e0 + par + 1)
                    load(1 - par, after, e0 + par + 1)
                    first = sp.value_load(gran0[0:1, bass.ds(e0 + par, 1)], min_val=0, max_val=MAXG)
                    sp.wait_ge(s_l2[1], first + 1)
                    load_bias(1 - par, after)
            total = sp.value_load(gran0[0:1, GE:GE + 1], min_val=GE, max_val=MAXG)
            for i in range(2):
                sp.wait_ge(s_put[i], total * 16 + 32)
                sp.dma_start(ysum[i][:, :, :], d["y"][i][0:N, :].rearrange("(p t) d -> p t d", t=NT)).then_inc(s_y, 16)
            for par in range(2):
                sp.wait_ge(s_bias[par], GE * 16 + 32 * (1 - par))
            sp.wait_ge(s_fin, 1)
            sp.dma_start(io["out"].rearrange("(p t) d -> p t d", t=NT), ysum[0][:, :, :]).then_inc(s_out, 16)
            sp.wait_ge(s_out, 16)

        @block.gpsimd
        def _(pool):
            nc.gpsimd.iota(put_at[:, :], [[0, 2]], base=N, channel_multiplier=1).then_inc(s_set, 1)
            nc.gpsimd.iota(get_at[:, :], [[0, 2]], base=N, channel_multiplier=1).then_inc(s_set, 1)
            pool.wait_ge(s_set, 4)

            def stand():
                pool.sem_inc(s_pool_turn, 1)

            def get():
                for i in range(2):
                    pool.indirect_dma_start(xrow[i][:, :], None, d["xrow"][:, :],
                                            bass.IndirectOffsetOnAxis(ap=get_at[:, i:i + 1], axis=0)).then_inc(s_get, 16)

            def put(g):
                for i in range(2):
                    if g is not None:
                        pool.wait_ge(s_ev[i], g + 1)
                        stand()
                    pool.indirect_dma_start(d["y"][i][:, :], bass.IndirectOffsetOnAxis(ap=put_at[:, i:i + 1], axis=0),
                                            part[i][:, :], None, compute_op=ALU.add).then_inc(s_put[i], 16)

            def body(par, e, g, j):
                pool.wait_ge(s_c, g + 1)
                for i in range(2):
                    pool.wait_ge(s_put[i], g * 16 + 16)
                stand()
                nc.gpsimd.tensor_copy(put_at[:, :], get_at[:, :]).then_inc(s_idx, 1)
                pool.wait_ge(s_idx, g * 2 + 1)
                stand()
                nc.gpsimd.tensor_copy(get_at[:, :], slots[:, bass.ds(e * SLOTS + j * 2, 2)]).then_inc(s_idx, 1)
                pool.wait_ge(s_idx, g * 2 + 2)
                stand()
                get()
                put(g)

            put(None)
            over_granules(pool, body)
            total = pool.value_load(gran0[0:1, GE:GE + 1], min_val=GE, max_val=MAXG)
            pool.wait_ge(s_c, total + 1)
            for i in range(2):
                pool.wait_ge(s_put[i], total * 16 + 16)
            stand()
            nc.gpsimd.tensor_copy(put_at[:, :], get_at[:, :]).then_inc(s_idx, 1)
            pool.wait_ge(s_idx, total * 2 + 1)
            stand()
            get()
            put(total)
            pool.wait_ge(s_pool_turn, total * 5 + 4)
            pool.wait_ge(s_pe_turn, GE)

        @block.tensor
        def _(pe):
            def transpose_x(n):
                pe.wait_ge(s_get, n * 32)
                for i in range(2):
                    for c in range(3):
                        tr = nc.tensor.transpose(xps[:, (3 * i + c) * P:(3 * i + c + 1) * P],
                                                 xrow[i][:, DR * c:DR * c + DR].bitcast(F16), ident16[:, :])
                tr.then_inc(s_xf, 1)

            def layer1(par, i):
                for bank_, c0, cn in PARTS:
                    for c in range(c0, c0 + cn):
                        o = hps[i][bank_][:, P * (c - c0):P * (c - c0) + P]
                        col = slice(P * c, P * c + P)
                        terms = ((w1h[par][:, col], xT[:, i, 0, :]), (w1h[par][:, col], xT[:, i, 1, :]),
                                 (w1l[par][:, col], xT[:, i, 0, :]), (w1hr[par][:, col], xT[:, i, 2, :]),
                                 (w1lb[par][0:KB, col], xTb[0:KB, i, :]))
                        for k, (w, x) in enumerate(terms):
                            mm = nc.tensor.matmul(o, w, x, start=(k == 0), stop=(k == len(terms) - 1))
                    mm.then_inc(s_l1, 1)

            def layer2(par, i, g):
                for n, (bank_, c0, cn) in enumerate(PARTS):
                    pe.wait_ge(s_hl, g * 4 + (2 * i + n + 1))
                    for c in range(c0, c0 + cn):
                        col, wcol = slice(P * c, P * c + P), slice(D * c, D * c + D)
                        for a, w in ((hidh, w2h), (hidh, w2l), (hidl, w2h)):
                            mm = nc.tensor.matmul(ops[i][:, 0:D], a[i][:, col], w[par][:, wcol],
                                                  start=(c == 0 and a is hidh and w is w2h),
                                                  stop=(c == KM - 1 and a is hidl))
                mm.then_inc(s_l2[i], 1)

            def start_expert(par, e, first):
                pe.wait_ge(s_wl, e + 1)
                pe.wait_ge(s_bias[par], (e - par) * 16 + 32)
                pe.sem_inc(s_pe_turn, 1)

            def body(par, e, g, j):
                pe.wait_ge(s_xt, g + 1)
                layer1(par, 0)
                layer1(par, 1)
                pe.wait_ge(s_ev[0], g + 1)
                layer2(par, 0, g)
                transpose_x(g + 2)
                pe.wait_ge(s_ev[1], g + 1)
                layer2(par, 1, g)

            for i in range(2):
                pe.sem_inc(s_l2[i], 1)
            pe.wait_ge(s_id, 16)
            pe.wait_ge(s_xtb, 2)
            transpose_x(1)
            over_granules(pe, body, start_expert)

        @block.scalar
        def _(act):
            def split_high(par, n, first):
                act.wait_ge(s_raw, n * 64)
                if first is not None:
                    act.wait_ge(s_l2[1], first + 1)
                nc.scalar.mul(w1h[par][:, :], raw1[:, :], WSCALE).then_inc(s_wh, 1)
                nc.scalar.mul(w1hr[par][:, :], raw1r[:, :], WSCALE).then_inc(s_wh, 1)
                nc.scalar.mul(w2h[par][:, :], raw2[:, :], WSCALE).then_inc(s_wh, 1)

            def body(par, e, g, j):
                for i in range(2):
                    act.wait_ge(s_l2[i], g + 1)
                    for n, (bank_, c0, cn) in enumerate(PARTS):
                        act.wait_ge(s_l1, g * 4 + (2 * i + n + 1))
                        cols = slice(P * c0, P * (c0 + cn))
                        nc.scalar.activation(hidh[i][:, cols], hps[i][bank_][:, 0:P * cn], ACT.Gelu, scale=1.0 / WSCALE)
                        nc.scalar.activation(hid[i][:, cols], hps[i][bank_][:, 0:P * cn], ACT.Gelu,
                                             scale=1.0 / WSCALE).then_inc(s_h, 1)

            split_high(0, 1, None)
            over_granules(act, body, lambda par, e, first: split_high(1 - par, e + 2, first))

        @block.vector
        def _(dve):
            def split_low(par, n):
                for k, (low, high, raw) in enumerate(((w1l[par][:, :], w1h[par][:, :], raw1[:, :]),
                                                      (w1lb[par][0:DR, :], w1hr[par][0:DR, :], raw1r[0:DR, :]),
                                                      (w2l[par][:, :], w2h[par][:, :], raw2[:, :]))):
                    dve.wait_ge(s_wh, (n - 1) * 3 + k + 1)
                    last = nc.vector.scalar_tensor_tensor(out=low, in0=raw, scalar=WSCALE, in1=high,
                                                          op0=ALU.mult, op1=ALU.subtract)
                last.then_inc(s_wl, 1)

            def copy_x(n):
                dve.wait_ge(s_xf, n)
                px = xps[:, 0:6 * P].rearrange("q (i c p) -> q i c p", i=2, c=3)
                nc.vector.tensor_copy(xT[:], px)
                nc.vector.tensor_copy(xTb[0:DR, :, :], px[0:DR, :, 2, :]).then_inc(s_xt, 1)

            def evacuate(i, g):
                dve.wait_ge(s_l2[i], g + 2)
                dve.wait_ge(s_put[i], g * 16 + 32)
                nc.vector.tensor_scalar(part[i][:, :], ops[i][:, 0:D], weight[:, i:i + 1], 1.0 / WSCALE,
                                        ALU.mult, ALU.mult).then_inc(s_ev[i], 1)

            def body(par, e, g, j):
                dve.wait_ge(s_ev[1], g + 1)
                for i in range(2):
                    w = xrow[i][:, D:XROW]
                    last = nc.vector.tensor_copy(weight[:, i:i + 1], w[:, bass.ds(e, 1)])
                last.then_inc(s_c, 1)
                for i in range(2):
                    for n, (bank_, c0, cn) in enumerate(PARTS):
                        dve.wait_ge(s_h, g * 4 + (2 * i + n + 1))
                        cols = slice(P * c0, P * (c0 + cn))
                        nc.vector.tensor_tensor(hidl[i][:, cols], hid[i][:, cols], hidh[i][:, cols],
                                                ALU.subtract).then_inc(s_hl, 1)
                dve.wait_ge(s_c, g + 2)
                evacuate(0, g)
                copy_x(g + 2)
                evacuate(1, g)

            for i in range(2):
                nc.vector.memset(part[i][:, :], 0.0).then_inc(s_set, 1)
            for i in range(2):
                nc.vector.memset(w1lb[i][DR:P, :], 0.0).then_inc(s_w3, 1)
            nc.vector.memset(xTb[DR:P, :, :], 0.0).then_inc(s_w3, 1)
            dve.wait_ge(s_w3, 3)
            for r in BROW:
                nc.vector.memset(xTb[r:r + 1, :, :], 1.0).then_inc(s_xtb, 1)
            dve.sem_inc(s_c, 1)
            for i in range(2):
                dve.sem_inc(s_ev[i], 1)
            split_low(0, 1)
            copy_x(1)
            over_granules(dve, body, lambda par, e, first: split_low(1 - par, e + 2))
            dve.wait_ge(s_y, 32)
            nc.vector.tensor_tensor(ysum[1][:], ysum[1][:], h[:], ALU.add).then_inc(s_set, 1)
            dve.wait_ge(s_set, 5)
            nc.vector.tensor_tensor(ysum[0][:], ysum[0][:], ysum[1][:], ALU.add).then_inc(s_fin, 1)


def kernel(x, x_txt, L0_tok_proj_w, L0_tok_proj_b, L0_tok_pos_emb, L0_txt_weight, L0_attn_w_q, L0_attn_w_k,
           L0_attn_w_v, L0_attn_w_o, L0_attn_b_o, L0_ffn_Wg, L0_ffn_bg, L0_ffn_We, L0_ffn_be, L0_ffn_W1,
           L0_ffn_b1, L0_ffn_W2, L0_ffn_b2):
    import numpy as np
    import concourse.bacc as bacc
    from concourse.bass_utils import run_bass_kernel_spmd

    a = np.asarray
    side = 16
    edge = 96 // side
    patches = a(x).reshape(B, 3, edge, side, edge, side).transpose(3, 5, 1, 2, 4, 0).reshape(KF, P, S_IMG * B)
    token = np.arange(N).reshape(P, NT) - HALF_N
    arrays = {
        "xpT": patches.transpose(1, 0, 2),
        "pwT": a(L0_tok_proj_w).T.reshape(KF, P, D).transpose(1, 0, 2),
        "idsT": a(x_txt).astype(np.int32).T.reshape(TXT_TILES, P).T,
        "wqkv": np.concatenate([a(L0_attn_w_q), a(L0_attn_w_k), a(L0_attn_w_v)], axis=1),
        "L0_tok_proj_b": a(L0_tok_proj_b), "L0_tok_pos_emb": a(L0_tok_pos_emb), "L0_txt_weight": a(L0_txt_weight),
        "L0_attn_w_o": a(L0_attn_w_o), "L0_attn_b_o": a(L0_attn_b_o),
        "wr": np.concatenate([a(L0_ffn_Wg), a(L0_ffn_We).transpose(1, 0, 2).reshape(D, GE)], axis=1),
        "br": np.concatenate([a(L0_ffn_bg), a(L0_ffn_be).reshape(GE)]),
        "W1": a(L0_ffn_W1).reshape(GE * D, M), "b1": a(L0_ffn_b1).reshape(GE, M),
        "W2": a(L0_ffn_W2).reshape(GE, KM, P, D).transpose(0, 2, 1, 3).reshape(GE, P, KM * D),
        "b2": a(L0_ffn_b2).reshape(GE, D),
        "ident": np.eye(P, dtype=np.float32), "ident16": np.eye(P, dtype=np.float16),
        "ltri": np.triu(np.ones((P, P), np.float16), 1), "ones": np.ones((P, P), np.float16),
        "iota": np.tile(np.arange(P, dtype=np.float16), (P, 1)),
        "code": (token + (token >= 0)).astype(np.float32),
        "pad_row": (N - HALF_N + np.arange(P, dtype=np.float32)).reshape(P, 1),
        "earlier": (np.arange(GE)[None, :] < np.arange(GE + 1)[:, None]).astype(np.float32).reshape(1, -1),
    }
    nc = bacc.Bacc("TRN2", target_bir_lowering=False, num_devices=1)
    io, inputs = {}, {}
    for name, value in arrays.items():
        value = np.ascontiguousarray(value)
        inputs[f"in_{name}"] = value
        io[name] = nc.dram_tensor(f"in_{name}", value.shape, mybir.dt.from_np(value.dtype), kind="ExternalInput").ap()
    io["out"] = nc.dram_tensor("out", [N, D], F32, kind="ExternalOutput").ap()
    build(nc, io)
    r = run_bass_kernel_spmd(nc, [inputs], core_ids=[0])
    return r.results[0]["out"].reshape(B, S, D)
```

```python
import concourse.bass as bass
from concourse import mybir
from contextlib import ExitStack

F32, F16, I32 = mybir.dt.float32, mybir.dt.float16, mybir.dt.int32
ALU, ACT, AX = mybir.AluOpType, mybir.ActivationFunctionType, mybir.AxisListType

P = 128
B, S_IMG, S_TXT = 32, 36, 32
S = S_IMG + S_TXT
N = B * S
NT = N // P
D = 192
DR = D - P
FEAT = 768
KF = FEAT // P
VOCAB = 8000
H, DH = 12, 64
INNER = H * DH
HP = H // 2
G, E, KG, KE = 4, 8, 2, 4
GE = G * E
M = 768
KM = M // P
LN_EPS, GATE_EPS = 1e-5, 1e-6
NPAIR = B // 2
S2 = 2 * S
IMG_TILES, TXT_TILES = S_IMG * B // P, S_TXT * B // P
NPADDED = N + P
XROW = D + GE
SLOTS = 18
GRAN = 2 * P
HALF_N = N // 2
WSCALE = 256.0
SG = P // B


def build(nc, io):
    ctx = ExitStack()
    with ctx:
        def sb(name, shape, dt=F32):
            return ctx.enter_context(nc.sbuf_tensor(name, shape, dt))

        def dram(name, shape, dt=F32):
            return nc.dram_tensor(name, shape, dt).ap()

        d = dict(h0=dram("h0_d", [N, D]), attn=dram("attn_d", [N, D]),
                 xrow=dram("xrow_d", [NPADDED, XROW]), b1s=dram("b1s_d", [2, GE, M], F16),
                 y=[dram("ya_d", [NPADDED, D]), dram("yb_d", [NPADDED, D])])
        ident = sb("ident", [P, P])
        ident16 = sb("ident16", [P, P], F16)
        h = sb("h", [P, NT, D])
        slots = sb("slots", [P, GE * SLOTS], I32)
        n_gran = sb("n_gran", [1, GE], I32)
        gran0 = sb("gran0", [1, GE + 1], I32)
        front(nc, io, ident, ident16, h, d)
        route(nc, io, ident, h, d, slots, n_gran, gran0)
        experts(nc, io, ident16, h, d, slots, n_gran, gran0)


def front(nc, io, ident, ident16, h0, d):
    h0_d, attn_d = d["h0"], d["attn"]
    ctx = ExitStack()
    with ctx:
        def sb(name, shape, dt=F32):
            return ctx.enter_context(nc.sbuf_tensor(name, shape, dt))

        def sem(name):
            return ctx.enter_context(nc.semaphore(name))

        bank = [ctx.enter_context(nc.psum_tensor(f"fbank{i}", [P, 512], F32)) for i in range(8)]
        tbank = [bank[2 + i][:, :].bitcast(F16) for i in range(2)]

        xp = sb("xp", [P, KF, S_IMG * B])
        pw = sb("pw", [P, KF, D])
        pos = sb("pos", [P, IMG_TILES, D])
        pbias = sb("pbias", [P, D])
        emb = sb("emb", [P, IMG_TILES, D])
        ids = sb("ids", [P, TXT_TILES], I32)
        idf = sb("idf", [P, TXT_TILES])
        idc = sb("idc", [P, TXT_TILES], I32)
        inside = sb("inside", [P, TXT_TILES])
        words = sb("words", [P, TXT_TILES, D])
        stats = sb("stats", [P, NT, 6])
        mv = sb("mv", [P, NT, 2])
        eps = sb("eps", [P, 1])
        rstd = sb("rstd", [P, NT])
        xn = sb("xn", [P, NT, D])
        x16 = sb("x16", [P, NT, 2 * D], F16)
        xnT = sb("xnT", [P, 3, N + S2], F16)
        bo = sb("bo", [P, D])
        wqkv = sb("wqkv", [P, 3 * INNER])
        wqkvr = sb("wqkvr", [P, 3 * INNER])
        wh, wl, whr, wlr = (sb(w, [P, 3 * INNER], F16) for w in ("wqkv_h", "wqkv_l", "wqkv_hr", "wqkv_lr"))
        wo = sb("wo", [P, HP, D])
        woh, wol = sb("wo_h", [P, HP, D], F16), sb("wo_l", [P, HP, D], F16)
        xq = sb("xq", [P, 3, S2], F16)
        xv = sb("xv", [P, 3, S2], F16)
        qk = sb("qk", [P, 2 * HP, S2])
        v = sb("v", [S, 2, INNER])
        mx = sb("mx", [S, 2, 2, HP])
        diff = sb("diff", [S, 2, 2, HP, S])
        ex = sb("ex", [S, 2, 2, HP, S])
        den = sb("den", [S, 2, 2, HP])
        rden = sb("rden", [S, 2, 2, HP])
        prob = sb("prob", [S, 2, 2, HP, S])
        probT = sb("probT", [S, 2, 2, HP, S])
        hTh, hTl = sb("hT_h", [P, 2, HP, S], F16), sb("hT_l", [P, 2, HP, S], F16)
        ao = sb("ao", [S, 2, D])

        s_id, s_pw, s_pos, s_idin = sem("ident_in"), sem("patch_weight_in"), sem("pos_in"), sem("ids_in")
        s_patch = [sem(f"patches{t}_in") for t in range(IMG_TILES)]
        s_w = sem("attn_weights_in")
        s_posb = sem("pos_biased")
        s_idc = sem("ids_clamped")
        s_words = sem("words_gathered")
        s_wm = sem("words_masked")
        s_pe = sem("patch_products")
        s_emb = sem("patch_rows")
        s_h0out, s_h0in = sem("h0_stored"), sem("h0_loaded")
        s_chain = sem("dve_step")
        s_var, s_std, s_xn = sem("variance_ready"), sem("std_ready"), sem("xn_ready")
        s_xh, s_x16 = sem("x_high"), sem("x_halves")
        s_wh, s_wl = sem("wqkv_high"), sem("wqkv_low")
        s_tp, s_tev = sem("xn_transposed"), sem("xnT_copied")
        s_pad = sem("pads_zeroed")
        s_xq, s_xv = sem("xq_ready"), sem("xv_ready")
        s_pf, s_pev = sem("projection_full"), sem("projection_copied")
        s_sf, s_df, s_ex, s_p = sem("scores_full"), sem("diff_ready"), sem("exp_ready"), sem("probs_ready")
        s_ptf, s_ptev = sem("probT_full"), sem("probT_copied")
        s_hf, s_hh, s_hev = sem("hT_full"), sem("hT_high"), sem("hT_halves")
        s_wf, s_wev, s_aout = sem("wo_full"), sem("wo_copied"), sem("attn_stored")
        s_ach = sem("softmax_step")
        s_turn = sem("pool_turn")

        block = ctx.enter_context(nc.Block())
        TG = [(t0, min(2, NT - t0)) for t0 in range(0, NT, 2)]
        img_rows = h0_d.rearrange("(b s) d -> b s d", s=S)
        HEADS_COLS = HP * S

        @block.sync
        def _(sp):
            sp.dma_start(ids[:, :], io["idsT"][:, :]).then_inc(s_idin, 16)
            sp.dma_start(pw[:, :, :], io["pwT"][:, :, :]).then_inc(s_pw, 16)
            for t in range(IMG_TILES):
                sp.dma_start(xp[:, :, P * t:P * t + P], io["xpT"][:, :, P * t:P * t + P]).then_inc(s_patch[t], 16)
                if t == 1:
                    sp.dma_start(pbias[:, :], io["L0_tok_proj_b"].partition_broadcast(P)).then_inc(s_pos, 16)
                    for a in range(SG):
                        src = io["L0_tok_pos_emb"].rearrange("(t a) d -> a t d", a=SG)[a]
                        sp.dma_start(pos[B * a:B * a + B, :, :], src.partition_broadcast(B)).then_inc(s_pos, 16)
            sp.dma_start(ident[:, :], io["ident"][:, :]).then_inc(s_id, 16)
            sp.dma_start(ident16[:, :], io["ident16"][:, :]).then_inc(s_id, 16)
            sp.dma_start(wqkv[:, :], io["wqkv"][0:P, :]).then_inc(s_w, 16)
            for k in range(2):
                sp.dma_start(wqkvr[DR * k:DR * k + DR, :], io["wqkv"][P:D, :]).then_inc(s_w, 16)
            sp.dma_start(wo[:, :, :], io["L0_attn_w_o"].rearrange("(c p) d -> p c d", p=P)).then_inc(s_w, 16)
            sp.dma_start(bo[:, :], io["L0_attn_b_o"].partition_broadcast(P)).then_inc(s_w, 16)
            sp.wait_ge(s_wm, 1)
            for a in range(SG):
                dst = img_rows[:, S_IMG + a:S:SG, :]
                sp.dma_start(dst, words[B * a:B * a + B, :, :]).then_inc(s_h0out, 16)
            sp.wait_ge(s_emb, IMG_TILES)
            for a in range(SG):
                dst = img_rows[:, a:S_IMG:SG, :]
                sp.dma_start(dst, emb[B * a:B * a + B, :, :]).then_inc(s_h0out, 16)
            sp.wait_ge(s_h0out, 16 * 2 * SG)
            sp.dma_start(h0[:, :, :], h0_d.rearrange("(p t) d -> p t d", t=NT)).then_inc(s_h0in, 16)
            sp.sem_inc(s_aout, 16)
            with sp.Fori(0, NPAIR) as i:
                for b in range(2):
                    sp.wait_ge(s_wev, 2 * i + b + 2)
                    sp.dma_start(attn_d[bass.ds(i * S2 + b * S, S), :], ao[:, b, :]).then_inc(s_aout, 16)
            sp.wait_ge(s_aout, 16 * B + 16)

        @block.gpsimd
        def _(pool):
            pool.wait_ge(s_idc, 1)
            for t in range(TXT_TILES):
                pool.indirect_dma_start(words[:, t, :], None, io["L0_txt_weight"][:, :],
                                        bass.IndirectOffsetOnAxis(ap=idc[:, t:t + 1], axis=0)).then_inc(s_words, 16)
            pool.wait_ge(s_tev, len(TG))
            pool.wait_ge(s_pad, 3)

            def columns(dst, k, done):
                nc.gpsimd.tensor_copy(dst[:, :, :], xnT[:, :, bass.ds(k * S2, S2)]).then_inc(done, 1)
            columns(xq, 0, s_xq)
            columns(xv, 0, s_xv)
            pool.wait_ge(s_pf, 4)
            columns(xq, 1, s_xq)
            with pool.Fori(0, NPAIR - 1) as i:
                pool.wait_ge(s_pf, 8 * i + 8)
                pool.sem_inc(s_turn, 1)
                columns(xv, i + 1, s_xv)
                pool.wait_ge(s_pf, 8 * i + 12)
                pool.sem_inc(s_turn, 1)
                columns(xq, i + 2, s_xq)
            pool.wait_ge(s_turn, 2 * (NPAIR - 1))

        @block.tensor
        def _(pe):
            pe.wait_ge(s_pw, 16)
            for t in range(IMG_TILES):
                pe.wait_ge(s_patch[t], 16)
                if t >= 2:
                    pe.wait_ge(s_emb, t - 1)
                for k in range(KF):
                    mm = nc.tensor.matmul(bank[t % 2][:, 0:D], xp[:, k, P * t:P * t + P], pw[:, k, :],
                                          start=(k == 0), stop=(k == KF - 1))
                mm.then_inc(s_pe, 1)
            pe.wait_ge(s_id, 32)
            for g, (t0, n) in enumerate(TG):
                pe.wait_ge(s_x16, g + 1)
                if g >= 2:
                    pe.wait_ge(s_tev, g - 1)
                for j in range(n):
                    for c in range(3):
                        o = P * (3 * j + c)
                        tr = nc.tensor.transpose(tbank[g % 2][:, o:o + P], x16[:, t0 + j, P * c:P * c + P],
                                                 ident16[:, :])
                tr.then_inc(s_tp, 1)
            pe.wait_ge(s_w, 80)
            pe.wait_ge(s_wl, 3)
            pe.wait_ge(s_pad, 3)

            TERMS = ((wh, 0), (wh, 1), (wl, 0), (whr, 2), (wlr, 2))

            def project_qk(k):
                pe.wait_ge(s_xq, k + 1)
                for f in range(4):
                    if not (isinstance(k, int) and 8 * k + f < 2):
                        pe.wait_ge(s_pev, 8 * k + f - 1)
                    for j in range(3):
                        c = 3 * f + j
                        for n, (w, x) in enumerate(TERMS):
                            mm = nc.tensor.matmul(bank[6 + f % 2][:, S2 * j:S2 * j + S2], w[:, P * c:P * c + P],
                                                  xq[:, x, :], start=(n == 0), stop=(n == len(TERMS) - 1))
                    mm.then_inc(s_pf, 1)

            def project_v(k):
                pe.wait_ge(s_xv, k + 1)
                for f in range(4):
                    b, half = divmod(f, 2)
                    pe.wait_ge(s_pev, 8 * k + 4 + f - 1)
                    lo, w_ = 2 * INNER + half * INNER // 2, INNER // 2
                    for n, (w, x) in enumerate(TERMS):
                        mm = nc.tensor.matmul(bank[6 + f % 2][0:S, 0:w_], xv[:, x, S * b:S * b + S], w[:, lo:lo + w_],
                                              start=(n == 0), stop=(n == len(TERMS) - 1))
                    mm.then_inc(s_pf, 1)

            def scores(k):
                pe.wait_ge(s_pev, 8 * k + 4)
                for b in range(2):
                    for hp in range(HP):
                        for odd in range(2):
                            mm = nc.tensor.matmul(bank[2 * b + odd][0:S, S * hp:S * hp + S],
                                                  qk[DH * odd:DH * odd + DH, hp, S * b:S * b + S],
                                                  qk[DH * odd:DH * odd + DH, HP + hp, S * b:S * b + S],
                                                  start=True, stop=True)
                    mm.then_inc(s_sf, 1)

            def transpose_probs(k):
                for b in range(2):
                    pe.wait_ge(s_p, 2 * k + b + 1)
                    for odd in range(2):
                        for hp in range(HP):
                            tr = nc.tensor.transpose(bank[2 * b + odd][0:S, S * hp:S * hp + S],
                                                     prob[:, b, odd, hp, :], ident[0:S, 0:S])
                    tr.then_inc(s_ptf, 1)

            def mix(k, b):
                if b == 0:
                    pe.wait_ge(s_pev, 8 * k + 8)
                pe.wait_ge(s_ptev, 2 * k + b + 1)
                pe.wait_ge(s_hev, 2 * k + b + 1)
                for hp in range(HP):
                    for odd in range(2):
                        h = 2 * hp + odd
                        mm = nc.tensor.matmul(bank[4][DH * odd:DH * odd + DH, S * hp:S * hp + S],
                                              v[:, b, DH * h:DH * h + DH], probT[:, b, odd, hp, :],
                                              start=True, stop=True)
                mm.then_inc(s_hf, 1)

            def output(k, b):
                pe.wait_ge(s_hev, 2 * k + b + 2)
                pe.wait_ge(s_wev, 2 * k + b + 1)
                for c in range(HP):
                    for n, (x, w) in enumerate(((hTh, woh), (hTh, wol), (hTl, woh))):
                        mm = nc.tensor.matmul(bank[5][0:S, 0:D], x[:, b, c, :], w[:, c, :],
                                              start=(c == 0 and n == 0), stop=(c == HP - 1 and n == 2))
                mm.then_inc(s_wf, 1)

            def attend(k, first=False):
                transpose_probs(k)
                for b in range(2):
                    if not first:
                        output(k - 1, b)
                    mix(k, b)

            def prepare(k):
                scores(k)
                project_v(k)
                project_qk(k + 1)

            project_qk(0)
            prepare(0)
            attend(0, first=True)
            prepare(1)
            with pe.Fori(1, NPAIR - 1) as i:
                attend(i)
                prepare(i + 1)
            attend(NPAIR - 1)
            for b in range(2):
                output(NPAIR - 1, b)

        @block.scalar
        def _(act):
            act.wait_ge(s_w, 80)
            for dst, src in ((wh, wqkv), (whr, wqkvr), (woh, wo)):
                nc.scalar.mul(dst[:], src[:], WSCALE).then_inc(s_wh, 1)
            act.wait_ge(s_var, 1)
            act.wait_ge(s_pad, 1)
            nc.scalar.activation(rstd[:, :], mv[:, :, 1], ACT.Sqrt, bias=eps[:, 0:1], scale=1.0).then_inc(s_std, 1)

            for g, (t0, n) in enumerate(TG):
                act.wait_ge(s_xn, t0 + n)
                nc.scalar.copy(x16[:, t0:t0 + n, 0:P], xn[:, t0:t0 + n, 0:P])
                nc.scalar.copy(x16[:, t0:t0 + n, 2 * P:2 * P + DR], xn[:, t0:t0 + n, P:D]).then_inc(s_xh, 1)

            def copy_qk(k):
                for f in range(4):
                    act.wait_ge(s_pf, 8 * k + f + 1)
                    nc.scalar.mul(qk[:, 3 * f:3 * f + 3, :], bank[6 + f % 2][:, 0:3 * S2], 1 / WSCALE).then_inc(s_pev, 1)

            def copy_v(k, f):
                b, half = divmod(f, 2)
                act.wait_ge(s_pf, 8 * k + 4 + f + 1)
                w = INNER // 2
                nc.scalar.mul(v[:, b, w * half:w * half + w], bank[6 + f % 2][0:S, 0:w], 1 / WSCALE).then_inc(s_pev, 1)

            def exponentials(k, b):
                act.wait_ge(s_df, 2 * k + b + 1)
                nc.scalar.activation(ex[:, b], diff[:, b], ACT.Exp, scale=float(DH) ** -0.5).then_inc(s_ex, 1)

            def copy_output(k, b):
                act.wait_ge(s_wf, 2 * k + b + 1)
                act.wait_ge(s_aout, 32 * k + 16)
                nc.scalar.mul(ao[:, b, :], bank[5][0:S, 0:D], 1 / WSCALE).then_inc(s_wev, 1)

            def attend(k, first=False):
                for b in range(2):
                    act.wait_ge(s_ptf, 2 * k + b + 1)
                    for odd in range(2):
                        cp = nc.scalar.copy(probT[:, b, odd], bank[2 * b + odd][0:S, 0:HEADS_COLS])
                    cp.then_inc(s_ptev, 1)
                for b in range(2):
                    if not first:
                        copy_output(k - 1, b)
                    act.wait_ge(s_hf, 2 * k + b + 1)
                    nc.scalar.copy(hTh[:, b], bank[4][:, 0:HEADS_COLS]).then_inc(s_hh, 1)

            def prepare(k):
                for b in range(2):
                    copy_v(k, 2 * b)
                    copy_v(k, 2 * b + 1)
                    exponentials(k, b)
                copy_qk(k + 1)

            act.sem_inc(s_wev, 1)
            copy_qk(0)
            prepare(0)
            attend(0, first=True)
            prepare(1)
            with act.Fori(1, NPAIR - 1) as i:
                attend(i)
                prepare(i + 1)
            attend(NPAIR - 1)
            for b in range(2):
                copy_output(NPAIR - 1, b)

        @block.vector
        def _(dve):
            n = [0]

            def link(ins):
                n[0] += 1
                ins.then_inc(s_chain, 1)
                dve.wait_ge(s_chain, n[0])

            nc.vector.memset(eps[:, :], LN_EPS).then_inc(s_pad, 1)
            nc.vector.memset(xnT[:, :, N:N + S2], 0.0).then_inc(s_pad, 1)
            nc.vector.memset(wlr[DR:P, :], 0.0).then_inc(s_pad, 1)
            dve.wait_ge(s_idin, 16)
            link(nc.vector.tensor_copy(idf[:, :], ids[:, :]))
            nc.vector.tensor_scalar(idc[:, :], idf[:, :], 0.0, float(VOCAB - 1), ALU.max, ALU.min).then_inc(s_idc, 1)
            link(nc.vector.tensor_scalar(inside[:, :], idf[:, :], 0.0, None, ALU.is_ge))
            link(nc.vector.scalar_tensor_tensor(out=inside[:, :], in0=idf[:, :], scalar=float(VOCAB - 1),
                                                in1=inside[:, :], op0=ALU.is_le, op1=ALU.mult))
            dve.wait_ge(s_pos, 16 * (1 + SG))
            link(nc.vector.tensor_tensor(pos[:, :, :], pos[:, :, :],
                                         pbias[:, :].unsqueeze(1).broadcast_to([P, IMG_TILES, D]), ALU.add))
            for t in range(IMG_TILES):
                dve.wait_ge(s_pe, t + 1)
                nc.vector.tensor_tensor(emb[:, t, :], bank[t % 2][:, 0:D], pos[:, t, :], ALU.add).then_inc(s_emb, 1)
                if t == 4:
                    dve.wait_ge(s_words, 16 * TXT_TILES)
                    nc.vector.tensor_tensor(words[:, :, :], words[:, :, :],
                                            inside[:, :].unsqueeze(2).broadcast_to([P, TXT_TILES, D]),
                                            ALU.mult).then_inc(s_wm, 1)
            for n_, (low, high, raw, rows) in enumerate(((wl, wh, wqkv, P), (wlr, whr, wqkvr, DR), (wol, woh, wo, P))):
                dve.wait_ge(s_wh, n_ + 1)
                nc.vector.scalar_tensor_tensor(out=low[0:rows], in0=raw[0:rows], scalar=WSCALE,
                                               in1=high[0:rows], op0=ALU.mult, op1=ALU.subtract).then_inc(s_wl, 1)
            def copy_columns(g):
                t0, cnt = TG[g]
                dve.wait_ge(s_tp, g + 1)
                out = xnT[:, :, 0:N].rearrange("q c (p t) -> q t c p", t=NT)[:, t0:t0 + cnt]
                src = tbank[g % 2][:, 0:3 * P * cnt].rearrange("q (t c p) -> q t c p", c=3, p=P)
                nc.vector.tensor_copy(out, src).then_inc(s_tev, 1)

            dve.wait_ge(s_h0in, 16)
            layer_norm(nc, dve, link, h0, stats, mv, rstd, xn, s_var, s_std, s_xn)
            for g, (t0, cnt) in enumerate(TG):
                dve.wait_ge(s_xh, g + 1)
                ts = slice(t0, t0 + cnt)
                nc.vector.tensor_tensor(x16[:, ts, P:2 * P], xn[:, ts, 0:P], x16[:, ts, 0:P], ALU.subtract)
                nc.vector.tensor_tensor(x16[:, ts, 2 * P + DR:2 * D], xn[:, ts, P:D], x16[:, ts, 2 * P:2 * P + DR],
                                        ALU.subtract).then_inc(s_x16, 1)
                if g >= 1:
                    copy_columns(g - 1)
            copy_columns(len(TG) - 1)
            dve.wait_ge(s_w, 80)
            nc.vector.tensor_tensor(h0[:], h0[:], bo[:, :].unsqueeze(1).broadcast_to([P, NT, D]), ALU.add)

            def softmax(k):
                for b in range(2):
                    dve.wait_ge(s_sf, 2 * k + b + 1)
                    for odd in range(2):
                        sc = bank[2 * b + odd][0:S, 0:HEADS_COLS].rearrange("q (h k) -> q h k", k=S)
                        mxs = nc.vector.tensor_reduce(mx[:, b, odd, :], sc, AX.X, ALU.max)
                    mxs.then_inc(s_ach, 1)
                    dve.wait_ge(s_ach, 6 * k + b + 1)
                    for odd in range(2):
                        sc = bank[2 * b + odd][0:S, 0:HEADS_COLS].rearrange("q (h k) -> q h k", k=S)
                        sub = nc.vector.tensor_tensor(diff[:, b, odd], sc,
                                                      mx[:, b, odd, :].unsqueeze(2).broadcast_to([S, HP, S]),
                                                      ALU.subtract)
                    sub.then_inc(s_df, 1)
                for b in range(2):
                    dve.wait_ge(s_ex, 2 * k + b + 1)
                    nc.vector.tensor_reduce(den[:, b], ex[:, b], AX.X, ALU.add).then_inc(s_ach, 1)
                    dve.wait_ge(s_ach, 6 * k + 2 * b + 3)
                    nc.vector.reciprocal(rden[:, b], den[:, b]).then_inc(s_ach, 1)
                    dve.wait_ge(s_ach, 6 * k + 2 * b + 4)
                    nc.vector.tensor_tensor(prob[:, b], ex[:, b],
                                            rden[:, b].unsqueeze(3).broadcast_to([S, 2, HP, S]),
                                            ALU.mult).then_inc(s_p, 1)

            def low_heads(k):
                for b in range(2):
                    dve.wait_ge(s_hh, 2 * k + b + 1)
                    nc.vector.tensor_tensor(hTl[:, b], bank[4][:, 0:HEADS_COLS].rearrange("q (h k) -> q h k", k=S),
                                            hTh[:, b], ALU.subtract).then_inc(s_hev, 1)

            dve.sem_inc(s_hev, 1)
            softmax(0)
            with dve.Fori(0, NPAIR - 1) as i:
                low_heads(i)
                softmax(i + 1)
            low_heads(NPAIR - 1)


def layer_norm(nc, dve, link, h, stats, mv, rstd, xn, s_var, s_std, s_xn):
    for t in range(NT):
        last = nc.vector.bn_stats(stats[:, t, :], h[:, t, :])
    link(last)
    for t in range(NT):
        last = nc.vector.bn_aggr(mv[:, t, :], stats[:, t, :])
    last.then_inc(s_var, 1)
    dve.wait_ge(s_std, 1)
    link(nc.vector.reciprocal(rstd[:, :], rstd[:, :]))
    for t in range(NT):
        nc.vector.tensor_scalar(xn[:, t, :], h[:, t, :], mv[:, t, 0:1], rstd[:, t:t + 1],
                                ALU.subtract, ALU.mult).then_inc(s_xn, 1)


def route(nc, io, ident, h, d, slots, n_gran, gran0):
    ctx = ExitStack()
    with ctx:
        def sb(name, shape, dt=F32):
            return ctx.enter_context(nc.sbuf_tensor(name, shape, dt))

        def sem(name):
            return ctx.enter_context(nc.semaphore(name))

        bank = [ctx.enter_context(nc.psum_tensor(f"rbank{i}", [P, 512], F32)) for i in range(8)]
        NR = G + GE
        TE = NT * GE
        at = sb("at", [P, NT, D])
        wr = sb("wr", [P, NR])
        wrr = sb("wrr", [DR, NR])
        br = sb("br", [P, NR])
        b2 = sb("b2", [GE, D])
        b1 = sb("b1", [GE, M])
        b1h = sb("b1h", [GE, M], F16)
        b1l = sb("b1l", [GE, M], F16)
        stats = sb("stats2", [P, NT, 6])
        mv = sb("mv2", [P, NT, 2])
        eps = sb("eps2", [P, 1])
        rstd = sb("rstd2", [P, NT])
        xn = sb("xn2", [P, NT, D])
        xrow = sb("xrow", [P, NT, XROW])
        x16 = xrow[:, :, 0:D].bitcast(F16)
        xT = sb("x2T", [P, NT, P])
        xTr = sb("x2Tr", [DR, NT, P])
        zeros = sb("zeros", [P, NPADDED // P * D])
        gl = sb("gl", [P, NT, 1, G])
        el = sb("el", [P, NT, G, E])
        cmp_g = sb("cmp_g", [P, NT, 1, G, G], F16)
        cmp_e = sb("cmp_e", [P, NT, G, E, E], F16)
        rank_g, rank_e = sb("rank_g", [P, NT, 1, G]), sb("rank_e", [P, NT, G, E])
        top_g, top_e = sb("top_g", [P, NT, 1]), sb("top_e", [P, NT, G])
        exp_g, exp_e = sb("exp_g", [P, NT, 1, G]), sb("exp_e", [P, NT, G, E])
        sum_g, sum_e = sb("sum_g", [P, NT, 1]), sb("sum_e", [P, NT, G])
        mask = sb("mask", [P, NT, G, E], F16)
        comb = sb("comb", [P, NT, G, E])
        before = sb("before", [P, NT + 1, GE], F16)
        ltri = sb("ltri", [P, P], F16)
        ones = sb("ones", [P, P], F16)
        pos_f = sb("pos_f", [P, GE, NT])
        pos_i = sb("pos_i", [P, GE, NT], I32)
        place_i = sb("place_i", [P, GE, NT], I32)
        place = sb("place", [P, GE, NT])
        tile_of = sb("tile_of", [P, GE, NT])
        code = sb("code", [P, NT])
        code_b = sb("code_b", [P, GE, NT])
        mask_f = sb("mask_f", [P, GE, NT])
        rhs = sb("rhs", [P, GE, NT, SLOTS], F16)
        iota = sb("iota", [P, P, NT], F16)
        one_hot = sb("one_hot", [P, 2, P, NT], F16)
        place_e = sb("place_e", [P, 2, NT], F16)
        rhs_e = sb("rhs_e", [P, 2, NT, SLOTS], F16)
        codes = sb("codes", [P, GE * SLOTS])
        pos_code = sb("pos_code", [P, GE * SLOTS])
        pad_row = sb("pad_row", [P, 1])
        empty = sb("empty", [P, GE * SLOTS])
        tot = sb("tot", [1, GE])
        tot_i = sb("tot_i", [1, GE], I32)
        n_f = sb("n_f", [1, GE])
        earlier = sb("earlier", [1, (GE + 1) * GE])
        prod = sb("prod", [1, (GE + 1) * GE])
        g0_f = sb("g0_f", [1, GE + 1])
        combT = sb("combT", [GE, NT, P])

        s_in, s_b1in = sem("router_in"), sem("b1_in")
        s_att = [sem(f"attn{k}_in") for k in range(3)]
        s_chain, s_z, s_zout = sem("route_step"), sem("zeros_ready"), sem("zeros_stored")
        s_var, s_std, s_xn = sem("variance2"), sem("std2"), sem("xn2_ready")
        s_hi, s_b1, s_b1out = sem("x_high"), sem("b1_halves"), sem("b1_stored")
        s_tp, s_tev = sem("xn2_transposed"), sem("x2T_copied")
        s_lg, s_dif, s_exp = sem("logits_full"), sem("logits_shifted"), sem("gates_exp")
        s_row, s_rowout = sem("rows_ready"), sem("rows_stored")
        s_bef, s_pos = sem("prefix_ready"), sem("positions_full")
        s_rhs, s_stage = sem("lists_ready"), sem("expert_staged")
        s_oh, s_lf, s_lev = sem("one_hots_ready"), sem("list_full"), sem("list_copied")
        s_ct, s_ctev, s_b2f, s_b2ev = sem("combT_full"), sem("combT_copied"), sem("b2_full"), sem("b2_added")
        block = ctx.enter_context(nc.Block())
        TG = [(t0, min(4, NT - t0)) for t0 in range(0, NT, 4)]
        AG = [(0, 6), (6, 12), (12, NT)]
        LG = [(0, 9), (9, NT - 9)]

        @block.sync
        def _(sp):
            for k, (t0, t1) in enumerate(AG):
                sp.dma_start(at[:, t0:t1, :], d["attn"].rearrange("(p t) d -> p t d", t=NT)[:, t0:t1, :]).then_inc(s_att[k], 16)
            sp.dma_start(b1[:, :], io["b1"][:, :]).then_inc(s_b1in, 16)
            for dst, src in ((wr, io["wr"][0:P, :]), (wrr, io["wr"][P:D, :]), (br, io["br"].partition_broadcast(P)),
                             (b2, io["b2"][:, :]), (ltri, io["ltri"][:, :]), (ones, io["ones"][:, :]),
                             (iota, io["iota"]), (code, io["code"][:, :]), (pad_row, io["pad_row"][:, :]),
                             (earlier, io["earlier"][:, :])):
                sp.dma_start(dst[:], src).then_inc(s_in, 16)
            sp.wait_ge(s_z, 1)
            for y in d["y"]:
                sp.dma_start(y.rearrange("(p t) d -> p (t d)", p=P), zeros[:, :]).then_inc(s_zout, 16)
            sp.dma_start(d["xrow"][N:NPADDED, :], zeros[:, 0:XROW]).then_inc(s_zout, 16)
            sp.wait_ge(s_b1, 1)
            sp.dma_start(d["b1s"][0], b1h[:, :]).then_inc(s_b1out, 16)
            sp.dma_start(d["b1s"][1], b1l[:, :]).then_inc(s_b1out, 16)
            sp.wait_ge(s_row, 1)
            sp.dma_start(d["xrow"][0:N, :].rearrange("(p t) d -> p t d", t=NT), xrow[:, :, :]).then_inc(s_rowout, 16)
            sp.wait_ge(s_zout, 48)
            sp.wait_ge(s_b1out, 32)
            sp.wait_ge(s_rowout, 16)

        @block.gpsimd
        def _(pool):
            nc.gpsimd.memset(zeros[:, :], 0.0).then_inc(s_z, 1)

        @block.scalar
        def _(act):
            act.wait_ge(s_var, 1)
            nc.scalar.activation(rstd[:, :], mv[:, :, 1], ACT.Sqrt, bias=eps[:, 0:1], scale=1.0).then_inc(s_std, 1)
            act.wait_ge(s_xn, NT)
            nc.scalar.copy(x16[:, :, 0:P], xn[:, :, 0:P])
            nc.scalar.copy(x16[:, :, 2 * P:2 * P + DR], xn[:, :, P:D]).then_inc(s_hi, 1)
            for n, (x, ex) in enumerate(((gl, exp_g), (el, exp_e))):
                act.wait_ge(s_dif, n + 1)
                nc.scalar.activation(ex[:], x[:], ACT.Exp).then_inc(s_exp, 1)
            act.wait_ge(s_rhs, 1)
            with act.Fori(0, GE // 2) as e_pair:
                e = e_pair * 2
                for par in range(2):
                    if par == 0:
                        act.wait_ge(s_lf, e + 1)
                    nc.scalar.copy(place_e[:, par, :], place[:, bass.ds(e + par, 1), :]).then_inc(s_stage, 1)
                    nc.scalar.copy(rhs_e[:, par], rhs[:, bass.ds(e + par, 1)]).then_inc(s_stage, 1)

        @block.tensor
        def _(pe):
            for g, (t0, n) in enumerate(TG):
                pe.wait_ge(s_xn, t0 + n)
                for part, (rows, lo) in enumerate(((P, 0), (DR, P))):
                    if g >= 1:
                        pe.wait_ge(s_tev, 2 * g - 1 + part)
                    for j in range(n):
                        tr = nc.tensor.transpose(bank[part][0:rows, P * j:P * j + P],
                                                 xn[:, t0 + j, lo:lo + rows], ident[:, :])
                    tr.then_inc(s_tp, 1)
            pe.wait_ge(s_tev, 2 * len(TG))
            pe.wait_ge(s_in, 160)
            for k, (t0, n) in enumerate(LG):
                for t in range(t0, t0 + n):
                    o = NR * (t - t0)
                    nc.tensor.matmul(bank[2 + k][:, o:o + NR], xT[:, t, :], wr[:, :], start=True, stop=False)
                    mm = nc.tensor.matmul(bank[2 + k][:, o:o + NR], xTr[:, t, :], wrr[:, :], start=False, stop=True)
                mm.then_inc(s_lg, 1)
            pe.wait_ge(s_bef, 1)
            for k, (t0, n) in enumerate(LG):
                for t in range(t0, t0 + n):
                    o = GE * (t - t0)
                    nc.tensor.matmul(bank[4 + k][:, o:o + GE], ltri[:, :], mask[:, t].rearrange("p g e -> p (g e)"),
                                     start=True, stop=False)
                    nc.tensor.matmul(bank[4 + k][:, o:o + GE], ones[:, :], before[:, t, :], start=False, stop=True)
            nc.tensor.matmul(bank[6][:, 0:GE], ones[:, :], before[:, NT, :], start=True, stop=True).then_inc(s_pos, 1)
            for g, (t0, n) in enumerate(TG):
                if g >= 1:
                    pe.wait_ge(s_ctev, g)
                for j in range(n):
                    tr = nc.tensor.transpose(bank[7][0:GE, P * j:P * j + P],
                                             comb[:, t0 + j].rearrange("p g e -> p (g e)"), ident[:, :])
                tr.then_inc(s_ct, 1)
            pe.wait_ge(s_ctev, len(TG))
            for t in range(NT):
                if t >= 2:
                    pe.wait_ge(s_b2ev, t - 1)
                nc.tensor.matmul(bank[t % 2][:, 0:D], combT[:, t, :], b2[:, :], start=True, stop=True).then_inc(s_b2f, 1)
            pe.sem_inc(s_lf, 1)
            with pe.Fori(0, GE // 2) as e_pair:
                e = e_pair * 2
                for par in range(2):
                    pe.wait_ge(s_oh, e + par + 1)
                    for t in range(NT):
                        mm = nc.tensor.matmul(bank[2 + par][:, 0:SLOTS], one_hot[:, par, :, t], rhs_e[:, par, t, :],
                                              start=(t == 0), stop=(t == NT - 1))
                    mm.then_inc(s_lf, 1)

        @block.vector
        def _(dve):
            n = [0]

            def link(ins):
                n[0] += 1
                ins.then_inc(s_chain, 1)
                dve.wait_ge(s_chain, n[0])

            nc.vector.memset(eps[:, :], LN_EPS)
            dve.wait_ge(s_b1in, 16)
            link(nc.vector.tensor_scalar(b1h[:, :], b1[:, :], WSCALE, None, ALU.mult))
            nc.vector.scalar_tensor_tensor(out=b1l[:, :], in0=b1[:, :], scalar=WSCALE, in1=b1h[:, :],
                                           op0=ALU.mult, op1=ALU.subtract).then_inc(s_b1, 1)
            for k, (t0, t1) in enumerate(AG):
                dve.wait_ge(s_att[k], 16)
                last = nc.vector.tensor_tensor(h[:, t0:t1], h[:, t0:t1], at[:, t0:t1], ALU.add)
            link(last)
            layer_norm(nc, dve, link, h, stats, mv, rstd, xn, s_var, s_std, s_xn)
            for g, (t0, cnt) in enumerate(TG):
                for part, (rows, dst) in enumerate(((P, xT), (DR, xTr))):
                    dve.wait_ge(s_tp, 2 * g + part + 1)
                    nc.vector.tensor_copy(dst[0:rows, t0:t0 + cnt, :],
                                          bank[part][0:rows, 0:P * cnt].rearrange("q (t p) -> q t p", p=P)).then_inc(s_tev, 1)
            dve.wait_ge(s_hi, 1)
            nc.vector.tensor_tensor(x16[:, :, P:2 * P], xn[:, :, 0:P], x16[:, :, 0:P], ALU.subtract)
            nc.vector.tensor_tensor(x16[:, :, 2 * P + DR:2 * D], xn[:, :, P:D], x16[:, :, 2 * P:2 * P + DR],
                                    ALU.subtract)
            dve.wait_ge(s_in, 160)
            for k, (t0, cnt) in enumerate(LG):
                dve.wait_ge(s_lg, k + 1)
                lg = bank[2 + k][:, 0:NR * cnt].rearrange("p (t r) -> p t r", r=NR)
                nc.vector.tensor_tensor(gl[:, t0:t0 + cnt, 0, :], lg[:, :, 0:G],
                                        br[:, 0:G].unsqueeze(1).broadcast_to([P, cnt, G]), ALU.add)
                last = nc.vector.tensor_tensor(el[:, t0:t0 + cnt].rearrange("p t g e -> p t (g e)"), lg[:, :, G:NR],
                                               br[:, G:NR].unsqueeze(1).broadcast_to([P, cnt, GE]), ALU.add)
            link(last)

            def shift_and_rank(x, cmp, rank, top, width):
                link(nc.vector.tensor_reduce(top[:], x[:], AX.X, ALU.max))
                link(nc.vector.memset(cmp[:], 0.0))
                shape = list(x.shape)
                for j in range(width):
                    for lo, hi, op in ((0, j, ALU.is_gt), (j + 1, width, ALU.is_ge)):
                        if lo < hi:
                            last = nc.vector.tensor_tensor(
                                cmp[:, :, :, lo:hi, j], x[:, :, :, j:j + 1].broadcast_to(shape[:3] + [hi - lo]),
                                x[:, :, :, lo:hi], op)
                link(last)
                link(nc.vector.tensor_reduce(rank[:], cmp[:], AX.X, ALU.add))
                nc.vector.tensor_tensor(x[:], x[:], top[:].unsqueeze(3).broadcast_to(shape), ALU.subtract).then_inc(s_dif, 1)

            def gates(ex, rank, total, k):
                shape = list(ex.shape)
                link(nc.vector.tensor_scalar(rank[:], rank[:], float(k), None, ALU.is_lt))
                link(nc.vector.tensor_tensor(ex[:], ex[:], rank[:], ALU.mult))
                link(nc.vector.tensor_reduce(total[:], ex[:], AX.X, ALU.add))
                link(nc.vector.reciprocal(total[:], total[:]))
                link(nc.vector.tensor_tensor(ex[:], ex[:], total[:].unsqueeze(3).broadcast_to(shape), ALU.mult))
                link(nc.vector.scalar_tensor_tensor(out=ex[:], in0=ex[:], scalar=GATE_EPS, in1=ex[:],
                                                    op0=ALU.is_ge, op1=ALU.mult))

            shift_and_rank(gl, cmp_g, rank_g, top_g, G)
            shift_and_rank(el, cmp_e, rank_e, top_e, E)
            dve.wait_ge(s_exp, 1)
            gates(exp_g, rank_g, sum_g, KG)
            dve.wait_ge(s_exp, 2)
            gates(exp_e, rank_e, sum_e, KE)
            by_group = [P, NT, G, E]
            link(nc.vector.tensor_tensor(mask[:], rank_e[:], rank_g[:, :, 0, :].unsqueeze(3).broadcast_to(by_group), ALU.mult))
            link(nc.vector.tensor_tensor(comb[:], exp_e[:], exp_g[:, :, 0, :].unsqueeze(3).broadcast_to(by_group), ALU.mult))
            nc.vector.tensor_copy(xrow[:, :, D:XROW], comb[:].rearrange("p t g e -> p t (g e)")).then_inc(s_row, 1)
            link(nc.vector.memset(before[:, 0, :], 0.0))
            for t in range(NT):
                last = nc.vector.tensor_tensor(before[:, t + 1, :], before[:, t, :],
                                               mask[:, t].rearrange("p g e -> p (g e)"), ALU.add)
                if t < NT - 1:
                    link(last)
            last.then_inc(s_bef, 1)
            nc.vector.tensor_copy(mask_f[:], mask[:].rearrange("p t g e -> p (g e) t"))
            nc.vector.tensor_copy(code_b[:], code[:, :].unsqueeze(1).broadcast_to([P, GE, NT]))
            nc.vector.memset(rhs[:, :, :, NT:SLOTS], 0.0)
            dve.wait_ge(s_pos, 1)
            for k, (t0, cnt) in enumerate(LG):
                last = nc.vector.tensor_copy(pos_i[:, :, t0:t0 + cnt],
                                             bank[4 + k][:, 0:GE * cnt].rearrange("p (t e) -> p e t", e=GE))
            link(last)
            nc.vector.tensor_scalar(place_i[:], pos_i[:], P - 1, None, ALU.bitwise_and)
            link(nc.vector.tensor_scalar(pos_i[:], pos_i[:], P.bit_length() - 1, None, ALU.arith_shift_right))
            link(nc.vector.tensor_copy(tile_of[:], pos_i[:]))
            link(nc.vector.scalar_tensor_tensor(out=place[:], in0=place_i[:], scalar=1.0, in1=mask_f[:],
                                                op0=ALU.add, op1=ALU.mult))
            link(nc.vector.tensor_scalar(place[:], place[:], -1.0, None, ALU.add))
            for a in range(NT):
                last = nc.vector.scalar_tensor_tensor(out=rhs[:, :, :, a], in0=tile_of[:], scalar=float(a),
                                                      in1=code_b[:], op0=ALU.is_equal, op1=ALU.mult)
            last.then_inc(s_rhs, 1)
            link(nc.vector.tensor_scalar(tot[:, :], bank[6][0:1, 0:GE], float(GRAN - 1), None, ALU.add))
            link(nc.vector.tensor_copy(tot_i[:, :], tot[:, :]))
            link(nc.vector.tensor_scalar(tot_i[:, :], tot_i[:, :], GRAN.bit_length() - 1, None, ALU.arith_shift_right))
            link(nc.vector.tensor_scalar(n_f[:, :], tot_i[:, :], 1.0, None, ALU.max))
            link(nc.vector.tensor_copy(n_gran[:, :], n_f[:, :]))
            e2 = [1, GE + 1, GE]
            link(nc.vector.tensor_tensor(prod[:, :].rearrange("o (a b) -> o a b", b=GE),
                                         earlier[:, :].rearrange("o (a b) -> o a b", b=GE),
                                         n_f[:, :].unsqueeze(1).broadcast_to(e2), ALU.mult))
            link(nc.vector.tensor_reduce(g0_f[:, :], prod[:, :].rearrange("o (a b) -> o a b", b=GE), AX.X, ALU.add))
            link(nc.vector.tensor_copy(gran0[:, :], g0_f[:, :]))
            for g, (t0, cnt) in enumerate(TG):
                dve.wait_ge(s_ct, g + 1)
                nc.vector.tensor_copy(combT[:, t0:t0 + cnt, :],
                                      bank[7][0:GE, 0:P * cnt].rearrange("q (t p) -> q t p", p=P)).then_inc(s_ctev, 1)
            for t in range(NT):
                dve.wait_ge(s_b2f, t + 1)
                nc.vector.tensor_tensor(h[:, t, :], h[:, t, :], bank[t % 2][:, 0:D], ALU.add).then_inc(s_b2ev, 1)

            with dve.Fori(0, GE // 2) as e_pair:
                e = e_pair * 2
                for par in range(2):
                    dve.wait_ge(s_stage, 2 * e + 2 * par + 2)
                    nc.vector.tensor_tensor(one_hot[:, par], place_e[:, par, :].unsqueeze(1).broadcast_to([P, P, NT]),
                                            iota[:, :, :], ALU.is_equal).then_inc(s_oh, 1)
                for par in range(2):
                    dve.wait_ge(s_lf, e + par + 2)
                    nc.vector.tensor_copy(codes[:, bass.ds((e + par) * SLOTS, SLOTS)],
                                          bank[2 + par][:, 0:SLOTS]).then_inc(s_lev, 1)
            dve.wait_ge(s_lev, GE)
            nc.vector.tensor_scalar(pos_code[:, :], codes[:, :], 0.0, None, ALU.is_gt)
            link(nc.vector.tensor_scalar(empty[:, :], codes[:, :], 0.0, pad_row[:, 0:1], ALU.is_equal, ALU.mult))
            link(nc.vector.tensor_tensor(codes[:, :], codes[:, :], pos_code[:, :], ALU.subtract))
            nc.vector.scalar_tensor_tensor(out=slots[:, :], in0=codes[:, :], scalar=float(HALF_N), in1=empty[:, :],
                                           op0=ALU.add, op1=ALU.add)


def experts(nc, io, ident16, h, d, slots, n_gran, gran0):
    ctx = ExitStack()
    with ctx:
        def sb(name, shape, dt=F32):
            return ctx.enter_context(nc.sbuf_tensor(name, shape, dt))

        def sem(name):
            return ctx.enter_context(nc.semaphore(name))

        raw1 = sb("raw1", [P, M])
        raw1r = sb("raw1r", [P, M])
        raw2 = sb("raw2", [P, KM * D])
        w1h = [sb(f"w1h{i}", [P, M], F16) for i in range(2)]
        w1l = [sb(f"w1l{i}", [P, M], F16) for i in range(2)]
        w1hr = [sb(f"w1hr{i}", [P, M], F16) for i in range(2)]
        w1lb = [sb(f"w1lb{i}", [P, M], F16) for i in range(2)]
        w2h = [sb(f"w2h{i}", [P, KM * D], F16) for i in range(2)]
        w2l = [sb(f"w2l{i}", [P, KM * D], F16) for i in range(2)]
        BROW = (DR, DR + 32)
        KB = BROW[1] + 1
        xrow = [sb(f"xg{i}", [P, XROW]) for i in range(2)]
        xT = sb("xT", [P, 2, 3, P], F16)
        xTb = sb("xTb", [P, 2, P], F16)
        hid = [sb(f"hid{i}", [P, KM * P]) for i in range(2)]
        hidh = [sb(f"hidh{i}", [P, KM * P], F16) for i in range(2)]
        hidl = [sb(f"hidl{i}", [P, KM * P], F16) for i in range(2)]
        weight = sb("weight", [P, 2])
        part = [sb(f"part{i}", [P, D]) for i in range(2)]
        wall = sb("wall", [P, 2, GE])
        get_at = sb("get_at", [P, 2], I32)
        kept_at = sb("kept_at", [P, 2], I32)
        put_at = [sb(f"put_at{i}", [P, 1], I32) for i in range(2)]
        ysum = [sb(f"ysum{i}", [P, NT, D]) for i in range(2)]
        hps = [[ctx.enter_context(nc.psum_tensor(f"hps{i}{j}", [P, 512], F32)) for j in range(2)] for i in range(2)]
        ops = [ctx.enter_context(nc.psum_tensor(f"ops{i}", [P, 512], F32)) for i in range(2)]
        xps = ctx.enter_context(nc.psum_tensor("xps", [P, 1024], F16))
        PARTS = ((0, 0, 4), (1, 4, 2))

        s_raw, s_bias = sem("raw_weights_in"), [sem("b1_rows_in0"), sem("b1_rows_in1")]
        s_w3, s_xtb, s_set = sem("bias_pads_zeroed"), sem("ones_rows_set"), sem("first_puts_set")
        s_wh, s_wl = sem("weights_high"), sem("weights_low")
        s_idx, s_get = sem("indices_copied"), sem("rows_gathered")
        s_c, s_used = sem("weights_taken"), sem("rows_used")
        s_pool_turn, s_pe_turn = sem("pool_turn"), sem("pe_turn")
        s_xf, s_xt = sem("x_transposed"), sem("xT_copied")
        s_l1, s_hh, s_h, s_hl = sem("hidden_full"), sem("hidden_high"), sem("hidden_ready"), sem("hidden_low")
        s_l2, s_ev, s_put = ([sem(f"{w}{i}") for i in range(2)] for w in ("out_full", "part_ready", "part_added"))
        s_y, s_fin, s_out = sem("sums_in"), sem("result_ready"), sem("result_stored")
        block = ctx.enter_context(nc.Block())
        W1 = io["W1"]
        W2 = io["W2"]

        def over_granules(eng, body, per_expert=lambda par, e, g: None):
            with eng.Fori(0, GE // 2) as e_pair:
                e0 = e_pair * 2
                for par in range(2):
                    first = eng.value_load(gran0[0:1, bass.ds(e0 + par, 1)], min_val=0, max_val=MAXG)
                    count = eng.value_load(n_gran[0:1, bass.ds(e0 + par, 1)], min_val=1, max_val=SLOTS // 2)
                    per_expert(par, e0 + par, first)
                    with eng.Fori(0, count) as j:
                        body(par, e0 + par, first + j, j)

        MAXG = N * KG * KE // GRAN + GE

        @block.sync
        def _(sp):
            def load(par, e, n):
                sp.dma_start(raw1[:, :], W1[bass.ds(e * D, P), :]).then_inc(s_raw, 16)
                for k in range(2):
                    sp.dma_start(raw1r[DR * k:DR * k + DR, :], W1[bass.ds(e * D + P, DR), :]).then_inc(s_raw, 16)
                sp.dma_start(raw2[:, :], W2[bass.ds(e, 1), :, :].rearrange("o p n -> (o p) n")).then_inc(s_raw, 16)

            def load_bias(par, e):
                for k in range(2):
                    sp.dma_start(w1lb[par][BROW[k]:BROW[k] + 1, :], d["b1s"][k, bass.ds(e, 1), :]).then_inc(s_bias[par], 16)

            load(0, 0, 0)
            sp.wait_ge(s_w3, 2)
            load_bias(0, 0)
            with sp.Fori(0, GE // 2) as e_pair:
                e0 = e_pair * 2
                for par in range(2):
                    after = (e0 + par + 1) % GE
                    sp.wait_ge(s_wl, e0 + par + 1)
                    load(1 - par, after, e0 + par + 1)
                    first = sp.value_load(gran0[0:1, bass.ds(e0 + par, 1)], min_val=0, max_val=MAXG)
                    sp.wait_ge(s_l2[1], first + 1)
                    load_bias(1 - par, after)
            total = sp.value_load(gran0[0:1, GE:GE + 1], min_val=GE, max_val=MAXG)
            for i in range(2):
                sp.wait_ge(s_put[i], total * 16 + 32 + 16 * i)
                sp.dma_start(ysum[i][:, :, :], d["y"][i][0:N, :].rearrange("(p t) d -> p t d", t=NT)).then_inc(s_y, 16)
            for par in range(2):
                sp.wait_ge(s_bias[par], GE * 16 + 32 * (1 - par))
            sp.wait_ge(s_fin, 1)
            sp.dma_start(io["out"].rearrange("(p t) d -> p t d", t=NT), ysum[0][:, :, :]).then_inc(s_out, 16)
            sp.wait_ge(s_out, 16)

        @block.gpsimd
        def _(pool):
            for at in (get_at, kept_at, *put_at):
                nc.gpsimd.iota(at[:, :], [[0, at.shape[1]]], base=N, channel_multiplier=1).then_inc(s_set, 1)
            pool.wait_ge(s_set, 6)

            def stand():
                pool.sem_inc(s_pool_turn, 1)

            def get():
                for i in range(2):
                    pool.indirect_dma_start(xrow[i][:, :], None, d["xrow"][:, :],
                                            bass.IndirectOffsetOnAxis(ap=get_at[:, i:i + 1], axis=0)).then_inc(s_get, 16)

            def put(i):
                pool.indirect_dma_start(d["y"][i][:, :], bass.IndirectOffsetOnAxis(ap=put_at[i][:, :], axis=0),
                                        part[i][:, :], None, compute_op=ALU.add).then_inc(s_put[i], 16)

            def turn(n, new_rows):
                pool.wait_ge(s_used, n + 1)
                pool.wait_ge(s_put[1], n * 16 + 16)
                stand()
                nc.gpsimd.tensor_copy(put_at[1][:, :], kept_at[:, 1:2]).then_inc(s_idx, 1)
                pool.wait_ge(s_idx, n * 4 + 1)
                stand()
                nc.gpsimd.tensor_copy(kept_at[:, :], get_at[:, :]).then_inc(s_idx, 1)
                pool.wait_ge(s_idx, n * 4 + 2)
                stand()
                if new_rows is not None:
                    nc.gpsimd.tensor_copy(get_at[:, :], new_rows).then_inc(s_idx, 1)
                    pool.wait_ge(s_idx, n * 4 + 3)
                    stand()
                get()
                pool.wait_ge(s_ev[1], n + 1)
                pool.wait_ge(s_put[0], n * 16 + 16)
                stand()
                put(1)
                nc.gpsimd.tensor_copy(put_at[0][:, :], kept_at[:, 0:1]).then_inc(s_idx, 1)
                pool.wait_ge(s_idx, n * 4 + (3 if new_rows is None else 4))
                pool.wait_ge(s_ev[0], n + 1)
                stand()
                put(0)

            for i in range(2):
                put(i)
            over_granules(pool, lambda par, e, g, j: turn(g, slots[:, bass.ds(e * SLOTS + j * 2, 2)]))
            total = pool.value_load(gran0[0:1, GE:GE + 1], min_val=GE, max_val=MAXG)
            turn(total, None)
            pool.wait_ge(s_put[1], total * 16 + 32)
            stand()
            nc.gpsimd.tensor_copy(put_at[1][:, :], kept_at[:, 1:2]).then_inc(s_idx, 1)
            pool.wait_ge(s_idx, total * 4 + 4)
            pool.wait_ge(s_ev[1], total + 2)
            stand()
            put(1)
            pool.wait_ge(s_pool_turn, total * 6 + 7)
            pool.wait_ge(s_pe_turn, GE)

        @block.tensor
        def _(pe):
            def transpose_x(n):
                pe.wait_ge(s_get, n * 32)
                for i in range(2):
                    for c in range(3):
                        tr = nc.tensor.transpose(xps[:, (3 * i + c) * P:(3 * i + c + 1) * P],
                                                 xrow[i][:, DR * c:DR * c + DR].bitcast(F16), ident16[:, :])
                tr.then_inc(s_xf, 1)

            def layer1(par, i):
                for bank_, c0, cn in PARTS:
                    for c in range(c0, c0 + cn):
                        o = hps[i][bank_][:, P * (c - c0):P * (c - c0) + P]
                        col = slice(P * c, P * c + P)
                        terms = ((w1h[par][:, col], xT[:, i, 0, :]), (w1h[par][:, col], xT[:, i, 1, :]),
                                 (w1l[par][:, col], xT[:, i, 0, :]), (w1hr[par][:, col], xT[:, i, 2, :]),
                                 (w1lb[par][0:KB, col], xTb[0:KB, i, :]))
                        for k, (w, x) in enumerate(terms):
                            mm = nc.tensor.matmul(o, w, x, start=(k == 0), stop=(k == len(terms) - 1))
                    mm.then_inc(s_l1, 1)

            def layer2(par, i, g):
                for n, (bank_, c0, cn) in enumerate(PARTS):
                    pe.wait_ge(s_hl, g * 4 + (2 * i + n + 1))
                    for c in range(c0, c0 + cn):
                        col, wcol = slice(P * c, P * c + P), slice(D * c, D * c + D)
                        for a, w in ((hidh, w2h), (hidh, w2l), (hidl, w2h)):
                            mm = nc.tensor.matmul(ops[i][:, 0:D], a[i][:, col], w[par][:, wcol],
                                                  start=(c == 0 and a is hidh and w is w2h),
                                                  stop=(c == KM - 1 and a is hidl))
                mm.then_inc(s_l2[i], 1)

            def start_expert(par, e, first):
                pe.wait_ge(s_wl, e + 1)
                pe.wait_ge(s_bias[par], (e - par) * 16 + 32)
                pe.sem_inc(s_pe_turn, 1)

            def body(par, e, g, j):
                pe.wait_ge(s_xt, g + 1)
                layer1(par, 0)
                layer1(par, 1)
                pe.wait_ge(s_ev[0], g + 1)
                layer2(par, 0, g)
                transpose_x(g + 2)
                pe.wait_ge(s_ev[1], g + 2)
                layer2(par, 1, g)

            for i in range(2):
                pe.sem_inc(s_l2[i], 1)
            pe.wait_ge(s_xtb, 2)
            transpose_x(1)
            over_granules(pe, body, start_expert)

        @block.scalar
        def _(act):
            def split_high(par, n, first):
                act.wait_ge(s_raw, n * 64)
                if first is not None:
                    act.wait_ge(s_l2[1], first + 1)
                nc.scalar.mul(w1h[par][:, :], raw1[:, :], WSCALE).then_inc(s_wh, 1)
                nc.scalar.mul(w1hr[par][:, :], raw1r[:, :], WSCALE).then_inc(s_wh, 1)
                nc.scalar.mul(w2h[par][:, :], raw2[:, :], WSCALE).then_inc(s_wh, 1)

            def body(par, e, g, j):
                for i in range(2):
                    act.wait_ge(s_l2[i], g + 1)
                    for n, (bank_, c0, cn) in enumerate(PARTS):
                        act.wait_ge(s_l1, g * 4 + (2 * i + n + 1))
                        cols = slice(P * c0, P * (c0 + cn))
                        nc.scalar.activation(hidh[i][:, cols], hps[i][bank_][:, 0:P * cn], ACT.Gelu, scale=1.0 / WSCALE)
                        nc.scalar.activation(hid[i][:, cols], hps[i][bank_][:, 0:P * cn], ACT.Gelu,
                                             scale=1.0 / WSCALE).then_inc(s_h, 1)

            split_high(0, 1, None)
            over_granules(act, body, lambda par, e, first: split_high(1 - par, e + 2, first))

        @block.vector
        def _(dve):
            def split_low(par, n):
                for k, (low, high, raw) in enumerate(((w1l[par][:, :], w1h[par][:, :], raw1[:, :]),
                                                      (w1lb[par][0:DR, :], w1hr[par][0:DR, :], raw1r[0:DR, :]),
                                                      (w2l[par][:, :], w2h[par][:, :], raw2[:, :]))):
                    dve.wait_ge(s_wh, (n - 1) * 3 + k + 1)
                    last = nc.vector.scalar_tensor_tensor(out=low, in0=raw, scalar=WSCALE, in1=high,
                                                          op0=ALU.mult, op1=ALU.subtract)
                last.then_inc(s_wl, 1)

            def copy_x(n):
                dve.wait_ge(s_xf, n)
                px = xps[:, 0:6 * P].rearrange("q (i c p) -> q i c p", i=2, c=3)
                nc.vector.tensor_copy(xT[:], px)
                nc.vector.tensor_copy(xTb[0:DR, :, :], px[0:DR, :, 2, :]).then_inc(s_xt, 1)
                for i in range(2):
                    last = nc.vector.tensor_copy(wall[:, i, :], xrow[i][:, D:XROW])
                last.then_inc(s_used, 1)

            def evacuate(i, g):
                dve.wait_ge(s_l2[i], g + 2)
                dve.wait_ge(s_put[i], g * 16 + 32 + 16 * i)
                nc.vector.tensor_scalar(part[i][:, :], ops[i][:, 0:D], weight[:, i:i + 1], 1.0 / WSCALE,
                                        ALU.mult, ALU.mult).then_inc(s_ev[i], 1)

            def body(par, e, g, j):
                dve.wait_ge(s_used, g + 2)
                dve.wait_ge(s_ev[1], g + 2)
                nc.vector.tensor_copy(weight[:, :].unsqueeze(2), wall[:, :, bass.ds(e, 1)]).then_inc(s_c, 1)
                for i in range(2):
                    for n, (bank_, c0, cn) in enumerate(PARTS):
                        dve.wait_ge(s_h, g * 4 + (2 * i + n + 1))
                        cols = slice(P * c0, P * (c0 + cn))
                        nc.vector.tensor_tensor(hidl[i][:, cols], hid[i][:, cols], hidh[i][:, cols],
                                                ALU.subtract).then_inc(s_hl, 1)
                dve.wait_ge(s_c, g + 1)
                evacuate(0, g)
                copy_x(g + 2)
                evacuate(1, g)

            for i in range(2):
                nc.vector.memset(part[i][:, :], 0.0).then_inc(s_set, 1)
            for i in range(2):
                nc.vector.memset(w1lb[i][DR:P, :], 0.0).then_inc(s_w3, 1)
            nc.vector.memset(xTb[DR:P, :, :], 0.0).then_inc(s_w3, 1)
            dve.wait_ge(s_w3, 3)
            for r in BROW:
                nc.vector.memset(xTb[r:r + 1, :, :], 1.0).then_inc(s_xtb, 1)
            dve.sem_inc(s_used, 1)
            for i in range(2):
                dve.sem_inc(s_ev[i], 1 + i)
            split_low(0, 1)
            copy_x(1)
            over_granules(dve, body, lambda par, e, first: split_low(1 - par, e + 2))
            dve.wait_ge(s_y, 32)
            nc.vector.tensor_tensor(ysum[1][:], ysum[1][:], h[:], ALU.add).then_inc(s_set, 1)
            dve.wait_ge(s_set, 7)
            nc.vector.tensor_tensor(ysum[0][:], ysum[0][:], ysum[1][:], ALU.add).then_inc(s_fin, 1)


def kernel(x, x_txt, L0_tok_proj_w, L0_tok_proj_b, L0_tok_pos_emb, L0_txt_weight, L0_attn_w_q, L0_attn_w_k,
           L0_attn_w_v, L0_attn_w_o, L0_attn_b_o, L0_ffn_Wg, L0_ffn_bg, L0_ffn_We, L0_ffn_be, L0_ffn_W1,
           L0_ffn_b1, L0_ffn_W2, L0_ffn_b2):
    import numpy as np
    import concourse.bacc as bacc
    from concourse.bass_utils import run_bass_kernel_spmd

    a = np.asarray
    side = 16
    edge = 96 // side
    patches = a(x).reshape(B, 3, edge, side, edge, side).transpose(3, 5, 1, 2, 4, 0).reshape(KF, P, S_IMG * B)
    token = np.arange(N).reshape(P, NT) - HALF_N
    arrays = {
        "xpT": patches.transpose(1, 0, 2),
        "pwT": a(L0_tok_proj_w).T.reshape(KF, P, D).transpose(1, 0, 2),
        "idsT": a(x_txt).astype(np.int32).T.reshape(TXT_TILES, P).T,
        "wqkv": np.concatenate([a(L0_attn_w_q), a(L0_attn_w_k), a(L0_attn_w_v)], axis=1),
        "L0_tok_proj_b": a(L0_tok_proj_b), "L0_tok_pos_emb": a(L0_tok_pos_emb), "L0_txt_weight": a(L0_txt_weight),
        "L0_attn_w_o": a(L0_attn_w_o), "L0_attn_b_o": a(L0_attn_b_o),
        "wr": np.concatenate([a(L0_ffn_Wg), a(L0_ffn_We).transpose(1, 0, 2).reshape(D, GE)], axis=1),
        "br": np.concatenate([a(L0_ffn_bg), a(L0_ffn_be).reshape(GE)]),
        "W1": a(L0_ffn_W1).reshape(GE * D, M), "b1": a(L0_ffn_b1).reshape(GE, M),
        "W2": a(L0_ffn_W2).reshape(GE, KM, P, D).transpose(0, 2, 1, 3).reshape(GE, P, KM * D),
        "b2": a(L0_ffn_b2).reshape(GE, D),
        "ident": np.eye(P, dtype=np.float32), "ident16": np.eye(P, dtype=np.float16),
        "ltri": np.triu(np.ones((P, P), np.float16), 1), "ones": np.ones((P, P), np.float16),
        "iota": np.tile(np.arange(P, dtype=np.float16)[None, :, None], (P, 1, NT)),
        "code": (token + (token >= 0)).astype(np.float32),
        "pad_row": (N - HALF_N + np.arange(P, dtype=np.float32)).reshape(P, 1),
        "earlier": (np.arange(GE)[None, :] < np.arange(GE + 1)[:, None]).astype(np.float32).reshape(1, -1),
    }
    nc = bacc.Bacc("TRN2", target_bir_lowering=False, num_devices=1)
    io, inputs = {}, {}
    for name, value in arrays.items():
        value = np.ascontiguousarray(value)
        inputs[f"in_{name}"] = value
        io[name] = nc.dram_tensor(f"in_{name}", value.shape, mybir.dt.from_np(value.dtype), kind="ExternalInput").ap()
    io["out"] = nc.dram_tensor("out", [N, D], F32, kind="ExternalOutput").ap()
    build(nc, io)
    r = run_bass_kernel_spmd(nc, [inputs], core_ids=[0])
    return r.results[0]["out"].reshape(B, S, D)
```

```python
import concourse.bass as bass
from concourse import mybir
from contextlib import ExitStack

F32, F16, I32 = mybir.dt.float32, mybir.dt.float16, mybir.dt.int32
ALU, ACT, AX = mybir.AluOpType, mybir.ActivationFunctionType, mybir.AxisListType

P = 128
B, S_IMG, S_TXT = 32, 36, 32
S = S_IMG + S_TXT
N = B * S
NT = N // P
D = 192
DR = D - P
FEAT = 768
KF = FEAT // P
VOCAB = 8000
H, DH = 12, 64
INNER = H * DH
HP = H // 2
G, E, KG, KE = 4, 8, 2, 4
GE = G * E
M = 768
KM = M // P
LN_EPS, GATE_EPS = 1e-5, 1e-6
NPAIR = B // 2
S2 = 2 * S
IMG_TILES, TXT_TILES = S_IMG * B // P, S_TXT * B // P
NPADDED = N + P
XROW = D + GE
SLOTS = 18
GRAN = 2 * P
HALF_N = N // 2
WSCALE = 256.0
SG = P // B


def build(nc, io):
    ctx = ExitStack()
    with ctx:
        def sb(name, shape, dt=F32):
            return ctx.enter_context(nc.sbuf_tensor(name, shape, dt))

        def dram(name, shape, dt=F32):
            return nc.dram_tensor(name, shape, dt).ap()

        d = dict(h0=dram("h0_d", [N, D]), attn=dram("attn_d", [N, D]),
                 xrow=dram("xrow_d", [NPADDED, XROW]), b1s=dram("b1s_d", [2, GE, M], F16),
                 y=[dram("ya_d", [NPADDED, D]), dram("yb_d", [NPADDED, D])])
        ident = sb("ident", [P, P])
        ident16 = sb("ident16", [P, P], F16)
        h = sb("h", [P, NT, D])
        slots = sb("slots", [P, GE * SLOTS], I32)
        n_gran = sb("n_gran", [1, GE], I32)
        gran0 = sb("gran0", [1, GE + 1], I32)
        tables = n_gran, gran0
        front(nc, io, ident, ident16, h, d)
        route(nc, io, ident, h, d, slots, tables)
        experts(nc, io, ident16, h, d, slots, tables)


def front(nc, io, ident, ident16, h0, d):
    h0_d, attn_d = d["h0"], d["attn"]
    ctx = ExitStack()
    with ctx:
        def sb(name, shape, dt=F32):
            return ctx.enter_context(nc.sbuf_tensor(name, shape, dt))

        def sem(name):
            return ctx.enter_context(nc.semaphore(name))

        bank = [ctx.enter_context(nc.psum_tensor(f"fbank{i}", [P, 512], F32)) for i in range(8)]
        tbank = [bank[2 + i][:, :].bitcast(F16) for i in range(2)]

        xp = sb("xp", [P, KF, S_IMG * B])
        pw = sb("pw", [P, KF, D])
        pos = sb("pos", [P, IMG_TILES, D])
        pbias = sb("pbias", [P, D])
        emb = sb("emb", [P, IMG_TILES, D])
        ids = sb("ids", [P, TXT_TILES], I32)
        idf = sb("idf", [P, TXT_TILES])
        idc = sb("idc", [P, TXT_TILES], I32)
        inside = sb("inside", [P, TXT_TILES])
        words = sb("words", [P, TXT_TILES, D])
        stats = sb("stats", [P, NT, 6])
        mv = sb("mv", [P, NT, 2])
        eps = sb("eps", [P, 1])
        rstd = sb("rstd", [P, NT])
        xn = sb("xn", [P, NT, D])
        x16 = sb("x16", [P, NT, 2 * D], F16)
        xnT = sb("xnT", [P, 3, N + S2], F16)
        bo = sb("bo", [P, D])
        wqkv = sb("wqkv", [P, 3 * INNER])
        wqkvr = sb("wqkvr", [P, 3 * INNER])
        wh, wl, whr, wlr = (sb(w, [P, 3 * INNER], F16) for w in ("wqkv_h", "wqkv_l", "wqkv_hr", "wqkv_lr"))
        wo = sb("wo", [P, HP, D])
        woh, wol = sb("wo_h", [P, HP, D], F16), sb("wo_l", [P, HP, D], F16)
        xq = sb("xq", [P, 3, S2], F16)
        xv = sb("xv", [P, 3, S2], F16)
        qk = sb("qk", [P, 2 * HP, S2])
        v = sb("v", [S, 2, INNER])
        mx = sb("mx", [S, 2, 2, HP])
        diff = sb("diff", [S, 2, 2, HP, S])
        ex = sb("ex", [S, 2, 2, HP, S])
        den = sb("den", [S, 2, 2, HP])
        rden = sb("rden", [S, 2, 2, HP])
        prob = sb("prob", [S, 2, 2, HP, S])
        probT = sb("probT", [S, 2, 2, HP, S])
        hTh, hTl = sb("hT_h", [P, 2, HP, S], F16), sb("hT_l", [P, 2, HP, S], F16)
        ao = sb("ao", [S, 2, D])

        s_id, s_pw, s_pos, s_idin = sem("ident_in"), sem("patch_weight_in"), sem("pos_in"), sem("ids_in")
        s_patch = [sem(f"patches{t}_in") for t in range(IMG_TILES)]
        s_w, s_wo = sem("qkv_weights_in"), sem("out_weights_in")
        s_posb = sem("pos_biased")
        s_idc = sem("ids_clamped")
        s_words = sem("words_gathered")
        s_wm = sem("words_masked")
        s_pe = sem("patch_products")
        s_emb = sem("patch_rows")
        s_h0out, s_h0in = sem("h0_stored"), [sem(f"h0_loaded{k}") for k in range(len(LN_TILES))]
        s_chain = sem("dve_step")
        s_var, s_std, s_xn = sem("variance_ready"), sem("std_ready"), sem("xn_ready")
        s_xh, s_x16 = sem("x_high"), sem("x_halves")
        s_wh, s_wl = sem("wqkv_high"), sem("wqkv_low")
        s_tp, s_tev = sem("xn_transposed"), sem("xnT_copied")
        s_pad = sem("pads_zeroed")
        s_xq, s_xv = sem("xq_ready"), sem("xv_ready")
        s_pf, s_pev = sem("projection_full"), sem("projection_copied")
        s_sf, s_df, s_ex, s_p = sem("scores_full"), sem("diff_ready"), sem("exp_ready"), sem("probs_ready")
        s_ptf, s_ptev = sem("probT_full"), sem("probT_copied")
        s_hf, s_hh, s_hev = sem("hT_full"), sem("hT_high"), sem("hT_halves")
        s_wf, s_wev, s_aout = sem("wo_full"), sem("wo_copied"), sem("attn_stored")
        s_ach = sem("softmax_step")
        s_turn = sem("pool_turn")

        block = ctx.enter_context(nc.Block())
        TG = [(t0, min(2, NT - t0)) for t0 in range(0, NT, 2)]
        LN_GROUPS = [[g for g, (t, _) in enumerate(TG) if t0 <= t < t1] for t0, t1 in LN_TILES]
        img_rows = h0_d.rearrange("(b s) d -> b s d", s=S)
        HEADS_COLS = HP * S

        @block.sync
        def _(sp):
            sp.dma_start(ids[:, :], io["idsT"][:, :]).then_inc(s_idin, 16)
            sp.dma_start(pw[:, :, :], io["pwT"][:, :, :]).then_inc(s_pw, 16)
            for t in range(IMG_TILES):
                sp.dma_start(xp[:, :, P * t:P * t + P], io["xpT"][:, :, P * t:P * t + P]).then_inc(s_patch[t], 16)
                if t == 1:
                    sp.dma_start(pbias[:, :], io["L0_tok_proj_b"].partition_broadcast(P)).then_inc(s_pos, 16)
                    for a in range(SG):
                        src = io["L0_tok_pos_emb"].rearrange("(t a) d -> a t d", a=SG)[a]
                        sp.dma_start(pos[B * a:B * a + B, :, :], src.partition_broadcast(B)).then_inc(s_pos, 16)
            sp.dma_start(ident[:, :], io["ident"][:, :]).then_inc(s_id, 16)
            sp.dma_start(ident16[:, :], io["ident16"][:, :]).then_inc(s_id, 16)
            sp.dma_start(wqkv[:, :], io["wqkv"][0:P, :]).then_inc(s_w, 16)
            for k in range(2):
                sp.dma_start(wqkvr[DR * k:DR * k + DR, :], io["wqkv"][P:D, :]).then_inc(s_w, 16)
            for first, last, rows, ready, count in ((0, S_IMG, emb, s_emb, IMG_TILES),
                                                    (S_IMG, S, words, s_wm, 1)):
                sp.wait_ge(ready, count)
                for a in range(SG):
                    sp.dma_start(img_rows[:, first + a:last:SG, :], rows[B * a:B * a + B, :, :]).then_inc(s_h0out, 16)
            sp.wait_ge(s_h0out, 16 * 2 * SG)
            for k, (t0, t1) in enumerate(LN_TILES):
                sp.dma_start(h0[:, t0:t1, :], h0_d.rearrange("(p t) d -> p t d", t=NT)[:, t0:t1, :]).then_inc(s_h0in[k], 16)
            sp.dma_start(wo[:, :, :], io["L0_attn_w_o"].rearrange("(c p) d -> p c d", p=P)).then_inc(s_wo, 16)
            sp.dma_start(bo[:, :], io["L0_attn_b_o"].partition_broadcast(P)).then_inc(s_wo, 16)
            sp.sem_inc(s_aout, 16)
            with sp.Fori(0, NPAIR) as i:
                for b in range(2):
                    sp.wait_ge(s_wev, 2 * i + b + 2)
                    sp.dma_start(attn_d[bass.ds(i * S2 + b * S, S), :], ao[:, b, :]).then_inc(s_aout, 16)
            sp.wait_ge(s_aout, 16 * B + 16)

        @block.gpsimd
        def _(pool):
            pool.wait_ge(s_idc, 1)
            for t in range(TXT_TILES):
                pool.indirect_dma_start(words[:, t, :], None, io["L0_txt_weight"][:, :],
                                        bass.IndirectOffsetOnAxis(ap=idc[:, t:t + 1], axis=0)).then_inc(s_words, 16)
            pool.wait_ge(s_tev, len(TG))
            pool.wait_ge(s_pad, 3)

            def columns(dst, k, done):
                nc.gpsimd.tensor_copy(dst[:, :, :], xnT[:, :, bass.ds(k * S2, S2)]).then_inc(done, 1)
            columns(xq, 0, s_xq)
            columns(xv, 0, s_xv)
            pool.wait_ge(s_pf, 4)
            columns(xq, 1, s_xq)
            with pool.Fori(0, NPAIR - 1) as i:
                pool.wait_ge(s_pf, 8 * i + 8)
                pool.sem_inc(s_turn, 1)
                columns(xv, i + 1, s_xv)
                pool.wait_ge(s_pf, 8 * i + 12)
                pool.sem_inc(s_turn, 1)
                columns(xq, i + 2, s_xq)
            pool.wait_ge(s_turn, 2 * (NPAIR - 1))

        @block.tensor
        def _(pe):
            pe.wait_ge(s_pw, 16)
            for t in range(IMG_TILES):
                pe.wait_ge(s_patch[t], 16)
                if t >= 2:
                    pe.wait_ge(s_emb, t - 1)
                for k in range(KF):
                    mm = nc.tensor.matmul(bank[t % 2][:, 0:D], xp[:, k, P * t:P * t + P], pw[:, k, :],
                                          start=(k == 0), stop=(k == KF - 1))
                mm.then_inc(s_pe, 1)
            pe.wait_ge(s_id, 32)
            for g, (t0, n) in enumerate(TG):
                pe.wait_ge(s_x16, g + 1)
                if g >= 2:
                    pe.wait_ge(s_tev, g - 1)
                for j in range(n):
                    for c in range(3):
                        o = P * (3 * j + c)
                        tr = nc.tensor.transpose(tbank[g % 2][:, o:o + P], x16[:, t0 + j, P * c:P * c + P],
                                                 ident16[:, :])
                tr.then_inc(s_tp, 1)
            pe.wait_ge(s_wl, 3)
            pe.wait_ge(s_pad, 3)

            TERMS = ((wh, 0), (wh, 1), (wl, 0), (whr, 2), (wlr, 2))

            def project_qk(k):
                pe.wait_ge(s_xq, k + 1)
                for f in range(4):
                    if not (isinstance(k, int) and 8 * k + f < 2):
                        pe.wait_ge(s_pev, 8 * k + f - 1)
                    for j in range(3):
                        c = 3 * f + j
                        for n, (w, x) in enumerate(TERMS):
                            mm = nc.tensor.matmul(bank[6 + f % 2][:, S2 * j:S2 * j + S2], w[:, P * c:P * c + P],
                                                  xq[:, x, :], start=(n == 0), stop=(n == len(TERMS) - 1))
                    mm.then_inc(s_pf, 1)

            def project_v(k):
                pe.wait_ge(s_xv, k + 1)
                for f in range(4):
                    b, half = divmod(f, 2)
                    pe.wait_ge(s_pev, 8 * k + 4 + f - 1)
                    lo, w_ = 2 * INNER + half * INNER // 2, INNER // 2
                    for n, (w, x) in enumerate(TERMS):
                        mm = nc.tensor.matmul(bank[6 + f % 2][0:S, 0:w_], xv[:, x, S * b:S * b + S], w[:, lo:lo + w_],
                                              start=(n == 0), stop=(n == len(TERMS) - 1))
                    mm.then_inc(s_pf, 1)

            def scores(k):
                pe.wait_ge(s_pev, 8 * k + 4)
                for b in range(2):
                    for hp in range(HP):
                        for odd in range(2):
                            mm = nc.tensor.matmul(bank[2 * b + odd][0:S, S * hp:S * hp + S],
                                                  qk[DH * odd:DH * odd + DH, hp, S * b:S * b + S],
                                                  qk[DH * odd:DH * odd + DH, HP + hp, S * b:S * b + S],
                                                  start=True, stop=True)
                    mm.then_inc(s_sf, 1)

            def transpose_probs(k):
                for b in range(2):
                    pe.wait_ge(s_p, 2 * k + b + 1)
                    for odd in range(2):
                        for hp in range(HP):
                            tr = nc.tensor.transpose(bank[2 * b + odd][0:S, S * hp:S * hp + S],
                                                     prob[:, b, odd, hp, :], ident[0:S, 0:S])
                    tr.then_inc(s_ptf, 1)

            def mix(k, b):
                if b == 0:
                    pe.wait_ge(s_pev, 8 * k + 8)
                pe.wait_ge(s_ptev, 2 * k + b + 1)
                pe.wait_ge(s_hev, 2 * k + b + 1)
                for hp in range(HP):
                    for odd in range(2):
                        h = 2 * hp + odd
                        mm = nc.tensor.matmul(bank[4][DH * odd:DH * odd + DH, S * hp:S * hp + S],
                                              v[:, b, DH * h:DH * h + DH], probT[:, b, odd, hp, :],
                                              start=True, stop=True)
                mm.then_inc(s_hf, 1)

            def output(k, b):
                pe.wait_ge(s_hev, 2 * k + b + 2)
                pe.wait_ge(s_wev, 2 * k + b + 1)
                for c in range(HP):
                    for n, (x, w) in enumerate(((hTh, woh), (hTh, wol), (hTl, woh))):
                        mm = nc.tensor.matmul(bank[5][0:S, 0:D], x[:, b, c, :], w[:, c, :],
                                              start=(c == 0 and n == 0), stop=(c == HP - 1 and n == 2))
                mm.then_inc(s_wf, 1)

            def attend(k, first=False):
                transpose_probs(k)
                for b in range(2):
                    if not first:
                        output(k - 1, b)
                    mix(k, b)

            def prepare(k):
                scores(k)
                project_v(k)
                project_qk(k + 1)

            project_qk(0)
            prepare(0)
            attend(0, first=True)
            prepare(1)
            with pe.Fori(1, NPAIR - 1) as i:
                attend(i)
                prepare(i + 1)
            attend(NPAIR - 1)
            for b in range(2):
                output(NPAIR - 1, b)

        @block.scalar
        def _(act):
            act.wait_ge(s_w, 48)
            for dst, src in ((wh, wqkv), (whr, wqkvr)):
                nc.scalar.mul(dst[:], src[:], WSCALE).then_inc(s_wh, 1)
            act.wait_ge(s_pad, 1)

            def copy_columns(g):
                t0, cnt = TG[g]
                act.wait_ge(s_tp, g + 1)
                out = xnT[:, :, 0:N].rearrange("q c (p t) -> q t c p", t=NT)[:, t0:t0 + cnt]
                src = tbank[g % 2][:, 0:3 * P * cnt].rearrange("q (t c p) -> q t c p", c=3, p=P)
                nc.scalar.copy(out, src).then_inc(s_tev, 1)

            for k in range(len(LN_TILES)):
                take_root(nc, act, k, mv, eps, rstd, s_var, s_std)
                for g in LN_GROUPS[k]:
                    t0, n = TG[g]
                    act.wait_ge(s_xn, t0 + n)
                    nc.scalar.copy(x16[:, t0:t0 + n, 0:P], xn[:, t0:t0 + n, 0:P])
                    nc.scalar.copy(x16[:, t0:t0 + n, 2 * P:2 * P + DR], xn[:, t0:t0 + n, P:D]).then_inc(s_xh, 1)
                for g in LN_GROUPS[k - 1] if k else ():
                    copy_columns(g)
            for g in LN_GROUPS[-1]:
                copy_columns(g)
            act.wait_ge(s_wo, 32)
            nc.scalar.mul(woh[:], wo[:], WSCALE).then_inc(s_wh, 1)

            def copy_qk(k):
                for f in range(4):
                    act.wait_ge(s_pf, 8 * k + f + 1)
                    nc.scalar.mul(qk[:, 3 * f:3 * f + 3, :], bank[6 + f % 2][:, 0:3 * S2], 1 / WSCALE).then_inc(s_pev, 1)

            def copy_v(k, f):
                b, half = divmod(f, 2)
                act.wait_ge(s_pf, 8 * k + 4 + f + 1)
                w = INNER // 2
                nc.scalar.mul(v[:, b, w * half:w * half + w], bank[6 + f % 2][0:S, 0:w], 1 / WSCALE).then_inc(s_pev, 1)

            def exponentials(k, b):
                act.wait_ge(s_df, 2 * k + b + 1)
                nc.scalar.activation(ex[:, b], diff[:, b], ACT.Exp, scale=float(DH) ** -0.5).then_inc(s_ex, 1)

            def copy_output(k, b):
                act.wait_ge(s_wf, 2 * k + b + 1)
                act.wait_ge(s_aout, 32 * k + 16)
                nc.scalar.mul(ao[:, b, :], bank[5][0:S, 0:D], 1 / WSCALE).then_inc(s_wev, 1)

            def attend(k, first=False):
                for b in range(2):
                    act.wait_ge(s_ptf, 2 * k + b + 1)
                    for odd in range(2):
                        cp = nc.scalar.copy(probT[:, b, odd], bank[2 * b + odd][0:S, 0:HEADS_COLS])
                    cp.then_inc(s_ptev, 1)
                for b in range(2):
                    if not first:
                        copy_output(k - 1, b)
                    act.wait_ge(s_hf, 2 * k + b + 1)
                    nc.scalar.copy(hTh[:, b], bank[4][:, 0:HEADS_COLS]).then_inc(s_hh, 1)

            def prepare(k):
                for b in range(2):
                    copy_v(k, 2 * b)
                    copy_v(k, 2 * b + 1)
                    exponentials(k, b)
                copy_qk(k + 1)

            act.sem_inc(s_wev, 1)
            copy_qk(0)
            prepare(0)
            attend(0, first=True)
            prepare(1)
            with act.Fori(1, NPAIR - 1) as i:
                attend(i)
                prepare(i + 1)
            attend(NPAIR - 1)
            for b in range(2):
                copy_output(NPAIR - 1, b)

        @block.vector
        def _(dve):
            n = [0]

            def link(ins):
                n[0] += 1
                ins.then_inc(s_chain, 1)
                dve.wait_ge(s_chain, n[0])

            nc.vector.memset(eps[:, :], LN_EPS).then_inc(s_pad, 1)
            nc.vector.memset(xnT[:, :, N:N + S2], 0.0).then_inc(s_pad, 1)
            nc.vector.memset(wlr[DR:P, :], 0.0).then_inc(s_pad, 1)
            dve.wait_ge(s_idin, 16)
            link(nc.vector.tensor_copy(idf[:, :], ids[:, :]))
            nc.vector.tensor_scalar(idc[:, :], idf[:, :], 0.0, float(VOCAB - 1), ALU.max, ALU.min).then_inc(s_idc, 1)
            link(nc.vector.tensor_scalar(inside[:, :], idf[:, :], 0.0, None, ALU.is_ge))
            link(nc.vector.scalar_tensor_tensor(out=inside[:, :], in0=idf[:, :], scalar=float(VOCAB - 1),
                                                in1=inside[:, :], op0=ALU.is_le, op1=ALU.mult))
            dve.wait_ge(s_pos, 16 * (1 + SG))
            link(nc.vector.tensor_tensor(pos[:, :, :], pos[:, :, :],
                                         pbias[:, :].unsqueeze(1).broadcast_to([P, IMG_TILES, D]), ALU.add))
            for t in range(IMG_TILES):
                dve.wait_ge(s_pe, t + 1)
                nc.vector.tensor_tensor(emb[:, t, :], bank[t % 2][:, 0:D], pos[:, t, :], ALU.add).then_inc(s_emb, 1)
            dve.wait_ge(s_words, 16 * TXT_TILES)
            nc.vector.tensor_tensor(words[:, :, :], words[:, :, :],
                                    inside[:, :].unsqueeze(2).broadcast_to([P, TXT_TILES, D]), ALU.mult).then_inc(s_wm, 1)
            for n_, (low, high, raw, rows) in enumerate(((wl, wh, wqkv, P), (wlr, whr, wqkvr, DR))):
                dve.wait_ge(s_wh, n_ + 1)
                nc.vector.scalar_tensor_tensor(out=low[0:rows], in0=raw[0:rows], scalar=WSCALE,
                                               in1=high[0:rows], op0=ALU.mult, op1=ALU.subtract).then_inc(s_wl, 1)
            def low_halves(k):
                for g in LN_GROUPS[k]:
                    t0, cnt = TG[g]
                    dve.wait_ge(s_xh, g + 1)
                    ts = slice(t0, t0 + cnt)
                    nc.vector.tensor_tensor(x16[:, ts, P:2 * P], xn[:, ts, 0:P], x16[:, ts, 0:P], ALU.subtract)
                    nc.vector.tensor_tensor(x16[:, ts, 2 * P + DR:2 * D], xn[:, ts, P:D], x16[:, ts, 2 * P:2 * P + DR],
                                            ALU.subtract).then_inc(s_x16, 1)

            layer_norm(nc, dve, link, lambda k: dve.wait_ge(s_h0in[k], 16), low_halves, h0, stats, mv, rstd, xn,
                       s_var, s_std, s_xn)
            dve.wait_ge(s_wh, 3)
            nc.vector.scalar_tensor_tensor(out=wol[:], in0=wo[:], scalar=WSCALE, in1=woh[:], op0=ALU.mult,
                                           op1=ALU.subtract).then_inc(s_wl, 1)
            nc.vector.tensor_tensor(h0[:], h0[:], bo[:, :].unsqueeze(1).broadcast_to([P, NT, D]), ALU.add)

            def softmax(k):
                for b in range(2):
                    dve.wait_ge(s_sf, 2 * k + b + 1)
                    for odd in range(2):
                        sc = bank[2 * b + odd][0:S, 0:HEADS_COLS].rearrange("q (h k) -> q h k", k=S)
                        mxs = nc.vector.tensor_reduce(mx[:, b, odd, :], sc, AX.X, ALU.max)
                    mxs.then_inc(s_ach, 1)
                    dve.wait_ge(s_ach, 6 * k + b + 1)
                    for odd in range(2):
                        sc = bank[2 * b + odd][0:S, 0:HEADS_COLS].rearrange("q (h k) -> q h k", k=S)
                        sub = nc.vector.tensor_tensor(diff[:, b, odd], sc,
                                                      mx[:, b, odd, :].unsqueeze(2).broadcast_to([S, HP, S]),
                                                      ALU.subtract)
                    sub.then_inc(s_df, 1)
                for b in range(2):
                    dve.wait_ge(s_ex, 2 * k + b + 1)
                    nc.vector.tensor_reduce(den[:, b], ex[:, b], AX.X, ALU.add).then_inc(s_ach, 1)
                    dve.wait_ge(s_ach, 6 * k + 2 * b + 3)
                    nc.vector.reciprocal(rden[:, b], den[:, b]).then_inc(s_ach, 1)
                    dve.wait_ge(s_ach, 6 * k + 2 * b + 4)
                    nc.vector.tensor_tensor(prob[:, b], ex[:, b],
                                            rden[:, b].unsqueeze(3).broadcast_to([S, 2, HP, S]),
                                            ALU.mult).then_inc(s_p, 1)

            def low_heads(k):
                for b in range(2):
                    dve.wait_ge(s_hh, 2 * k + b + 1)
                    nc.vector.tensor_tensor(hTl[:, b], bank[4][:, 0:HEADS_COLS].rearrange("q (h k) -> q h k", k=S),
                                            hTh[:, b], ALU.subtract).then_inc(s_hev, 1)

            dve.sem_inc(s_hev, 1)
            softmax(0)
            with dve.Fori(0, NPAIR - 1) as i:
                low_heads(i)
                softmax(i + 1)
            low_heads(NPAIR - 1)


LN_TILES = ((0, 4), (4, 8), (8, 12), (12, NT))


def layer_norm(nc, dve, link, arrive, after, h, stats, mv, rstd, xn, s_var, s_std, s_xn):
    for k, (t0, t1) in enumerate(LN_TILES):
        arrive(k)
        for t in range(t0, t1):
            last = nc.vector.bn_stats(stats[:, t, :], h[:, t, :])
        link(last)
        for t in range(t0, t1):
            last = nc.vector.bn_aggr(mv[:, t, :], stats[:, t, :])
        last.then_inc(s_var, 1)
        if k > 0:
            after(k - 1)
        dve.wait_ge(s_std, k + 1)
        link(nc.vector.reciprocal(rstd[:, t0:t1], rstd[:, t0:t1]))
        for t in range(t0, t1):
            nc.vector.tensor_scalar(xn[:, t, :], h[:, t, :], mv[:, t, 0:1], rstd[:, t:t + 1],
                                    ALU.subtract, ALU.mult).then_inc(s_xn, 1)
    after(len(LN_TILES) - 1)


def take_root(nc, act, k, mv, eps, rstd, s_var, s_std):
    t0, t1 = LN_TILES[k]
    act.wait_ge(s_var, k + 1)
    nc.scalar.activation(rstd[:, t0:t1], mv[:, t0:t1, 1], ACT.Sqrt, bias=eps[:, 0:1], scale=1.0).then_inc(s_std, 1)


def route(nc, io, ident, h, d, slots, tables):
    n_gran, gran0 = tables
    ctx = ExitStack()
    with ctx:
        def sb(name, shape, dt=F32):
            return ctx.enter_context(nc.sbuf_tensor(name, shape, dt))

        def sem(name):
            return ctx.enter_context(nc.semaphore(name))

        bank = [ctx.enter_context(nc.psum_tensor(f"rbank{i}", [P, 512], F32)) for i in range(8)]
        NR = G + GE
        TE = NT * GE
        at = sb("at", [P, NT, D])
        wr = sb("wr", [P, NR])
        wrr = sb("wrr", [DR, NR])
        br = sb("br", [P, NR])
        b2 = sb("b2", [GE, D])
        b1 = sb("b1", [GE, M])
        b1h = sb("b1h", [GE, M], F16)
        b1l = sb("b1l", [GE, M], F16)
        stats = sb("stats2", [P, NT, 6])
        mv = sb("mv2", [P, NT, 2])
        eps = sb("eps2", [P, 1])
        rstd = sb("rstd2", [P, NT])
        xn = sb("xn2", [P, NT, D])
        xrow = sb("xrow", [P, NT, XROW])
        x16 = xrow[:, :, 0:D].bitcast(F16)
        xT = sb("x2T", [P, NT, P])
        xTr = sb("x2Tr", [DR, NT, P])
        zeros = sb("zeros", [P, NPADDED // P * D])
        gl = sb("gl", [P, NT, 1, G])
        el = sb("el", [P, NT, G, E])
        cmp_g = sb("cmp_g", [P, NT, 1, G, G], F16)
        cmp_e = sb("cmp_e", [P, NT, G, E, E], F16)
        rank_g, rank_e = sb("rank_g", [P, NT, 1, G]), sb("rank_e", [P, NT, G, E])
        top_g, top_e = sb("top_g", [P, NT, 1]), sb("top_e", [P, NT, G])
        exp_g, exp_e = sb("exp_g", [P, NT, 1, G]), sb("exp_e", [P, NT, G, E])
        sum_g, sum_e = sb("sum_g", [P, NT, 1]), sb("sum_e", [P, NT, G])
        mask = sb("mask", [P, NT, G, E], F16)
        comb = sb("comb", [P, NT, G, E])
        before = sb("before", [P, NT + 1, GE], F16)
        ltri = sb("ltri", [P, P], F16)
        ones = sb("ones", [P, P], F16)
        pos_f = sb("pos_f", [P, GE, NT])
        pos_i = sb("pos_i", [P, GE, NT], I32)
        place_i = sb("place_i", [P, GE, NT], I32)
        place = sb("place", [P, GE, NT])
        tile_of = sb("tile_of", [P, GE, NT])
        code = sb("code", [P, NT])
        code_b = sb("code_b", [P, GE, NT])
        mask_f = sb("mask_f", [P, GE, NT])
        rhs = sb("rhs", [P, GE, NT, SLOTS], F16)
        iota = sb("iota", [P, P, NT], F16)
        one_hot = sb("one_hot", [P, 2, P, NT], F16)
        place_e = sb("place_e", [P, 2, NT], F16)
        rhs_e = sb("rhs_e", [P, 2, NT, SLOTS], F16)
        codes = sb("codes", [P, GE * SLOTS])
        pos_code = sb("pos_code", [P, GE * SLOTS])
        pad_row = sb("pad_row", [P, 1])
        empty = sb("empty", [P, GE * SLOTS])
        tot = sb("tot", [1, GE])
        tot_i = sb("tot_i", [1, GE], I32)
        n_f = sb("n_f", [1, GE])
        earlier = sb("earlier", [1, (GE + 1) * GE])
        prod = sb("prod", [1, (GE + 1) * GE])
        g0_f = sb("g0_f", [1, GE + 1])
        combT = sb("combT", [GE, NT, P])
        hb = sb("hb", [P, NT, D])

        s_in, s_b1in = sem("router_in"), sem("b1_in")
        s_att = [sem(f"attn{k}_in") for k in range(len(LN_TILES))]
        s_chain, s_z, s_zout = sem("route_step"), sem("zeros_ready"), sem("zeros_stored")
        s_var, s_std, s_xn = sem("variance2"), sem("std2"), sem("xn2_ready")
        s_hi, s_b1, s_b1out = sem("x_high"), sem("b1_halves"), sem("b1_stored")
        s_tp, s_tev = sem("xn2_transposed"), sem("x2T_copied")
        s_lg, s_dif, s_exp = sem("logits_full"), sem("logits_shifted"), sem("gates_exp")
        s_row, s_rowout = sem("rows_ready"), sem("rows_stored")
        s_bef, s_pos = sem("prefix_ready"), sem("positions_full")
        s_rhs, s_stage = sem("lists_ready"), sem("expert_staged")
        s_oh, s_lf, s_lev = sem("one_hots_ready"), sem("list_full"), sem("list_copied")
        s_ct, s_ctev, s_b2f, s_b2ev = sem("combT_full"), sem("combT_copied"), sem("b2_full"), sem("b2_added")
        s_comb, s_mf = sem("weights_ready"), sem("mask_and_code_spread")
        s_hb, s_cz, s_rz = sem("b2_weighed"), sem("cmp_zeroed"), sem("rhs_zeroed")
        block = ctx.enter_context(nc.Block())
        TG = [(t0, min(4, NT - t0)) for t0 in range(0, NT, 4)]
        LG = [(0, 9), (9, NT - 9)]

        @block.sync
        def _(sp):
            for k, (t0, t1) in enumerate(LN_TILES):
                sp.dma_start(at[:, t0:t1, :], d["attn"].rearrange("(p t) d -> p t d", t=NT)[:, t0:t1, :]).then_inc(s_att[k], 16)
            sp.dma_start(b1[:, :], io["b1"][:, :]).then_inc(s_b1in, 16)
            for dst, src in ((wr, io["wr"][0:P, :]), (wrr, io["wr"][P:D, :]), (br, io["br"].partition_broadcast(P)),
                             (b2, io["b2"][:, :]), (ltri, io["ltri"][:, :]), (ones, io["ones"][:, :]),
                             (iota, io["iota"]), (code, io["code"][:, :]), (pad_row, io["pad_row"][:, :]),
                             (earlier, io["earlier"][:, :])):
                sp.dma_start(dst[:], src).then_inc(s_in, 16)
            sp.wait_ge(s_z, 1)
            sp.dma_start(d["y"][1].rearrange("(p t) d -> p (t d)", p=P), zeros[:, :]).then_inc(s_zout, 16)
            sp.dma_start(d["y"][0][N:NPADDED, :], zeros[:, 0:D]).then_inc(s_zout, 16)
            sp.dma_start(d["xrow"][N:NPADDED, :], zeros[:, 0:XROW]).then_inc(s_zout, 16)
            sp.wait_ge(s_b1, 1)
            sp.dma_start(d["b1s"][0], b1h[:, :]).then_inc(s_b1out, 16)
            sp.dma_start(d["b1s"][1], b1l[:, :]).then_inc(s_b1out, 16)
            sp.wait_ge(s_row, 1)
            sp.dma_start(d["xrow"][0:N, :].rearrange("(p t) d -> p t d", t=NT), xrow[:, :, :]).then_inc(s_rowout, 16)
            sp.wait_ge(s_b2ev, 1)
            sp.dma_start(d["y"][0][0:N, :].rearrange("(p t) d -> p t d", t=NT), h[:, :, :]).then_inc(s_zout, 16)
            sp.wait_ge(s_zout, 64)
            sp.wait_ge(s_b1out, 32)
            sp.wait_ge(s_rowout, 16)

        @block.gpsimd
        def _(pool):
            nc.gpsimd.memset(zeros[:, :], 0.0).then_inc(s_z, 1)
            pool.wait_ge(s_z, 1)
            for n, cmp in enumerate((cmp_g, cmp_e)):
                nc.gpsimd.memset(cmp[:], 0.0).then_inc(s_cz, 1)
                pool.wait_ge(s_cz, n + 1)
            nc.gpsimd.memset(rhs[:, :, :, NT:SLOTS], 0.0).then_inc(s_rz, 1)
            pool.wait_ge(s_rz, 1)
            pool.wait_ge(s_hb, NT)
            nc.gpsimd.tensor_tensor(h[:], h[:], hb[:], ALU.add).then_inc(s_b2ev, 1)
            pool.wait_ge(s_b2ev, 1)

        @block.scalar
        def _(act):

            def copy_columns(g):
                t0, cnt = TG[g]
                for part, (rows, dst) in enumerate(((P, xT), (DR, xTr))):
                    act.wait_ge(s_tp, 2 * g + part + 1)
                    nc.scalar.copy(dst[0:rows, t0:t0 + cnt, :],
                                   bank[part][0:rows, 0:P * cnt].rearrange("q (t p) -> q t p", p=P)).then_inc(s_tev, 1)

            for k in range(len(LN_TILES)):
                take_root(nc, act, k, mv, eps, rstd, s_var, s_std)
                if k > 0:
                    copy_columns(k - 1)
            act.wait_ge(s_xn, NT)
            nc.scalar.copy(x16[:, :, 0:P], xn[:, :, 0:P])
            nc.scalar.copy(x16[:, :, 2 * P:2 * P + DR], xn[:, :, P:D]).then_inc(s_hi, 1)
            for g in range(len(LN_TILES) - 1, len(TG)):
                copy_columns(g)
            for n, (x, ex) in enumerate(((gl, exp_g), (el, exp_e))):
                act.wait_ge(s_dif, n + 1)
                nc.scalar.activation(ex[:], x[:], ACT.Exp).then_inc(s_exp, 1)
            act.wait_ge(s_in, 160)
            nc.scalar.copy(code_b[:], code[:, :].unsqueeze(1).broadcast_to([P, GE, NT])).then_inc(s_mf, 1)
            act.wait_ge(s_comb, 1)
            nc.scalar.copy(mask_f[:], mask[:].rearrange("p t g e -> p (g e) t")).then_inc(s_mf, 1)
            nc.scalar.copy(xrow[:, :, D:XROW], comb[:].rearrange("p t g e -> p t (g e)")).then_inc(s_row, 1)
            for g, (t0, cnt) in enumerate(TG):
                act.wait_ge(s_ct, g + 1)
                nc.scalar.copy(combT[:, t0:t0 + cnt, :],
                               bank[7][0:GE, 0:P * cnt].rearrange("q (t p) -> q t p", p=P)).then_inc(s_ctev, 1)

            def stage(e, par):
                nc.scalar.copy(place_e[:, par, :], place[:, bass.ds(e, 1), :]).then_inc(s_stage, 1)
                nc.scalar.copy(rhs_e[:, par], rhs[:, bass.ds(e, 1)]).then_inc(s_stage, 1)

            for t in range(NT):
                act.wait_ge(s_b2f, t + 1)
                nc.scalar.copy(hb[:, t, :], bank[t % 2][:, 0:D]).then_inc(s_hb, 1)
                if t == 4:
                    act.wait_ge(s_rhs, 1)
                    for par in range(2):
                        stage(par, par)
            with act.Fori(0, GE // 2 - 1) as e_pair:
                for par in range(2):
                    act.wait_ge(s_lf, e_pair * 2 + (par + 1))
                    stage(e_pair * 2 + (par + 2), par)

        @block.tensor
        def _(pe):
            def logits(g):
                pe.wait_ge(s_tev, 2 * g + 2)
                for t in range(TG[g][0], sum(TG[g])):
                    k = int(t >= LG[1][0])
                    o = NR * (t - LG[k][0])
                    nc.tensor.matmul(bank[2 + k][:, o:o + NR], xT[:, t, :], wr[:, :], start=True, stop=False)
                    mm = nc.tensor.matmul(bank[2 + k][:, o:o + NR], xTr[:, t, :], wrr[:, :], start=False, stop=True)
                    if t + 1 == sum(LG[k]):
                        mm.then_inc(s_lg, 1)

            for g, (t0, n) in enumerate(TG):
                pe.wait_ge(s_xn, t0 + n)
                for part, (rows, lo) in enumerate(((P, 0), (DR, P))):
                    if g >= 1:
                        pe.wait_ge(s_tev, 2 * g - 1 + part)
                    for j in range(n):
                        tr = nc.tensor.transpose(bank[part][0:rows, P * j:P * j + P],
                                                 xn[:, t0 + j, lo:lo + rows], ident[:, :])
                    tr.then_inc(s_tp, 1)
                if g == 0:
                    pe.wait_ge(s_in, 160)
                else:
                    logits(g - 1)
            logits(len(TG) - 1)
            pe.wait_ge(s_bef, 1)
            for k, (t0, n) in enumerate(LG):
                for t in range(t0, t0 + n):
                    o = GE * (t - t0)
                    nc.tensor.matmul(bank[4 + k][:, o:o + GE], ltri[:, :], mask[:, t].rearrange("p g e -> p (g e)"),
                                     start=True, stop=False)
                    nc.tensor.matmul(bank[4 + k][:, o:o + GE], ones[:, :], before[:, t, :], start=False, stop=True)
            nc.tensor.matmul(bank[6][:, 0:GE], ones[:, :], before[:, NT, :], start=True, stop=True).then_inc(s_pos, 1)
            pe.wait_ge(s_comb, 1)
            for g, (t0, n) in enumerate(TG):
                if g >= 1:
                    pe.wait_ge(s_ctev, g)
                for j in range(n):
                    tr = nc.tensor.transpose(bank[7][0:GE, P * j:P * j + P],
                                             comb[:, t0 + j].rearrange("p g e -> p (g e)"), ident[:, :])
                tr.then_inc(s_ct, 1)
            pe.wait_ge(s_ctev, len(TG))
            for t in range(NT):
                if t >= 2:
                    pe.wait_ge(s_hb, t - 1)
                nc.tensor.matmul(bank[t % 2][:, 0:D], combT[:, t, :], b2[:, :], start=True, stop=True).then_inc(s_b2f, 1)
            with pe.Fori(0, GE // 2) as e_pair:
                e = e_pair * 2
                for par in range(2):
                    pe.wait_ge(s_oh, e + par + 1)
                    for t in range(NT):
                        mm = nc.tensor.matmul(bank[2 + par][:, 0:SLOTS], one_hot[:, par, :, t], rhs_e[:, par, t, :],
                                              start=(t == 0), stop=(t == NT - 1))
                    mm.then_inc(s_lf, 1)

        @block.vector
        def _(dve):
            n = [0]

            def link(ins):
                n[0] += 1
                ins.then_inc(s_chain, 1)
                dve.wait_ge(s_chain, n[0])

            nc.vector.memset(eps[:, :], LN_EPS)
            def add_attention(k):
                t0, t1 = LN_TILES[k]
                dve.wait_ge(s_att[k], 16)
                link(nc.vector.tensor_tensor(h[:, t0:t1], h[:, t0:t1], at[:, t0:t1], ALU.add))

            layer_norm(nc, dve, link, add_attention, lambda k: None, h, stats, mv, rstd, xn, s_var, s_std, s_xn)

            def low_halves(t0, t1):
                dve.wait_ge(s_hi, 1)
                nc.vector.tensor_tensor(x16[:, t0:t1, P:2 * P], xn[:, t0:t1, 0:P], x16[:, t0:t1, 0:P], ALU.subtract)
                nc.vector.tensor_tensor(x16[:, t0:t1, 2 * P + DR:2 * D], xn[:, t0:t1, P:D],
                                        x16[:, t0:t1, 2 * P:2 * P + DR], ALU.subtract)

            low_halves(0, NT)
            dve.wait_ge(s_b1in, 16)
            link(nc.vector.tensor_scalar(b1h[:, :], b1[:, :], WSCALE, None, ALU.mult))
            nc.vector.scalar_tensor_tensor(out=b1l[:, :], in0=b1[:, :], scalar=WSCALE, in1=b1h[:, :],
                                           op0=ALU.mult, op1=ALU.subtract).then_inc(s_b1, 1)
            dve.wait_ge(s_in, 160)
            for k, (t0, cnt) in enumerate(LG):
                dve.wait_ge(s_lg, k + 1)
                lg = bank[2 + k][:, 0:NR * cnt].rearrange("p (t r) -> p t r", r=NR)
                nc.vector.tensor_tensor(gl[:, t0:t0 + cnt, 0, :], lg[:, :, 0:G],
                                        br[:, 0:G].unsqueeze(1).broadcast_to([P, cnt, G]), ALU.add)
                last = nc.vector.tensor_tensor(el[:, t0:t0 + cnt].rearrange("p t g e -> p t (g e)"), lg[:, :, G:NR],
                                               br[:, G:NR].unsqueeze(1).broadcast_to([P, cnt, GE]), ALU.add)
            link(last)

            def shift_and_rank(x, cmp, rank, top, width):
                link(nc.vector.tensor_reduce(top[:], x[:], AX.X, ALU.max))
                shape = list(x.shape)
                for j in range(width):
                    for lo, hi, op in ((0, j, ALU.is_gt), (j + 1, width, ALU.is_ge)):
                        if lo < hi:
                            last = nc.vector.tensor_tensor(
                                cmp[:, :, :, lo:hi, j], x[:, :, :, j:j + 1].broadcast_to(shape[:3] + [hi - lo]),
                                x[:, :, :, lo:hi], op)
                link(last)
                half = width // 2
                while half > 1:
                    link(nc.vector.tensor_tensor(cmp[:, :, :, :, 0:half], cmp[:, :, :, :, 0:half],
                                                 cmp[:, :, :, :, half:2 * half], ALU.add))
                    half //= 2
                link(nc.vector.tensor_tensor(rank[:], cmp[:, :, :, :, 0], cmp[:, :, :, :, 1], ALU.add))
                nc.vector.tensor_tensor(x[:], x[:], top[:].unsqueeze(3).broadcast_to(shape), ALU.subtract).then_inc(s_dif, 1)

            def gates(ex, rank, total, k):
                shape = list(ex.shape)
                link(nc.vector.tensor_scalar(rank[:], rank[:], float(k), None, ALU.is_lt))
                link(nc.vector.tensor_tensor(ex[:], ex[:], rank[:], ALU.mult))
                link(nc.vector.tensor_reduce(total[:], ex[:], AX.X, ALU.add))
                link(nc.vector.reciprocal(total[:], total[:]))
                link(nc.vector.tensor_tensor(ex[:], ex[:], total[:].unsqueeze(3).broadcast_to(shape), ALU.mult))
                link(nc.vector.scalar_tensor_tensor(out=ex[:], in0=ex[:], scalar=GATE_EPS, in1=ex[:],
                                                    op0=ALU.is_ge, op1=ALU.mult))

            dve.wait_ge(s_cz, 2)
            shift_and_rank(gl, cmp_g, rank_g, top_g, G)
            shift_and_rank(el, cmp_e, rank_e, top_e, E)
            dve.wait_ge(s_exp, 1)
            gates(exp_g, rank_g, sum_g, KG)
            dve.wait_ge(s_exp, 2)
            gates(exp_e, rank_e, sum_e, KE)
            by_group = [P, NT, G, E]
            link(nc.vector.tensor_tensor(mask[:], rank_e[:], rank_g[:, :, 0, :].unsqueeze(3).broadcast_to(by_group), ALU.mult))
            nc.vector.tensor_tensor(comb[:], exp_e[:], exp_g[:, :, 0, :].unsqueeze(3).broadcast_to(by_group),
                                    ALU.mult).then_inc(s_comb, 1)
            link(nc.vector.memset(before[:, 0, :], 0.0))
            for t in range(NT):
                last = nc.vector.tensor_tensor(before[:, t + 1, :], before[:, t, :],
                                               mask[:, t].rearrange("p g e -> p (g e)"), ALU.add)
                if t < NT - 1:
                    link(last)
            last.then_inc(s_bef, 1)
            dve.wait_ge(s_mf, 2)
            dve.wait_ge(s_rz, 1)
            dve.wait_ge(s_pos, 1)
            for k, (t0, cnt) in enumerate(LG):
                last = nc.vector.tensor_copy(pos_i[:, :, t0:t0 + cnt],
                                             bank[4 + k][:, 0:GE * cnt].rearrange("p (t e) -> p e t", e=GE))
            link(last)
            nc.vector.tensor_scalar(place_i[:], pos_i[:], P - 1, None, ALU.bitwise_and)
            link(nc.vector.tensor_scalar(pos_i[:], pos_i[:], P.bit_length() - 1, None, ALU.arith_shift_right))
            link(nc.vector.tensor_copy(tile_of[:], pos_i[:]))
            link(nc.vector.scalar_tensor_tensor(out=place[:], in0=place_i[:], scalar=1.0, in1=mask_f[:],
                                                op0=ALU.add, op1=ALU.mult))
            link(nc.vector.tensor_scalar(place[:], place[:], -1.0, None, ALU.add))
            for a in range(NT):
                last = nc.vector.scalar_tensor_tensor(out=rhs[:, :, :, a], in0=tile_of[:], scalar=float(a),
                                                      in1=code_b[:], op0=ALU.is_equal, op1=ALU.mult)
            last.then_inc(s_rhs, 1)
            link(nc.vector.tensor_scalar(tot[:, :], bank[6][0:1, 0:GE], float(GRAN - 1), None, ALU.add))
            link(nc.vector.tensor_copy(tot_i[:, :], tot[:, :]))
            link(nc.vector.tensor_scalar(tot_i[:, :], tot_i[:, :], GRAN.bit_length() - 1, None, ALU.arith_shift_right))
            link(nc.vector.tensor_scalar(n_f[:, :], tot_i[:, :], 1.0, None, ALU.max))
            link(nc.vector.tensor_copy(n_gran[:, :], n_f[:, :]))
            e2 = [1, GE + 1, GE]
            link(nc.vector.tensor_tensor(prod[:, :].rearrange("o (a b) -> o a b", b=GE),
                                         earlier[:, :].rearrange("o (a b) -> o a b", b=GE),
                                         n_f[:, :].unsqueeze(1).broadcast_to(e2), ALU.mult))
            link(nc.vector.tensor_reduce(g0_f[:, :], prod[:, :].rearrange("o (a b) -> o a b", b=GE), AX.X, ALU.add))
            link(nc.vector.tensor_copy(gran0[:, :], g0_f[:, :]))
            def one_hots(e, par):
                dve.wait_ge(s_stage, 2 * e + 2)
                nc.vector.tensor_tensor(one_hot[:, par], place_e[:, par, :].unsqueeze(1).broadcast_to([P, P, NT]),
                                        iota[:, :, :], ALU.is_equal).then_inc(s_oh, 1)

            def keep_list(e, par):
                dve.wait_ge(s_lf, e + 1)
                nc.vector.tensor_copy(codes[:, bass.ds(e * SLOTS, SLOTS)], bank[2 + par][:, 0:SLOTS]).then_inc(s_lev, 1)

            for par in range(2):
                one_hots(par, par)
            with dve.Fori(0, GE // 2 - 1) as e_pair:
                for par in range(2):
                    keep_list(e_pair * 2 + par, par)
                    one_hots(e_pair * 2 + (par + 2), par)
            for par in range(2):
                keep_list(GE - 2 + par, par)
            dve.wait_ge(s_lev, GE)
            nc.vector.tensor_scalar(pos_code[:, :], codes[:, :], 0.0, None, ALU.is_gt)
            link(nc.vector.tensor_scalar(empty[:, :], codes[:, :], 0.0, pad_row[:, 0:1], ALU.is_equal, ALU.mult))
            link(nc.vector.tensor_tensor(codes[:, :], codes[:, :], pos_code[:, :], ALU.subtract))
            nc.vector.scalar_tensor_tensor(out=slots[:, :], in0=codes[:, :], scalar=float(HALF_N), in1=empty[:, :],
                                           op0=ALU.add, op1=ALU.add)


def experts(nc, io, ident16, h, d, slots, tables):
    n_gran, gran0 = tables
    ctx = ExitStack()
    with ctx:
        def sb(name, shape, dt=F32):
            return ctx.enter_context(nc.sbuf_tensor(name, shape, dt))

        def sem(name):
            return ctx.enter_context(nc.semaphore(name))

        raw1 = sb("raw1", [P, M])
        raw1r = sb("raw1r", [P, M])
        raw2 = sb("raw2", [P, KM * D])
        w1h = [sb(f"w1h{i}", [P, M], F16) for i in range(2)]
        w1l = [sb(f"w1l{i}", [P, M], F16) for i in range(2)]
        w1hr = [sb(f"w1hr{i}", [P, M], F16) for i in range(2)]
        w1lb = [sb(f"w1lb{i}", [P, M], F16) for i in range(2)]
        w2h = [sb(f"w2h{i}", [P, KM * D], F16) for i in range(2)]
        w2l = [sb(f"w2l{i}", [P, KM * D], F16) for i in range(2)]
        BROW = (DR, DR + 32)
        KB = BROW[1] + 1
        xrow = [sb(f"xg{i}", [P, XROW]) for i in range(2)]
        xT = sb("xT", [P, 2, 3, P], F16)
        xTb = sb("xTb", [P, 2, P], F16)
        hid = [sb(f"hid{i}", [P, KM * P]) for i in range(2)]
        hidh = [sb(f"hidh{i}", [P, KM * P], F16) for i in range(2)]
        hidl = [sb(f"hidl{i}", [P, KM * P], F16) for i in range(2)]
        weight = sb("weight", [P, 2])
        unit, unit_gelu = sb("unit", [P, 1]), sb("unit_gelu", [P, 1])
        part = [sb(f"part{i}", [P, D]) for i in range(2)]
        wall = sb("wall", [P, 2, GE])
        get_at = sb("get_at", [P, 2], I32)
        kept_at = sb("kept_at", [P, 2], I32)
        last_at = sb("last_at", [P, 2], I32)
        put_at = [sb(f"put_at{i}", [P, 1], I32) for i in range(2)]
        ysum = [sb(f"ysum{i}", [P, NT, D]) for i in range(2)]
        hps = [[ctx.enter_context(nc.psum_tensor(f"hps{i}{j}", [P, 512], F32)) for j in range(2)] for i in range(2)]
        ops = [ctx.enter_context(nc.psum_tensor(f"ops{i}", [P, 512], F32)) for i in range(2)]
        xps = ctx.enter_context(nc.psum_tensor("xps", [P, 1024], F16))
        PARTS = ((0, 0, 4), (1, 4, 2))

        s_raw = [sem(f"raw_weights{i}_in") for i in range(3)]
        s_bias = [sem("b1_rows_in0"), sem("b1_rows_in1")]
        s_w3, s_xtb, s_set = sem("bias_pads_zeroed"), sem("ones_rows_set"), sem("first_puts_set")
        s_wh, s_wl = sem("weights_high"), sem("weights_low")
        s_idx, s_get = sem("indices_copied"), sem("rows_gathered")
        s_unit, s_table = sem("unit_set"), sem("gelu_table_in")
        s_c, s_used = sem("weights_taken"), sem("rows_used")
        s_pool_turn, s_pe_turn, s_dve_turn = sem("pool_turn"), sem("pe_turn"), sem("dve_turn")
        s_xf, s_xt = sem("x_transposed"), sem("xT_copied")
        s_l1, s_hh, s_h, s_hl = sem("hidden_full"), sem("hidden_high"), sem("hidden_ready"), sem("hidden_low")
        s_l2, s_ev, s_put = ([sem(f"{w}{i}") for i in range(2)] for w in ("out_full", "part_ready", "part_added"))
        OUT_TILES = ((0, 5), (5, 10), (10, 14), (14, NT))
        s_y = [sem(f"sums{k}_in") for k in range(len(OUT_TILES))]
        s_fin, s_out = sem("result_ready"), sem("result_stored")
        block = ctx.enter_context(nc.Block())
        W1 = io["W1"]
        W2 = io["W2"]

        def over_granules(eng, body, split=None):
            with eng.Fori(0, GE // 2) as e_pair:
                e0 = e_pair * 2
                first = eng.value_load(gran0[0:1, bass.ds(e0, 1)], min_val=0, max_val=MAXG)
                for par in range(2):
                    if par == 1:
                        first = first + count
                    count = eng.value_load(n_gran[0:1, bass.ds(e0 + par, 1)], min_val=1, max_val=SLOTS // 2)
                    if split is None:
                        with eng.Fori(0, count) as j:
                            body(par, e0 + par, first + j, j)
                    else:
                        body(par, e0 + par, first, 0, split)
                        with eng.If(count > 1):
                            with eng.Fori(1, count) as j:
                                body(par, e0 + par, first + j, j)

        MAXG = N * KG * KE // GRAN + GE

        @block.sync
        def _(sp):
            def load(e, step):
                if step == 0:
                    sp.dma_start(raw1[:, :], W1[bass.ds(e * D, P), :]).then_inc(s_raw[0], 16)
                elif step == 1:
                    for k in range(2):
                        sp.dma_start(raw1r[DR * k:DR * k + DR, :], W1[bass.ds(e * D + P, DR), :]).then_inc(s_raw[1], 16)
                else:
                    sp.dma_start(raw2[:, :], W2[bass.ds(e, 1), :, :].rearrange("o p n -> (o p) n")).then_inc(s_raw[2], 16)

            def load_bias(par, e):
                for k in range(2):
                    sp.dma_start(w1lb[par][BROW[k]:BROW[k] + 1, :], d["b1s"][k, bass.ds(e, 1), :]).then_inc(s_bias[par], 16)

            for step in range(3):
                load(0, step)
            sp.wait_ge(s_w3, 2)
            load_bias(0, 0)
            with sp.Fori(0, GE // 2) as e_pair:
                e0 = e_pair * 2
                for par in range(2):
                    after = (e0 + par + 1) % GE
                    for step in range(3):
                        sp.wait_ge(s_wl, (e0 + par) * 3 + (step + 1))
                        load(after, step)
                    first = sp.value_load(gran0[0:1, bass.ds(e0 + par, 1)], min_val=0, max_val=MAXG)
                    sp.wait_ge(s_l2[1], first + 1)
                    load_bias(1 - par, after)
            total = sp.value_load(gran0[0:1, GE:GE + 1], min_val=GE, max_val=MAXG)
            for par in range(2):
                sp.wait_ge(s_bias[par], GE * 16 + 32 * (1 - par))
            by_tile = [y.rearrange("(p t) d -> p t d", t=NT) for y in (d["y"][0][0:N, :], d["y"][1][0:N, :], io["out"])]
            for i in range(2):
                sp.wait_ge(s_put[i], total * 16 + 48)
                for k, (t0, t1) in enumerate(OUT_TILES):
                    sp.dma_start(ysum[i][:, t0:t1, :], by_tile[i][:, t0:t1, :]).then_inc(s_y[k], 16)
            for k, (t0, t1) in enumerate(OUT_TILES):
                sp.wait_ge(s_fin, k + 1)
                sp.dma_start(by_tile[2][:, t0:t1, :], ysum[0][:, t0:t1, :]).then_inc(s_out, 16)
            sp.wait_ge(s_out, 16 * len(OUT_TILES))

        @block.gpsimd
        def _(pool):
            for at in (get_at, kept_at, last_at, *put_at):
                nc.gpsimd.iota(at[:, :], [[0, at.shape[1]]], base=N, channel_multiplier=1).then_inc(s_set, 1)
            pool.wait_ge(s_set, 7)

            def stand():
                pool.sem_inc(s_pool_turn, 1)

            def get():
                for i in range(2):
                    pool.indirect_dma_start(xrow[i][:, :], None, d["xrow"][:, :],
                                            bass.IndirectOffsetOnAxis(ap=get_at[:, i:i + 1], axis=0)).then_inc(s_get, 16)

            def put(i):
                pool.indirect_dma_start(d["y"][i][:, :], bass.IndirectOffsetOnAxis(ap=put_at[i][:, :], axis=0),
                                        part[i][:, :], None, compute_op=ALU.add).then_inc(s_put[i], 16)

            def copy_rows(dst, src, count):
                stand()
                nc.gpsimd.tensor_copy(dst, src).then_inc(s_idx, 1)
                pool.wait_ge(s_idx, count)

            def put_tile(i, n, count):
                pool.wait_ge(s_put[i], n * 16 + 16)
                copy_rows(put_at[i][:, :], last_at[:, i:i + 1], count)
                pool.wait_ge(s_ev[i], n + 1)
                stand()
                put(i)

            def turn(n, new_rows):
                pool.wait_ge(s_used, n + 1)
                pool.wait_ge(s_xf, n + 1)
                done = n * 5
                if new_rows is not None:
                    done = done + 1
                    copy_rows(get_at[:, :], new_rows, done)
                stand()
                get()
                put_tile(0, n, done + 1)
                pool.wait_ge(s_put[1], n * 16 + 16)
                copy_rows(put_at[1][:, :], last_at[:, 1:2], done + 2)
                copy_rows(last_at[:, :], kept_at[:, :], done + 3)
                copy_rows(kept_at[:, :], get_at[:, :], done + 4)
                pool.wait_ge(s_ev[1], n + 1)
                stand()
                put(1)

            for i in range(2):
                put(i)
            over_granules(pool, lambda par, e, g, j: turn(g, slots[:, bass.ds(e * SLOTS + j * 2, 2)]))
            total = pool.value_load(gran0[0:1, GE:GE + 1], min_val=GE, max_val=MAXG)
            turn(total, None)
            for i in range(2):
                put_tile(i, total + 1, total * 5 + (5 + i))
            pool.wait_ge(s_pool_turn, total * 8 + 11)
            pool.wait_ge(s_pe_turn, GE)

        @block.tensor
        def _(pe):
            def transpose_x(n):
                pe.wait_ge(s_get, n * 32)
                for i in range(2):
                    for c in range(3):
                        tr = nc.tensor.transpose(xps[:, (3 * i + c) * P:(3 * i + c + 1) * P],
                                                 xrow[i][:, DR * c:DR * c + DR].bitcast(F16), ident16[:, :])
                tr.then_inc(s_xf, 1)

            def layer1(par, i):
                for bank_, c0, cn in PARTS:
                    for c in range(c0, c0 + cn):
                        o = hps[i][bank_][:, P * (c - c0):P * (c - c0) + P]
                        col = slice(P * c, P * c + P)
                        terms = ((w1h[par][:, col], xT[:, i, 0, :]), (w1h[par][:, col], xT[:, i, 1, :]),
                                 (w1l[par][:, col], xT[:, i, 0, :]), (w1hr[par][:, col], xT[:, i, 2, :]),
                                 (w1lb[par][0:KB, col], xTb[0:KB, i, :]))
                        for k, (w, x) in enumerate(terms):
                            mm = nc.tensor.matmul(o, w, x, start=(k == 0), stop=(k == len(terms) - 1))
                    mm.then_inc(s_l1, 1)

            def layer2(par, i, g, e):
                pe.wait_ge(s_wl, e * 3 + 3)
                for n, (bank_, c0, cn) in enumerate(PARTS):
                    pe.wait_ge(s_hl, g * 4 + (2 * i + n + 1))
                    for c in range(c0, c0 + cn):
                        col, wcol = slice(P * c, P * c + P), slice(D * c, D * c + D)
                        for a, w in ((hidh, w2h), (hidh, w2l), (hidl, w2h)):
                            mm = nc.tensor.matmul(ops[i][:, 0:D], a[i][:, col], w[par][:, wcol],
                                                  start=(c == 0 and a is hidh and w is w2h),
                                                  stop=(c == KM - 1 and a is hidl))
                mm.then_inc(s_l2[i], 1)

            def granule(par, g, e):
                pe.wait_ge(s_xt, g + 1)
                layer1(par, 0)
                layer1(par, 1)
                pe.wait_ge(s_ev[0], g + 2)
                layer2(par, 0, g, e)
                transpose_x(g + 2)
                pe.wait_ge(s_ev[1], g + 2)
                layer2(par, 1, g, e)

            for i in range(2):
                pe.sem_inc(s_l2[i], 1)
            pe.sem_inc(s_xf, 1)
            pe.wait_ge(s_xtb, 2)
            transpose_x(1)
            with pe.Fori(0, GE // 2) as e_pair:
                e0 = e_pair * 2
                first = pe.value_load(gran0[0:1, bass.ds(e0, 1)], min_val=0, max_val=MAXG)
                for par in range(2):
                    e = e0 + par
                    if par == 1:
                        first = first + count
                    count = pe.value_load(n_gran[0:1, bass.ds(e, 1)], min_val=1, max_val=SLOTS // 2)
                    pe.wait_ge(s_wl, e * 3 + 2)
                    pe.wait_ge(s_bias[par], e0 * 16 + 32)
                    pe.sem_inc(s_pe_turn, 1)
                    with pe.Fori(0, count) as j:
                        granule(par, first + j, e)

        @block.scalar
        def _(act):
            def split_high(par, n, steps, first=None):
                if first is not None:
                    act.wait_ge(s_l2[1], first + 1)
                for k in steps:
                    act.wait_ge(s_raw[k], n * (16, 32, 16)[k])
                    high, raw = ((w1h, raw1), (w1hr, raw1r), (w2h, raw2))[k]
                    nc.scalar.mul(high[par][:, :], raw[:, :], WSCALE).then_inc(s_wh, 1)

            def copy_x(n):
                act.wait_ge(s_xf, n + 1)
                px = xps[:, 0:6 * P].rearrange("q (i c p) -> q i c p", i=2, c=3)
                nc.scalar.copy(xT[:], px)
                nc.scalar.copy(xTb[0:DR, :, :], px[0:DR, :, 2, :]).then_inc(s_xt, 1)

            def body(par, e, g, j, split=False):
                if split:
                    act.wait_ge(s_table, e + 1)
                    nc.scalar.activation(unit_gelu[:, :], unit[:, :], ACT.Gelu).then_inc(s_table, 1)
                    split_high(1 - par, e + 2, (0,), g)
                for i in range(2):
                    act.wait_ge(s_l2[i], g + 1)
                    for n, (bank_, c0, cn) in enumerate(PARTS):
                        act.wait_ge(s_l1, g * 4 + (2 * i + n + 1))
                        cols = slice(P * c0, P * (c0 + cn))
                        nc.scalar.activation(hidh[i][:, cols], hps[i][bank_][:, 0:P * cn], ACT.Gelu, scale=1.0 / WSCALE)
                        nc.scalar.activation(hid[i][:, cols], hps[i][bank_][:, 0:P * cn], ACT.Gelu,
                                             scale=1.0 / WSCALE).then_inc(s_h, 1)
                if split:
                    split_high(1 - par, e + 2, (1,))
                copy_x(g + 2)
                if split:
                    split_high(1 - par, e + 2, (2,))

            act.wait_ge(s_unit, 1)
            nc.scalar.activation(unit_gelu[:, :], unit[:, :], ACT.Gelu).then_inc(s_table, 1)
            split_high(0, 1, (0, 1, 2))
            copy_x(1)
            over_granules(act, body, split=True)
            act.wait_ge(s_table, GE + 1)

        @block.vector
        def _(dve):
            def split_low(par, n, steps=(0, 1, 2)):
                for k in steps:
                    low, high, raw = ((w1l[par][:, :], w1h[par][:, :], raw1[:, :]),
                                      (w1lb[par][0:DR, :], w1hr[par][0:DR, :], raw1r[0:DR, :]),
                                      (w2l[par][:, :], w2h[par][:, :], raw2[:, :]))[k]
                    dve.wait_ge(s_wh, (n - 1) * 3 + k + 1)
                    nc.vector.scalar_tensor_tensor(out=low, in0=raw, scalar=WSCALE, in1=high,
                                                   op0=ALU.mult, op1=ALU.subtract).then_inc(s_wl, 1)

            def take_weights(n):
                dve.wait_ge(s_get, n * 32)
                for i in range(2):
                    last = nc.vector.tensor_copy(wall[:, i, :], xrow[i][:, D:XROW])
                last.then_inc(s_used, 1)

            def evacuate(i, g):
                dve.wait_ge(s_l2[i], g + 2)
                dve.wait_ge(s_put[i], g * 16 + 48)
                nc.vector.tensor_scalar(part[i][:, :], ops[i][:, 0:D], weight[:, i:i + 1], 1.0 / WSCALE,
                                        ALU.mult, ALU.mult).then_inc(s_ev[i], 1)

            def body(par, e, g, j, split=False):
                dve.wait_ge(s_used, g + 2)
                dve.wait_ge(s_ev[1], g + 2)
                dve.sem_inc(s_dve_turn, 1)
                nc.vector.tensor_copy(weight[:, :].unsqueeze(2), wall[:, :, bass.ds(e, 1)]).then_inc(s_c, 1)
                if split:
                    split_low(1 - par, e + 2, (0,))
                for i in range(2):
                    for n, (bank_, c0, cn) in enumerate(PARTS):
                        dve.wait_ge(s_h, g * 4 + (2 * i + n + 1))
                        cols = slice(P * c0, P * (c0 + cn))
                        nc.vector.tensor_tensor(hidl[i][:, cols], hid[i][:, cols], hidh[i][:, cols],
                                                ALU.subtract).then_inc(s_hl, 1)
                dve.wait_ge(s_c, g + 1)
                evacuate(0, g)
                take_weights(g + 2)
                if split:
                    split_low(1 - par, e + 2, (1,))
                evacuate(1, g)
                if split:
                    split_low(1 - par, e + 2, (2,))

            for i in range(2):
                nc.vector.memset(part[i][:, :], 0.0).then_inc(s_set, 1)
            for i in range(2):
                nc.vector.memset(w1lb[i][DR:P, :], 0.0).then_inc(s_w3, 1)
            nc.vector.memset(xTb[DR:P, :, :], 0.0).then_inc(s_w3, 1)
            dve.wait_ge(s_w3, 3)
            for r in BROW:
                nc.vector.memset(xTb[r:r + 1, :, :], 1.0).then_inc(s_xtb, 1)
            dve.sem_inc(s_used, 1)
            nc.vector.memset(unit[:, :], 0.0).then_inc(s_unit, 1)
            for i in range(2):
                dve.sem_inc(s_ev[i], 2)
            split_low(0, 1)
            take_weights(1)
            over_granules(dve, body, split=True)
            total = dve.value_load(gran0[0:1, GE:GE + 1], min_val=GE, max_val=MAXG)
            dve.wait_ge(s_dve_turn, total)
            for k, (t0, t1) in enumerate(OUT_TILES):
                dve.wait_ge(s_y[k], 32)
                nc.vector.tensor_tensor(ysum[0][:, t0:t1], ysum[0][:, t0:t1], ysum[1][:, t0:t1], ALU.add).then_inc(s_fin, 1)


def kernel(x, x_txt, L0_tok_proj_w, L0_tok_proj_b, L0_tok_pos_emb, L0_txt_weight, L0_attn_w_q, L0_attn_w_k,
           L0_attn_w_v, L0_attn_w_o, L0_attn_b_o, L0_ffn_Wg, L0_ffn_bg, L0_ffn_We, L0_ffn_be, L0_ffn_W1,
           L0_ffn_b1, L0_ffn_W2, L0_ffn_b2):
    import numpy as np
    import concourse.bacc as bacc
    from concourse.bass_utils import run_bass_kernel_spmd

    a = np.asarray
    side = 16
    edge = 96 // side
    patches = a(x).reshape(B, 3, edge, side, edge, side).transpose(3, 5, 1, 2, 4, 0).reshape(KF, P, S_IMG * B)
    token = np.arange(N).reshape(P, NT) - HALF_N
    arrays = {
        "xpT": patches.transpose(1, 0, 2),
        "pwT": a(L0_tok_proj_w).T.reshape(KF, P, D).transpose(1, 0, 2),
        "idsT": a(x_txt).astype(np.int32).T.reshape(TXT_TILES, P).T,
        "wqkv": np.concatenate([a(L0_attn_w_q), a(L0_attn_w_k), a(L0_attn_w_v)], axis=1),
        "L0_tok_proj_b": a(L0_tok_proj_b), "L0_tok_pos_emb": a(L0_tok_pos_emb), "L0_txt_weight": a(L0_txt_weight),
        "L0_attn_w_o": a(L0_attn_w_o), "L0_attn_b_o": a(L0_attn_b_o),
        "wr": np.concatenate([a(L0_ffn_Wg), a(L0_ffn_We).transpose(1, 0, 2).reshape(D, GE)], axis=1),
        "br": np.concatenate([a(L0_ffn_bg), a(L0_ffn_be).reshape(GE)]),
        "W1": a(L0_ffn_W1).reshape(GE * D, M), "b1": a(L0_ffn_b1).reshape(GE, M),
        "W2": a(L0_ffn_W2).reshape(GE, KM, P, D).transpose(0, 2, 1, 3).reshape(GE, P, KM * D),
        "b2": a(L0_ffn_b2).reshape(GE, D),
        "ident": np.eye(P, dtype=np.float32), "ident16": np.eye(P, dtype=np.float16),
        "ltri": np.triu(np.ones((P, P), np.float16), 1), "ones": np.ones((P, P), np.float16),
        "iota": np.tile(np.arange(P, dtype=np.float16)[None, :, None], (P, 1, NT)),
        "code": (token + (token >= 0)).astype(np.float32),
        "pad_row": (N - HALF_N + np.arange(P, dtype=np.float32)).reshape(P, 1),
        "earlier": (np.arange(GE)[None, :] < np.arange(GE + 1)[:, None]).astype(np.float32).reshape(1, -1),
    }
    nc = bacc.Bacc("TRN2", target_bir_lowering=False, num_devices=1)
    io, inputs = {}, {}
    for name, value in arrays.items():
        value = np.ascontiguousarray(value)
        inputs[f"in_{name}"] = value
        io[name] = nc.dram_tensor(f"in_{name}", value.shape, mybir.dt.from_np(value.dtype), kind="ExternalInput").ap()
    io["out"] = nc.dram_tensor("out", [N, D], F32, kind="ExternalOutput").ap()
    build(nc, io)
    r = run_bass_kernel_spmd(nc, [inputs], core_ids=[0])
    return r.results[0]["out"].reshape(B, S, D)
```
